# Optimizing a Trainium2 kernel written in Bass

```python
import numpy as np
import jax
import jax.numpy as jnp

def _softmax(x, axis=-1):
    return jax.nn.softmax(x, axis=axis)

def _gelu(x):
    return jax.nn.gelu(x, approximate=True)

def _silu(x):
    return jax.nn.silu(x)

def _sigmoid(x):
    return jax.nn.sigmoid(x)

def _layernorm(x, axis=-1, eps=1e-05):
    m = jnp.mean(x, axis=axis, keepdims=True)
    v = jnp.var(x, axis=axis, keepdims=True)
    return (x - m) / jnp.sqrt(v + eps)

def _scatter_add(tgt, idx, src, axis=0):
    return tgt.at[idx].add(src)

def _segment_sum(src, seg, n):
    return jax.ops.segment_sum(src, seg, n)
kernel_name = 'mk_seq_postln_d1_jaxref_r4_df3bac'

def setup_inputs(seed: int=0):
    np.random.seed(seed)
    _w = jnp.asarray

    def _L0_attn_setup():
        import jax, jax.numpy as jnp
        import numpy as np
        EMBED_DIM = 256
        NUM_HEADS = 16
        HEAD_DIM = EMBED_DIM // NUM_HEADS
        NUM_LANDMARKS = 64
        REG = 1e-06
        BATCH = 2
        SEQ = 2048

        def _sq_dists(X, L):
            Xn = jnp.sum(X * X, axis=-1, keepdims=True)
            Ln = jnp.sum(L * L, axis=-1, keepdims=True)
            XL = jnp.einsum('bhnd,bhkd->bhnk', X, L)
            return jnp.maximum(Xn + jnp.swapaxes(Ln, -2, -1) - 2.0 * XL, 0.0)
        key = jax.random.key(seed)
        ks = jax.random.split(key, 10)
        s = 0.02
        inp = {'query': jax.random.normal(ks[0], (BATCH, SEQ, EMBED_DIM), dtype=jnp.float32), 'Wq': jax.random.normal(ks[1], (EMBED_DIM, EMBED_DIM), dtype=jnp.float32) * s, 'bq': jnp.zeros((EMBED_DIM,), jnp.float32), 'Wk': jax.random.normal(ks[2], (EMBED_DIM, EMBED_DIM), dtype=jnp.float32) * s, 'bk': jnp.zeros((EMBED_DIM,), jnp.float32), 'Wv': jax.random.normal(ks[3], (EMBED_DIM, EMBED_DIM), dtype=jnp.float32) * s, 'bv': jnp.zeros((EMBED_DIM,), jnp.float32), 'Wo': jax.random.normal(ks[4], (EMBED_DIM, EMBED_DIM), dtype=jnp.float32) * s, 'bo': jnp.zeros((EMBED_DIM,), jnp.float32), 'temperature': jnp.asarray(float(HEAD_DIM), jnp.float32), 'landmark_idx': jnp.arange(NUM_LANDMARKS, dtype=jnp.int32) * (SEQ // NUM_LANDMARKS)}
        return inp
    _L0_attn_in = _L0_attn_setup()

    def _L0_ffn_setup():
        import jax, jax.numpy as jnp
        import numpy as np
        D_MODEL = 256
        NUM_EXPERTS = 8
        TOP_K = 2
        key = jax.random.key(seed)
        ks = jax.random.split(key, 5)
        scale = 1.0 / np.sqrt(D_MODEL)
        x = jax.random.normal(ks[0], (4, 512, D_MODEL), dtype=jnp.float32)
        We = jax.random.uniform(ks[1], (NUM_EXPERTS, D_MODEL, D_MODEL), jnp.float32, -scale, scale)
        be = jax.random.uniform(ks[2], (NUM_EXPERTS, D_MODEL), jnp.float32, -scale, scale)
        Wg = jax.random.uniform(ks[3], (NUM_EXPERTS, D_MODEL), jnp.float32, -scale, scale)
        bg = jax.random.uniform(ks[4], (NUM_EXPERTS,), jnp.float32, -scale, scale)
        return {'x': x, 'We': We, 'be': be, 'Wg': Wg, 'bg': bg}
    _L0_ffn_in = _L0_ffn_setup()
    _d = {'L0_attn_query': _L0_attn_in['query'], 'L0_attn_Wq': _L0_attn_in['Wq'], 'L0_attn_bq': _L0_attn_in['bq'], 'L0_attn_Wk': _L0_attn_in['Wk'], 'L0_attn_bk': _L0_attn_in['bk'], 'L0_attn_Wv': _L0_attn_in['Wv'], 'L0_attn_bv': _L0_attn_in['bv'], 'L0_attn_Wo': _L0_attn_in['Wo'], 'L0_attn_bo': _L0_attn_in['bo'], 'L0_attn_temperature': _L0_attn_in['temperature'], 'L0_attn_landmark_idx': _L0_attn_in['landmark_idx'], 'L0_ffn_We': _L0_ffn_in['We'], 'L0_ffn_be': _L0_ffn_in['be'], 'L0_ffn_Wg': _L0_ffn_in['Wg'], 'L0_ffn_bg': _L0_ffn_in['bg']}
    _x0 = _d['L0_attn_query']
    _d['L0_attn_query'] = jax.random.normal(jax.random.fold_in(jax.random.key(seed), 1), (8, 2048, 256), dtype=_x0.dtype)
    del _x0
    return _d

def reference(L0_attn_query, L0_attn_Wq, L0_attn_bq, L0_attn_Wk, L0_attn_bk, L0_attn_Wv, L0_attn_bv, L0_attn_Wo, L0_attn_bo, L0_attn_temperature, L0_attn_landmark_idx, L0_ffn_We, L0_ffn_be, L0_ffn_Wg, L0_ffn_bg):

    def _L0_attn_ref(query, Wq, bq, Wk, bk, Wv, bv, Wo, bo, temperature, landmark_idx):
        import jax, jax.numpy as jnp
        import numpy as np
        EMBED_DIM = 256
        NUM_HEADS = 16
        HEAD_DIM = EMBED_DIM // NUM_HEADS
        NUM_LANDMARKS = 64
        REG = 1e-06
        BATCH = 2
        SEQ = 2048

        def _sq_dists(X, L):
            Xn = jnp.sum(X * X, axis=-1, keepdims=True)
            Ln = jnp.sum(L * L, axis=-1, keepdims=True)
            XL = jnp.einsum('bhnd,bhkd->bhnk', X, L)
            return jnp.maximum(Xn + jnp.swapaxes(Ln, -2, -1) - 2.0 * XL, 0.0)
        b, n, _ = query.shape
        Q = (query @ Wq.T + bq).reshape(b, n, NUM_HEADS, HEAD_DIM).transpose(0, 2, 1, 3)
        K = (query @ Wk.T + bk).reshape(b, n, NUM_HEADS, HEAD_DIM).transpose(0, 2, 1, 3)
        V = (query @ Wv.T + bv).reshape(b, n, NUM_HEADS, HEAD_DIM).transpose(0, 2, 1, 3)
        landmarks = K[:, :, landmark_idx, :]
        C_Q = _sq_dists(Q, landmarks)
        C_K = _sq_dists(K, landmarks)
        W_sq = C_K[:, :, landmark_idx, :]
        Phi_Q = jnp.exp(-C_Q / temperature)
        Phi_K = jnp.exp(-C_K / temperature)
        W_kernel = jnp.exp(-W_sq / temperature) + REG * jnp.eye(NUM_LANDMARKS, dtype=query.dtype)
        Z = jnp.einsum('bhnk,bhnd->bhkd', Phi_K, V)
        Y = jnp.linalg.solve(W_kernel, Z)
        out_unnorm = jnp.einsum('bhnk,bhkd->bhnd', Phi_Q, Y)
        Phi_K_sum = jnp.sum(Phi_K, axis=-2)[..., None]
        norm = jnp.einsum('bhnk,bhko->bhno', Phi_Q, jnp.linalg.solve(W_kernel, Phi_K_sum))
        norm = jnp.maximum(norm, 1e-10)
        out = out_unnorm / norm
        out = out.transpose(0, 2, 1, 3).reshape(b, n, EMBED_DIM)
        return out @ Wo.T + bo

    def _L0_ffn_ref(x, We, be, Wg, bg):
        import jax, jax.numpy as jnp
        import numpy as np
        D_MODEL = 256
        NUM_EXPERTS = 8
        TOP_K = 2
        B, S, D = x.shape
        xf = x.reshape(-1, D)
        gate_logits = xf @ Wg.T + bg
        topk_vals, topk_idx = jax.lax.top_k(gate_logits, TOP_K)
        gate_w = jax.nn.softmax(topk_vals, axis=-1)
        all_out = jnp.einsum('nd,ehd->neh', xf, We) + be
        sel = jnp.take_along_axis(all_out, topk_idx[:, :, None], axis=1)
        out = jnp.sum(sel * gate_w[:, :, None], axis=1)
        return out.reshape(B, S, D)
    x = L0_attn_query
    x = _layernorm(x + _L0_attn_ref(x, L0_attn_Wq, L0_attn_bq, L0_attn_Wk, L0_attn_bk, L0_attn_Wv, L0_attn_bv, L0_attn_Wo, L0_attn_bo, L0_attn_temperature, L0_attn_landmark_idx), axis=-1)
    x = _layernorm(x + _L0_ffn_ref(x, L0_ffn_We, L0_ffn_be, L0_ffn_Wg, L0_ffn_bg), axis=-1)
    return x

_drawn_inputs = setup_inputs


def setup_inputs(seed=0):
    import zlib

    import numpy as np

    out = dict(_drawn_inputs(seed))
    spreads = {'L0_attn_bq': (0.0, 0.8),
     'L0_attn_bk': (0.0, 0.8),
     'L0_attn_bv': (0.0, 0.1),
     'L0_attn_bo': (0.0, 0.1)}
    factors = {'L0_attn_Wq': 8.0, 'L0_attn_Wk': 8.0, 'L0_attn_Wv': 3.651}
    for name, (base, spread) in spreads.items():
        noise = np.random.default_rng([zlib.crc32(name.encode()), seed]).standard_normal(out[name].shape)
        drawn = base * np.exp(spread * noise) if base else spread * noise
        out[name] = jnp.asarray(drawn.astype(out[name].dtype))
    for name, factor in factors.items():
        out[name] = (out[name] * factor).astype(out[name].dtype)
    return out
```

```python
import concourse.bass as bass
from concourse import mybir
from contextlib import ExitStack

BATCH, SEQ, D, H, HD, NL, E = 8, 2048, 256, 16, 16, 64, 8
P = 128
T = BATCH * SEQ
CH = 512
CPB = SEQ // CH
NCH = T // CH
KC = D // P
HPS = H // KC
PAIRS = H // 2
TPC = CH // P
AHEAD = 2
REG = 1e-6
EPS = 1e-5
NORM_MIN = 1e-10
BIG = 3.0e38
GJ_PIECES = 4
GJ_POOL = 3

C_ID, C_HEAD, C_NEG, C_LO, C_M16, C_NSEL, C_IOTA, C_REG, C_EXP, C_BES, C_EPS, C_MINUS, C_END = (
    0, 128, 136, 200, 201, 217, 225, 233, 297, 301, 302, 306, 310)


def program(nc, xT, x, wq, wk, wv, wo, we, wg, bq, bk, bv, bo, be3, bg, temp, idx, gbase, consts, out):
    f32, f32r = mybir.dt.float32, mybir.dt.float32r
    i32, u32 = mybir.dt.int32, mybir.dt.uint32
    ALU, ACT = mybir.AluOpType, mybir.ActivationFunctionType

    w_dram = nc.dram_tensor("w_dram", [BATCH * H, NL, NL], f32).ap()
    winv_dram = nc.dram_tensor("winv_dram", [(BATCH + 1) * H, NL, NL], f32).ap()
    xT_v = xT.rearrange("(k p) t -> p k t", p=P)
    x_v = x.rearrange("(c t p) d -> c p t d", t=TPC, p=P)
    out_v = out.rearrange("(c t p) d -> c p t d", t=TPC, p=P)

    ctx = ExitStack()
    with ctx:
        def sb(name, shape, dt=f32):
            return ctx.enter_context(nc.sbuf_tensor(name, shape, dt))

        def sem(name):
            return ctx.enter_context(nc.semaphore(name))

        bank = [ctx.enter_context(nc.psum_tensor(f"bank{i}", [P, 512], f32)) for i in range(8)]

        cst = sb("cst", [P, C_END])
        ident = cst[:, C_ID:C_ID + P]
        neg_block = cst[:, C_NEG:C_NEG + 64].rearrange("p (s r) -> p s r", s=KC)
        lo_sign = cst[:, C_LO:C_LO + 1]
        neg_sel = cst[:, C_NSEL:C_NSEL + 8].rearrange("p (u i) -> p u i", u=2)
        bq_sb, bk_sb = sb("bq_sb", [P, KC]), sb("bk_sb", [P, KC])
        bv_sb, bo_sb = sb("bv_sb", [P, D]), sb("bo_sb", [P, D])
        bg_sb, temp_sb, invt = sb("bg_sb", [P, E]), sb("temp_sb", [P, 1]), sb("invt", [P, 1])
        phi_max, phi_min, tpos = sb("phi_max", [P, 1]), sb("phi_min", [P, 1]), sb("tpos", [P, 1])
        idx_sb, gbase_sb, rows_sb = sb("idx_sb", [P, 1], i32), sb("gbase_sb", [P, 4], i32), sb("rows_sb", [P, 4], i32)
        wh, wl = sb("wh", [P, 4, KC, D], f32r), sb("wl", [P, 4, KC, D], f32r)
        with nc.sbuf_tensor("inversion", [P, 2, NL * NL], f32) as inversion:
            g_all, t_all = inversion[:, 0], inversion[:, 1]
        g3 = g_all.rearrange("p (r c) -> p r c", r=NL)
        t3 = t_all.rearrange("p (r c) -> p r c", r=NL)
        w_raw = t_all[:, 0:2048].rearrange("p (w k n) -> p w k n", w=4, k=KC)
        wk_sb = [t_all[0:64, 2048 + 1024 * i:3072 + 1024 * i].rearrange("p (s h k) -> p s h k", s=KC, h=HPS)
                 for i in range(2)]
        weh, wel = sb("weh", [P, KC, E * D], f32r), sb("wel", [P, KC, E * D], f32r)
        wg_raw, wg_s = sb("wg_raw", [P, KC, E]), sb("wg_s", [P, KC, 2 * E], f32r)
        be_s = sb("be_s", [24, D], f32r)
        sel_q = sb("sel_q", [32, PAIRS, P], f32r)

        NB1 = BATCH + 1
        l2h, l2l = sb("l2h", [P, KC, NB1 * NL]), sb("l2l", [P, KC, NB1 * NL])
        nlt, nlt_cur = sb("nlt", [P, NB1, PAIRS]), sb("nlt_cur", [P, PAIRS])
        bdh, bdl = [sb("bdh0", [P, KC, HPS, NL], f32r)], [sb("bdl0", [P, KC, HPS, NL], f32r)]

        x_raw = [sb(f"x_raw{i}", [P, KC, CH]) for i in range(2)]
        xh = [sb(f"xh{i}", [P, KC, CH], f32r) for i in range(2)]
        xl = [sb(f"xl{i}", [P, KC, CH], f32r) for i in range(2)]
        kh, kl = [sb("kh0", [P, KC, CH], f32r)], [sb("kl0", [P, KC, CH], f32r)]
        sq = sb("sq", [P, KC, CH])
        augk = [sb("augk0", [64, CH], f32r)]
        aug_hi = sb("aug_hi", [32, CH], f32r)
        phi = sb("phi", [P, 8, CH])
        zt = sb("zt", [P, NB1, 4 * NL])
        attn_h, attn_l = sb("attn_h", [P, KC, CH], f32r), sb("attn_l", [P, KC, CH], f32r)
        x1h, x1l = sb("x1h", [P, KC, CH], f32r), sb("x1l", [P, KC, CH], f32r)
        lm_x = phi[:, 0:2, :].rearrange("p a (b d) -> p (a b) d", b=2)
        gj_f, gj_r, gj_p = sb("gj_f", [P, NL]), sb("gj_r", [P, NL]), sb("gj_p", [P, 1])
        zero_c, minus1 = sb("zero_c", [P, NL]), sb("minus1", [P, 1])
        st1, mv1, ve1, rs1, nm1 = (sb("st1", [P, TPC, 6]), sb("mv1", [P, TPC, 2]), sb("ve1", [P, TPC]),
                                   sb("rs1", [P, TPC]), sb("nm1", [P, TPC]))
        st2, mv2, ve2, rs2, nm2 = (sb("st2", [P, TPC, 6]), sb("mv2", [P, TPC, 2]), sb("ve2", [P, TPC]),
                                   sb("rs2", [P, TPC]), sb("nm2", [P, TPC]))
        nt1, nt2 = sb("nt1", [P, TPC]), sb("nt2", [P, TPC])
        lg0, lg, m8, i8 = (sb("lg0", [P, TPC, E]), sb("lg", [P, TPC, E]), sb("m8", [P, TPC, 8]),
                           sb("i8", [P, TPC, 8], u32))
        if2, gd, ge, gs, gw1, gw2 = (sb("if2", [P, TPC, 2]), sb("gd", [P, TPC]), sb("ge", [P, TPC]),
                                     sb("gs", [P, TPC]), sb("gw1", [P, TPC]), sb("gw2", [P, TPC]))
        oh1, oh2, gate, gate_h = (sb("oh1", [P, TPC, E]), sb("oh2", [P, TPC, E]), sb("gate", [P, TPC, E]),
                                  sb("gate_h", [P, TPC, E], f32r))
        g_st, g_t = sb("g_st", [P, TPC, 24]), sb("g_t", [24, CH], f32r)

        with ExitStack() as stage1:
            def sb1(name, shape, dt=f32):
                return stage1.enter_context(nc.sbuf_tensor(name, shape, dt))

            v_aug = [sb1(f"v_aug{i}", [P, TPC, H, 32]) for i in range(2)]
            be_raw, be_tmp = sb1("be_raw", [24, D]), sb1("be_tmp", [24, D], f32r)
            bdh.append(sb1("bdh1", [P, KC, HPS, NL], f32r))
            bdl.append(sb1("bdl1", [P, KC, HPS, NL], f32r))
            augm = [sb1(f"augm{i}", [64, KC, HPS, NL], f32r) for i in range(2)]
            ln_rows = sb1("ln_rows", [64, NB1 * NL])
            kh.append(sb1("kh1", [P, KC, CH], f32r))
            kl.append(sb1("kl1", [P, KC, CH], f32r))
            augk.append(sb1("augk1", [64, CH], f32r))
        x_tok = [sb(f"x_tok{i}", [P, TPC, D]) for i in range(2)]
        h_res, x1, acc = sb("h_res", [P, TPC, D]), sb("x1", [P, TPC, D]), sb("acc", [P, TPC, D])
        y_out = [sb(f"y_out{i}", [P, TPC, D]) for i in range(2)]
        nrm, rcp = sb("nrm", [P, CH]), sb("rcp", [P, CH])
        attn = sb("attn", [P, KC, CH])
        zt_cur, zk = sb("zt_cur", [P, 4 * NL]), sb("zk", [64, H * 32])
        winv_sb, y_cur = sb("winv_sb", [64, H, NL]), sb("y_cur", [P, PAIRS, 64])
        we_raw = [a[:].rearrange("p t d -> p (t d)") for a in (h_res, x1, *y_out)]

        small_loaded, w_loaded, we_loaded = sem("small_loaded"), sem("w_loaded"), sem("we_loaded")
        rows_ready, gathered, const_set, setup_done = sem("rows_ready"), sem("gathered"), sem("const_set"), sem("setup_done")
        w_split_h, w_split_l = sem("w_split_h"), sem("w_split_l")
        lmT_done, l2_ready, nl_done, nl_ready = sem("lmT_done"), sem("l2_ready"), sem("nl_done"), sem("nl_ready")
        bd_ready, bdl_ready, w_ready, w_stored, g_loaded = (
            sem("bd_ready"), sem("bdl_ready"), sem("w_ready"), [sem(f"w_stored{i}") for i in range(2)], sem("g_loaded"))
        dve_step, pool_step = sem("dve_step"), sem("pool_step")
        dve_waited, pe_waited = sem("dve_waited"), sem("pe_waited")
        x_loaded, xh_ready, xl_ready = [sem(f"x_loaded{i}") for i in range(2)], sem("xh_ready"), sem("xl_ready")
        kproj_done, s_ready, kl_done, norm_done, aug_done = (
            sem("kproj_done"), sem("s_ready"), sem("kl_done"), sem("norm_done"), sem("aug_done"))
        vproj_done, v_done = sem("vproj_done"), sem("v_done")
        dist_done, exp_done, phi_ready, z_done, zt_saved = (
            sem("dist_done"), sem("exp_done"), sem("phi_ready"), sem("z_done"), sem("zt_saved"))
        gj_ready, gj_prod, inv_done = sem("gj_ready"), sem("gj_prod"), sem("inv_done")
        winv_stored, winv_loaded, zt_cur_ready, ztr_done, zk_ready, y_done, y_ready = (
            sem("winv_stored"), sem("winv_loaded"), sem("zt_cur_ready"), sem("ztr_done"), sem("zk_ready"),
            sem("y_done"), sem("y_ready"))
        xq_loaded, xqh_ready, xql_ready, xt_loaded, xb_ready = (
            [sem(f"xq_loaded{i}") for i in range(2)], sem("xqh_ready"), sem("xql_ready"),
            [sem(f"xt_loaded{i}") for i in range(2)], sem("xb_ready"))
        qproj_done, qs_ready, ql_done, qnorm_done, qaug_done = (
            sem("qproj_done"), sem("qs_ready"), sem("ql_done"), sem("qnorm_done"), sem("qaug_done"))
        nlt_ready, qbd_ready, qdist_done, qexp_done, qphi_ready = (
            sem("nlt_ready"), sem("qbd_ready"), sem("qdist_done"), sem("qexp_done"), sem("qphi_ready"))
        out_done, attn_ready, attnh_ready, attnl_ready = (
            sem("out_done"), sem("attn_ready"), sem("attnh_ready"), sem("attnl_ready"))
        wo_done, h_done, ln1_stats, ln1_coef, x1_ready, x1t_done, x1h_ready, x1l_ready = (
            sem("wo_done"), sem("h_done"), sem("ln1_stats"), sem("ln1_coef"), sem("x1_ready"),
            sem("x1t_done"), sem("x1h_ready"), sem("x1l_ready"))
        gate_done, gate_read, gd_ready, ge_ready, gst_ready, gtr_done, gt_ready, be_done = (
            sem("gate_done"), sem("gate_read"), sem("gd_ready"), sem("ge_ready"), sem("gst_ready"),
            sem("gtr_done"), sem("gt_ready"), sem("be_done"))
        ffn_done, comb_done, acc_done, ln2_stats, ln2_coef, res_ready, res_stored = (
            sem("ffn_done"), sem("comb_done"), sem("acc_done"), sem("ln2_stats"), sem("ln2_coef"),
            sem("res_ready"), [sem(f"res_stored{i}") for i in range(2)])

        block = ctx.enter_context(nc.Block())

        W_EXPS = 2 * BATCH

        def raw(ap):
            return ap.bitcast(f32)

        def rep(ap, axis, n):
            a = ap.unsqueeze(axis)
            shape = list(a.shape)
            shape[axis] = n
            return a.broadcast_to(shape)

        def in_batch(b, n=NL):
            return bass.ds(b * n, n)

        class Steps:

            def __init__(self, eng, semaphore):
                self.eng, self.sem, self.base, self.n = eng, semaphore, 0, 0

            def did(self, instruction):
                self.n += 1
                instruction.then_inc(self.sem, 1)

            def wait(self):
                self.eng.wait_ge(self.sem, self.base + self.n)

            def then(self, instruction):
                self.did(instruction)
                self.wait()

            def enter(self, i, per_turn):
                self.start = self.base + self.n
                self.per_turn, self.n = per_turn, 0
                self.base = self.start + i * per_turn

            def leave(self, turns):
                assert self.n == self.per_turn, (self.n, self.per_turn)
                self.base, self.n = self.start + turns * self.per_turn, 0

        def product3(outp, ah, al, bh, bl, first, last):
            nc.tensor.matmul(outp, ah, bh, start=first, stop=False)
            nc.tensor.matmul(outp, al, bh, start=False, stop=False)
            return nc.tensor.matmul(outp, ah, bl, start=False, stop=last)

        @block.sync
        def _(sp):
            sp.sem_inc(z_done, TPC)
            sp.sem_inc(qexp_done, PAIRS)
            sp.sem_inc(acc_done, TPC)
            sp.sem_inc(comb_done, 2)
            sp.sem_inc(h_done, TPC)
            sp.sem_inc(x1_ready, TPC)
            sp.sem_inc(res_ready, TPC)
            sp.sem_inc(zt_saved, 1)
            for i in range(2):
                sp.sem_inc(res_stored[i], 16)
            for dst, src in ((cst, consts), (idx_sb, idx), (gbase_sb, gbase), (bq_sb, bq), (bk_sb, bk), (bv_sb, bv),
                             (bo_sb, bo), (bg_sb, bg), (temp_sb, temp), (be_raw, be3)):
                sp.dma_start(dst[:], src).then_inc(small_loaded, 16)
            sp.dma_start(wg_raw[:], wg.rearrange("(k p) e -> p k e", p=P)).then_inc(small_loaded, 16)
            for i, w in enumerate((wk, wv, wq, wo)):
                sp.dma_start(w_raw[:, i], w.rearrange("(k p) n -> p k n", p=P)).then_inc(w_loaded, 16)
            for c in range(2):
                sp.dma_start(x_raw[(c + 1) % 2][:], xT_v[:, :, c * CH:(c + 1) * CH]).then_inc(x_loaded[c], 16)
            for b in range(BATCH):
                sp.wait_ge(w_ready, 2 * b + 2)
                sp.dma_start(w_dram[b * H:(b + 1) * H].rearrange("s k j -> k s j"),
                             wk_sb[b % 2].rearrange("p s h k -> p (s h) k")).then_inc(w_stored[b % 2], 16)
            for i in range(2):
                sp.wait_ge(w_stored[i], 16 * BATCH // 2)
            sp.dma_start(g_all, w_dram.rearrange("s k j -> s (k j)")).then_inc(g_loaded, 16)
            with sp.Fori(0, BATCH) as b:
                for cc in range(CPB):
                    c = b * CPB + cc
                    sp.wait_ge(xl_ready, c + 2)
                    sp.dma_start(x_raw[(cc + 1) % 2][:],
                                 xT_v[:, :, bass.ds((c + 2) * CH, CH)]).then_inc(x_loaded[cc % 2], 16)
            sp.wait_ge(inv_done, 1)
            flat = winv_dram.rearrange("s k j -> s (k j)")
            sp.dma_start(flat[0:P], g_all).then_inc(winv_stored, 16)
            sp.dma_start(flat[P:P + H], g_all[0:H]).then_inc(winv_stored, 16)
            sp.wait_ge(xl_ready, NCH + 3)
            for c in range(2):
                sp.dma_start(x_raw[c][:], xT_v[:, :, c * CH:(c + 1) * CH]).then_inc(xq_loaded[c], 16)
            sp.wait_ge(winv_stored, 32)
            for sem_done, count in ((z_done, TPC * (NCH + 1)), (v_done, 2 * (NCH + 1)), (kl_done, 2 * (NCH + 2)),
                                    (aug_done, NCH + 2)):
                sp.wait_ge(sem_done, count)
            for i in range(2 * KC):
                k, half = i // 2, i % 2
                sp.dma_start(we_raw[i], we[k * P:(k + 1) * P, 1024 * half:1024 * (half + 1)]).then_inc(we_loaded, 16)
            winv_b = winv_dram.rearrange("s k j -> k s j")
            sp.dma_start(winv_sb[:], winv_b[:, 0:H, :]).then_inc(winv_loaded, 16)
            sp.dma_start(x_tok[0][:], x_v[0]).then_inc(xt_loaded[0], 16)
            with sp.Fori(0, BATCH) as b:
                for cc in range(CPB):
                    p = b * CPB + cc
                    sp.wait_ge(xql_ready, p + 1)
                    sp.dma_start(x_raw[cc % 2][:],
                                 xT_v[:, :, bass.ds((p + 2) * CH, CH)]).then_inc(xq_loaded[cc % 2], 16)
                    if cc == CPB - 2:
                        sp.wait_ge(y_done, b + 1)
                        sp.dma_start(winv_sb[:], winv_b[:, in_batch(b + 1, H), :]).then_inc(winv_loaded, 16)
                    sp.wait_ge(h_done, TPC * (p + 1))
                    sp.dma_start(x_tok[(cc + 1) % 2][:],
                                 x_v[bass.ds(p + 1, 1)].rearrange("a p t d -> (a p) t d")).then_inc(xt_loaded[(cc + 1) % 2], 16)
                    sp.wait_ge(res_ready, TPC * (p + 2))
                    sp.dma_start(out_v[bass.ds(p, 1)].rearrange("a p t d -> (a p) t d"),
                                 y_out[cc % 2][:]).then_inc(res_stored[cc % 2], 16)
            for i in range(2):
                sp.wait_ge(res_stored[i], 16 * (NCH // 2 + 1))

        @block.gpsimd
        def _(pool):
            own = Steps(pool, pool_step)
            pool.wait_ge(small_loaded, 16 * 11)
            nc.gpsimd.tensor_tensor(rows_sb[:], gbase_sb[:], idx_sb[:].broadcast_to([P, 4]), ALU.add).then_inc(rows_ready, 1)
            pool.wait_ge(rows_ready, 1)
            for i in range(4):
                nc.gpsimd.indirect_dma_start(
                    out=lm_x[:, i, :], out_offset=None, in_=x,
                    in_offset=bass.IndirectOffsetOnAxis(ap=rows_sb[:, i:i + 1].bitcast(u32), axis=0)).then_inc(gathered, 16)
            nc.gpsimd.memset(v_aug[0][:], 0.0)
            own.then(nc.gpsimd.memset(v_aug[1][:], 0.0))
            for i in range(2):
                last = nc.gpsimd.memset(v_aug[i][:, :, :, HD:HD + 1], 1.0)
            last.then_inc(const_set, 1)

            def block_lo(b, at):
                for s in range(KC):
                    last = nc.gpsimd.tensor_tensor(
                        bdl[at][:, s], rep(l2l[:, s, in_batch(b)], 1, HPS),
                        rep(cst[:, C_HEAD:C_HEAD + HPS], 2, NL), ALU.mult)
                return last

            pool.wait_ge(l2_ready, 1)
            for b in range(BATCH):
                if b >= 2:
                    pool.wait_ge(dist_done, 2 * (b - 1))
                block_lo(b, b % 2).then_inc(bdl_ready, 1)
            rows = NL // GJ_PIECES
            with pool.Fori(0, NL) as s:
                pool.wait_ge(gj_ready, s + 1)
                for q in range(GJ_POOL):
                    r = slice(q * rows, (q + 1) * rows)
                    nc.gpsimd.tensor_tensor(t3[:, r, :], rep(gj_f[:, r], 2, NL), rep(gj_r[:], 1, rows),
                                            ALU.mult).then_inc(gj_prod, 1)

            def layernorm_coefs(mv, ve, rs, nt, nm, cols):
                own.then(nc.gpsimd.tensor_tensor(ve[:, cols], mv[:, cols, 1], cst[:, C_EPS:C_EPS + TPC][:, cols], ALU.add))
                own.then(nc.gpsimd.tensor_tensor(rs[:, cols], ve[:, cols], cst[:, C_EXP:C_EXP + TPC][:, cols], ALU.pow))
                own.then(nc.gpsimd.tensor_tensor(nt[:, cols], mv[:, cols, 0], rs[:, cols], ALU.mult))
                return nc.gpsimd.tensor_tensor(nm[:, cols], nt[:, cols], cst[:, C_MINUS:C_MINUS + TPC][:, cols], ALU.mult)

            def block_q(b):
                for s in range(KC):
                    for dst, src in ((bdh[0], l2h), (bdl[0], l2l)):
                        last = nc.gpsimd.tensor_tensor(
                            dst[:, s], rep(src[:, s, in_batch(b)], 1, HPS),
                            rep(cst[:, C_HEAD:C_HEAD + HPS], 2, NL), ALU.mult)
                last.then_inc(qbd_ready, 1)

            def split_lo(c, at):
                pool.wait_ge(xqh_ready, c + 1)
                nc.gpsimd.tensor_tensor(xl[at][:], x_raw[at][:], raw(xh[at][:]), ALU.subtract).then_inc(xql_ready, 1)

            def attn_lo(c, s):
                pool.wait_ge(attnh_ready, 2 * c + s + 1)
                nc.gpsimd.tensor_tensor(attn_l[:, s], attn[:, s], raw(attn_h[:, s]), ALU.subtract).then_inc(attnl_ready, 1)

            def residual(at, turn):
                pool.wait_ge(xt_loaded[at], 16 * (turn + 1))
                nc.gpsimd.tensor_tensor(x_tok[at][:], x_tok[at][:], rep(bo_sb[:], 1, TPC), ALU.add).then_inc(xb_ready, 1)

            def ln2(p, t):
                pool.wait_ge(ln2_stats, TPC * p + t + 1)
                layernorm_coefs(mv2, ve2, rs2, nt2, nm2, slice(t, t + 1)).then_inc(ln2_coef, 1)

            pool.wait_ge(dist_done, W_EXPS + 8 * NCH)
            pool.wait_ge(bd_ready, 2 * BATCH + 1)
            block_q(0)
            pool.wait_ge(vproj_done, 2 * (NCH + 1))
            split_lo(0, 0)
            split_lo(1, 1)
            residual(0, 0)
            attn_lo(0, 0)
            attn_lo(0, 1)
            with pool.Fori(0, BATCH) as b:
                own.enter(b, CPB * (3 + 3 * TPC))
                for cc in range(CPB):
                    p = b * CPB + cc
                    if cc == CPB - 1:
                        pool.wait_ge(qdist_done, PAIRS * (p + 1))
                        block_q(b + 1)
                    pool.wait_ge(ln1_stats, p + 1)
                    layernorm_coefs(mv1, ve1, rs1, nt1, nm1, slice(0, TPC)).then_inc(ln1_coef, 1)
                    split_lo(p + 2, cc % 2)
                    attn_lo(p + 1, 0)
                    ln2(p, 0)
                    ln2(p, 1)
                    ln2(p, 2)
                    attn_lo(p + 1, 1)
                    ln2(p, 3)
                    residual((cc + 1) % 2, 2 * b + (cc + 1) // 2)
                own.leave(BATCH)

        @block.scalar
        def _(act):
            def split_hi(at, ready):
                nc.scalar.activation(xh[at][:], x_raw[at][:], ACT.Copy).then_inc(ready, 1)

            act.wait_ge(small_loaded, 16 * 11)
            act.wait_ge(w_loaded, 64)
            nc.scalar.activation(wh[:], w_raw, ACT.Copy).then_inc(w_split_h, 1)
            for k in range(KC):
                act.wait_ge(lmT_done, k + 1)
                last = nc.scalar.activation(xh[0][:, k], bank[k][:], ACT.Copy)
            last.then_inc(xh_ready, 1)
            for s in range(KC):
                act.wait_ge(kproj_done, s + 1)
                nc.scalar.activation(kh[0][:, s], bank[2 + s][:], ACT.Identity, bias=bk_sb[:, s:s + 1])
                nc.scalar.activation(sq[:, s], bank[2 + s][:], ACT.Square, bias=bk_sb[:, s:s + 1]).then_inc(s_ready, 1)
            act.wait_ge(setup_done, 1)
            act.wait_ge(nl_done, 1)
            nc.scalar.activation(nlt[:, 0:BATCH, :].rearrange("p b i -> p (b i)"), bank[5][:, 0:BATCH * PAIRS], ACT.Copy,
                                 scale=invt[:]).then_inc(nl_ready, 1)
            act.wait_ge(nl_ready, 1)
            nc.scalar.activation(nlt[:, BATCH, :], nlt[:, 0, :], ACT.Copy).then_inc(nl_ready, 1)
            for b in range(BATCH):
                for s in range(KC):
                    act.wait_ge(dist_done, 2 * b + s + 1)
                    if b >= 2:
                        act.wait_ge(w_stored[b % 2], 16 * (b // 2))
                    nc.scalar.activation(wk_sb[b % 2][:, s].rearrange("p h k -> p (h k)"), bank[6 + s][0:64, :],
                                         ACT.Exp, scale=invt[0:64, :]).then_inc(exp_done, 1)

            def exps(c, t):
                for s in range(KC):
                    n = 2 * t + s
                    act.wait_ge(dist_done, W_EXPS + 8 * c + n + 1)
                    if s == 0:
                        act.wait_ge(z_done, TPC * c + t + 1)
                    nc.scalar.activation(phi[:, n], bank[6 + s][:], ACT.Exp, scale=invt[:]).then_inc(exp_done, 1)

            def keys(c, at):
                for s in range(KC):
                    act.wait_ge(kproj_done, 2 * (c + 1) + s + 1)
                    if s == 0:
                        act.wait_ge(norm_done, c + 1)
                    nc.scalar.activation(kh[at][:, s], bank[2 + s][:], ACT.Identity, bias=bk_sb[:, s:s + 1])
                    nc.scalar.activation(sq[:, s], bank[2 + s][:], ACT.Square, bias=bk_sb[:, s:s + 1]).then_inc(s_ready, 1)

            act.wait_ge(x_loaded[0], 16)
            split_hi(1, xh_ready)
            act.wait_ge(kproj_done, 2)
            act.wait_ge(x_loaded[1], 16)
            split_hi(0, xh_ready)
            keys(0, 1)
            act.wait_ge(dist_done, W_EXPS)
            act.wait_ge(l2_ready, 1)
            with act.Fori(0, BATCH) as b:
                for cc in range(CPB):
                    c = b * CPB + cc
                    exps(c, 0)
                    act.wait_ge(dist_done, W_EXPS + 8 * c)
                    keys(c + 1, cc % 2)
                    exps(c, 1)
                    exps(c, 2)
                    exps(c, 3)
                    act.wait_ge(x_loaded[cc % 2], 16 * (2 * b + cc // 2 + 2))
                    act.wait_ge(vproj_done, 2 * (c + 1))
                    split_hi((cc + 1) % 2, xh_ready)
                    if cc == CPB - 1:
                        act.wait_ge(z_done, TPC * (c + 2))
                        nc.scalar.activation(zt[:, bass.ds(b, 1), :].rearrange("p a z -> p (a z)"),
                                             bank[5][:, 0:4 * NL], ACT.Copy).then_inc(zt_saved, 1)
            act.wait_ge(zt_saved, BATCH + 1)
            nc.scalar.activation(zt[:, BATCH, :], zt[:, 0, :], ACT.Copy).then_inc(zt_saved, 1)
            act.wait_ge(zt_saved, BATCH + 2)

            def z_of_batch(b):
                act.wait_ge(ztr_done, b)
                nc.scalar.activation(zt_cur[:], zt[:, bass.ds(b, 1), :].rearrange("p a z -> p (a z)"),
                                     ACT.Copy).then_inc(zt_cur_ready, 1)

            def norms_of_batch(b):
                nc.scalar.activation(nlt_cur[:], nlt[:, bass.ds(b, 1), :].rearrange("p a i -> p (a i)"),
                                     ACT.Copy).then_inc(nlt_ready, 1)
                act.wait_ge(nlt_ready, b + 1)

            def z_landmark_major(b):
                act.wait_ge(ztr_done, b + 1)
                act.wait_ge(y_done, b)
                nc.scalar.activation(zk[:], bank[5][0:64, :], ACT.Copy).then_inc(zk_ready, 1)

            def queries(c):
                for s in range(KC):
                    act.wait_ge(qproj_done, 2 * c + s + 1)
                    if s == 0:
                        act.wait_ge(qdist_done, PAIRS * c)
                        act.wait_ge(qnorm_done, c)
                    nc.scalar.activation(kh[0][:, s], bank[6 + s][:], ACT.Identity, bias=bq_sb[:, s:s + 1])
                    nc.scalar.activation(sq[:, s], bank[6 + s][:], ACT.Square, bias=bq_sb[:, s:s + 1]).then_inc(qs_ready, 1)

            def q_exps(c, half):
                for i in range(4 * half, 4 * half + 4):
                    act.wait_ge(qdist_done, PAIRS * c + i + 1)
                    if i == 4 * half:
                        act.wait_ge(out_done, 2 * c)
                    nc.scalar.activation(phi[:, i], bank[6 + i % 2][:], ACT.Exp,
                                         bias=nlt_cur[:, i:i + 1], scale=invt[:]).then_inc(qexp_done, 1)

            def attn_hi(c, s):
                act.wait_ge(attn_ready, 2 * c + s + 1)
                act.wait_ge(wo_done, 2 * c)
                nc.scalar.activation(attn_h[:, s], attn[:, s], ACT.Copy).then_inc(attnh_ready, 1)

            def query_hi(c, at, turn):
                act.wait_ge(xq_loaded[at], 16 * (turn + 1))
                act.wait_ge(qproj_done, 2 * c - 2)
                split_hi(at, xqh_ready)

            def result(p, t, at, turn):
                act.wait_ge(ln2_coef, TPC * p + t + 1)
                if t == 0:
                    act.wait_ge(res_stored[at], 16 * (turn + 1))
                nc.scalar.activation(y_out[at][:, t], acc[:, t], ACT.Identity, bias=nm2[:, t:t + 1],
                                     scale=rs2[:, t:t + 1]).then_inc(res_ready, 1)

            act.wait_ge(vproj_done, 2 * (NCH + 1))
            for c in range(2):
                act.wait_ge(xq_loaded[c], 16)
                split_hi(c, xqh_ready)
            act.wait_ge(winv_stored, 32)
            for i in range(2 * KC):
                act.wait_ge(we_loaded, 32 * KC)
                nc.scalar.activation(weh[:, i // 2, 1024 * (i % 2):1024 * (i % 2 + 1)], we_raw[i],
                                     ACT.Copy).then_inc(w_split_h, 1)
            act.wait_ge(v_done, 2 * (NCH + 1))
            act.wait_ge(norm_done, NCH + 2)
            z_of_batch(0)
            norms_of_batch(0)
            queries(0)
            z_landmark_major(0)
            q_exps(0, 0)
            attn_hi(0, 0)
            q_exps(0, 1)
            attn_hi(0, 1)
            with act.Fori(0, BATCH) as b:
                for cc in range(CPB):
                    p = b * CPB + cc
                    c = p + 1
                    if cc == CPB - 1:
                        z_of_batch(b + 1)
                    queries(c)
                    if cc == CPB - 1:
                        z_landmark_major(b + 1)
                        act.wait_ge(qexp_done, PAIRS * (c + 1))
                        norms_of_batch(b + 1)
                    act.wait_ge(ln1_coef, p + 1)
                    for t in range(TPC):
                        nc.scalar.activation(x1[:, t], h_res[:, t], ACT.Identity, bias=nm1[:, t:t + 1],
                                             scale=rs1[:, t:t + 1]).then_inc(x1_ready, 1)
                    for tp in range(2):
                        act.wait_ge(x1t_done, 2 * p + tp + 1)
                        nc.scalar.activation(x1h[:, :, tp * 256:tp * 256 + 256].rearrange("p k (t j) -> p t k j", t=2),
                                             bank[tp][:].rearrange("p (t k j) -> p t k j", t=2, k=KC),
                                             ACT.Copy).then_inc(x1h_ready, 1)
                    q_exps(c, 0)
                    query_hi(p + 2, cc % 2, 2 * b + cc // 2 + 1)
                    act.wait_ge(gd_ready, p + 1)
                    nc.scalar.activation(ge[:], gd[:], ACT.Exp).then_inc(ge_ready, 1)
                    act.wait_ge(gtr_done, p + 1)
                    nc.scalar.activation(g_t[:], bank[1][0:24, :], ACT.Copy).then_inc(gt_ready, 1)
                    attn_hi(c, 0)
                    result(p, 0, cc % 2, 2 * b + cc // 2)
                    q_exps(c, 1)
                    result(p, 1, cc % 2, 2 * b + cc // 2)
                    result(p, 2, cc % 2, 2 * b + cc // 2)
                    attn_hi(c, 1)
                    result(p, 3, cc % 2, 2 * b + cc // 2)

        @block.vector
        def _(dve):
            own = Steps(dve, dve_step)
            V = nc.vector
            V.memset(zero_c[:], 0.0)
            V.memset(raw(augk[0][:]), 1.0)
            V.memset(raw(augk[1][:]), 1.0)
            own.did(V.memset(minus1[:], -1.0))
            dve.wait_ge(small_loaded, 16 * 11)
            V.reciprocal(invt[:], temp_sb[:])
            own.then(V.tensor_scalar(tpos[:], temp_sb[:], 0.0, None, ALU.is_gt))
            own.then(V.tensor_scalar(phi_min[:], tpos[:], -1.0, 1.0, ALU.mult, ALU.add))
            V.scalar_tensor_tensor(phi_max[:], phi_min[:], BIG, tpos[:], ALU.mult, ALU.add)
            mask = cst[0:32, C_M16:C_M16 + H]
            V.tensor_copy(sel_q[:].rearrange("p i (u k) -> p i u k", u=2),
                          rep(mask.rearrange("p (i u) -> p i u", u=2), 3, NL))
            for i in range(2):
                last = V.tensor_copy(augm[i][0:32], rep(mask.rearrange("p (s h) -> p s h", s=KC), 3, NL))
            V.tensor_copy(be_tmp[:], be_raw[:])
            own.then(V.tensor_copy(wg_s[:, :, 0:E], wg_raw[:]))
            V.tensor_tensor(wg_s[:, :, E:2 * E], wg_raw[:], raw(wg_s[:, :, 0:E]), ALU.subtract)
            V.scalar_tensor_tensor(be_s[:], raw(be_tmp[:]), cst[0:24, C_BES:C_BES + 1], be_raw[:], ALU.mult,
                                   ALU.add).then_inc(setup_done, 1)
            dve.wait_ge(w_split_h, 1)
            V.tensor_tensor(wl[:], w_raw, raw(wh[:]), ALU.subtract).then_inc(w_split_l, 1)
            dve.wait_ge(xh_ready, 1)
            for k in range(KC):
                last = V.tensor_tensor(xl[0][:, k], bank[k][:], raw(xh[0][:, k]), ALU.subtract)
            last.then_inc(xl_ready, 1)

            def project_lo(dst, hi, src, bias, s):
                return V.scalar_tensor_tensor(dst[:, s], src[:], bias[:, s:s + 1], raw(hi[:, s]), ALU.add, ALU.subtract)

            def norm_rows(dst, src):
                own.then(V.tensor_copy(aug_hi[:], src[0:32, :]))
                return V.scalar_tensor_tensor(dst, raw(aug_hi[:]), lo_sign[0:32, :], src[0:32, :], ALU.mult, ALU.add)

            for s in range(KC):
                dve.wait_ge(s_ready, s + 1)
                project_lo(kl[0], kh[0], bank[2 + s], bk_sb, s).then_inc(kl_done, 1)
            dve.wait_ge(kl_done, 2)
            V.tensor_scalar(l2h[:, :, 0:BATCH * NL], raw(kh[0][:]), 2.0, None, ALU.mult)
            V.tensor_scalar(l2l[:, :, 0:BATCH * NL], raw(kl[0][:]), 2.0, None, ALU.mult)
            V.tensor_scalar(l2h[:, :, BATCH * NL:], raw(kh[0][:, :, 0:NL]), 2.0, None, ALU.mult)
            V.tensor_scalar(l2l[:, :, BATCH * NL:], raw(kl[0][:, :, 0:NL]), 2.0, None, ALU.mult).then_inc(l2_ready, 1)
            dve.wait_ge(norm_done, 1)
            norm_rows(augk[0][0:32, :], bank[4]).then_inc(aug_done, 1)
            dve.wait_ge(aug_done, 1)
            V.tensor_copy(ln_rows[32:64, 0:BATCH * NL], raw(augk[0][0:32, :]))
            own.then(V.tensor_copy(ln_rows[32:64, BATCH * NL:], raw(augk[0][0:32, 0:NL])))

            def block_hi(b, at, low):
                for s in range(KC):
                    V.tensor_tensor(bdh[at][:, s], rep(l2h[:, s, in_batch(b)], 1, HPS),
                                    rep(cst[:, C_HEAD:C_HEAD + HPS], 2, NL), ALU.mult)
                    if low:
                        V.tensor_tensor(bdl[at][:, s], rep(l2l[:, s, in_batch(b)], 1, HPS),
                                        rep(cst[:, C_HEAD:C_HEAD + HPS], 2, NL), ALU.mult)
                    last = V.tensor_tensor(augm[at][32:64, s], rep(ln_rows[32:64, in_batch(b)], 1, HPS),
                                           rep(cst[32:64, C_M16 + HPS * s:C_M16 + HPS * (s + 1)], 2, NL), ALU.mult)
                return last

            def kernel_matrix(b):
                for s in range(KC):
                    dve.wait_ge(exp_done, 2 * b + s + 1)
                    w = wk_sb[b % 2][:, s]
                    own.then(V.tensor_scalar(w, w, phi_max[0:64, :], phi_min[0:64, :], ALU.min, ALU.max))
                    V.tensor_tensor(w, w, rep(cst[0:64, C_REG:C_REG + NL], 1, HPS), ALU.add).then_inc(w_ready, 1)

            dve.wait_ge(l2_ready, 1)
            for b in range(BATCH):
                if b >= 2:
                    dve.wait_ge(dist_done, 2 * (b - 1))
                block_hi(b, b % 2, False).then_inc(bd_ready, 1)
                if b >= 1:
                    kernel_matrix(b - 1)
            kernel_matrix(BATCH - 1)

            def clamp(c, t):
                for s in range(KC):
                    n = 2 * t + s
                    dve.wait_ge(exp_done, W_EXPS + 8 * c + n + 1)
                    V.tensor_scalar(phi[:, n], phi[:, n], phi_max[:], phi_min[:], ALU.min, ALU.max).then_inc(phi_ready, 1)

            def keys_lo(c, at):
                for s in range(KC):
                    dve.wait_ge(s_ready, 2 * (c + 1) + s + 1)
                    project_lo(kl[at], kh[at], bank[2 + s], bk_sb, s).then_inc(kl_done, 1)

            def values(c, tp, at):
                dve.wait_ge(vproj_done, 2 * c + tp + 1)
                dve.wait_ge(z_done, TPC * c)
                V.tensor_tensor(v_aug[at][:, 2 * tp:2 * tp + 2, :, 0:HD],
                                bank[tp][:].rearrange("p (t h d) -> p t h d", t=2, h=H),
                                rep(bv_sb[:].rearrange("p (h d) -> p h d", h=H), 1, 2), ALU.add).then_inc(v_done, 1)

            def key_norms(c, at):
                dve.wait_ge(norm_done, c + 2)
                norm_rows(augk[at][0:32, :], bank[4]).then_inc(aug_done, 1)

            def split_lo(c, at):
                dve.wait_ge(xh_ready, c + 2)
                V.tensor_tensor(xl[at][:], x_raw[at][:], raw(xh[at][:]), ALU.subtract).then_inc(xl_ready, 1)

            def gj_begin(s):
                at = bass.ds(s, 1)
                column = g3[:, :, at].rearrange("p r a -> p (r a)")
                row = g3[:, at, :].rearrange("p a c -> p (a c)")
                V.tensor_scalar(gj_f[:], column, 1.0, None, ALU.mult)
                own.then(V.reciprocal(gj_p[:], g3[:, at, at].rearrange("p a c -> p (a c)")))
                own.then(V.tensor_scalar(gj_r[:], row, gj_p[:], None, ALU.mult))
                V.tensor_scalar(gj_r[:, at], gj_p[:], 1.0, None, ALU.mult)
                V.tensor_copy(gj_f[:, at], minus1[:])
                own.then(V.tensor_scalar(column, zero_c[:], 1.0, None, ALU.mult))
                V.tensor_scalar(row, zero_c[:], 1.0, None, ALU.mult).then_inc(gj_ready, 1)

            def gj_update(s, pieces):
                for q in pieces:
                    r = slice(q * rows, (q + 1) * rows)
                    if q < GJ_POOL:
                        dve.wait_ge(gj_prod, GJ_POOL * s + q + 1)
                    else:
                        dve.wait_ge(gj_ready, s + 1)
                        own.then(V.tensor_tensor(t3[:, r, :], rep(gj_f[:, r], 2, NL), rep(gj_r[:], 1, rows), ALU.mult))
                    own.did(V.tensor_tensor(g3[:, r, :], g3[:, r, :], t3[:, r, :], ALU.subtract))

            rows = NL // GJ_PIECES
            dve.wait_ge(x_loaded[0], 16)
            split_lo(0, 1)
            keys_lo(0, 1)
            dve.wait_ge(const_set, 1)
            for tp in range(2):
                values(0, tp, 0)
            key_norms(0, 1)
            dve.wait_ge(x_loaded[1], 16)
            split_lo(1, 0)
            block_hi(0, 0, True).then_inc(bd_ready, 1)
            dve.wait_ge(g_loaded, 16)
            with dve.Fori(0, BATCH) as b:
                own.enter(b, CPB * (1 + 2 * (3 + GJ_PIECES + 1)))
                for cc in range(CPB):
                    c = b * CPB + cc
                    own.wait()
                    gj_begin(2 * c)
                    clamp(c, 0)
                    keys_lo(c + 1, cc % 2)
                    gj_update(2 * c, [3])
                    values(c + 1, 0, (cc + 1) % 2)
                    clamp(c, 1)
                    gj_update(2 * c, [0])
                    gj_update(2 * c, [1])
                    clamp(c, 2)
                    gj_update(2 * c, [2])
                    values(c + 1, 1, (cc + 1) % 2)
                    own.wait()
                    gj_begin(2 * c + 1)
                    clamp(c, 3)
                    if cc == CPB - 1:
                        dve.wait_ge(dist_done, W_EXPS + 8 * (c + 1))
                        block_hi(b + 1, 0, True).then_inc(bd_ready, 1)
                    dve.wait_ge(dist_done, W_EXPS + 8 * c)
                    key_norms(c + 1, cc % 2)
                    gj_update(2 * c + 1, [3])
                    split_lo(c + 2, (cc + 1) % 2)
                    gj_update(2 * c + 1, [0, 1, 2])
                own.leave(BATCH)
            own.wait()
            V.tensor_copy(minus1[:], minus1[:]).then_inc(inv_done, 1)

            def queries_lo(c):
                for s in range(KC):
                    dve.wait_ge(qs_ready, 2 * c + s + 1)
                    project_lo(kl[0], kh[0], bank[6 + s], bq_sb, s).then_inc(ql_done, 1)

            def query_norms(c):
                dve.wait_ge(qnorm_done, c + 1)
                norm_rows(augk[0][0:32, :], bank[4]).then_inc(qaug_done, 1)

            def q_clamp(c, half):
                for i in range(4 * half, 4 * half + 4):
                    dve.wait_ge(qexp_done, PAIRS * (c + 1) + i + 1)
                    V.tensor_scalar(phi[:, i], phi[:, i], phi_max[:], phi_min[:], ALU.min, ALU.max).then_inc(qphi_ready, 1)

            def landmark_values(b):
                dve.wait_ge(y_done, b + 1)
                y = bank[4][:, 0:PAIRS * 32].rearrange("p (i c) -> p i c", i=PAIRS)
                for u in range(2):
                    half = slice(64 * u, 64 * u + 64)
                    V.tensor_copy(y_cur[half, :, 16 * u:16 * u + 16], y[half, :, 0:HD])
                    last = V.tensor_copy(y_cur[half, :, 32 + 16 * u:48 + 16 * u],
                                         y[half, :, HD:HD + 1].broadcast_to([64, PAIRS, HD]))
                last.then_inc(y_ready, 1)

            def normalise(c, s):
                dve.wait_ge(out_done, 2 * c + s + 1)
                own.then(V.tensor_scalar(nrm[:], bank[5][:], NORM_MIN, None, ALU.max))
                own.then(V.reciprocal(rcp[:], nrm[:]))
                if not isinstance(c, int):
                    dve.wait_ge(attnl_ready, 2 * c + s - 1)
                V.tensor_tensor(attn[:, s], bank[4][:], rcp[:], ALU.mult).then_inc(attn_ready, 1)

            def residual_stats(p, at):
                dve.wait_ge(xb_ready, p + 1)
                dve.wait_ge(x1_ready, TPC * (p + 1))
                for t in range(TPC):
                    if t % 2 == 0:
                        dve.wait_ge(wo_done, 2 * p + t // 2 + 1)
                    V.tensor_tensor(h_res[:, t], bank[t // 2][:, 256 * (t % 2):256 * (t % 2) + 256], x_tok[at][:, t],
                                    ALU.add).then_inc(h_done, 1)
                dve.wait_ge(h_done, TPC * (p + 2))
                for t in range(TPC):
                    step = V.bn_stats(st1[:, t], h_res[:, t])
                own.then(step)
                dve.sem_inc(dve_waited, 1)
                for t in range(TPC):
                    step = V.bn_aggr(mv1[:, t], st1[:, t])
                step.then_inc(ln1_stats, 1)

            def gates(p):
                dve.wait_ge(gate_done, p + 1)
                logit = bank[0][:, 0:TPC * 2 * E].rearrange("p (t e) -> p t e", t=TPC)
                own.then(V.tensor_tensor(lg0[:], logit[:, :, 0:E], rep(bg_sb[:], 1, TPC), ALU.add))
                V.tensor_tensor(lg[:], logit[:, :, E:2 * E], lg0[:], ALU.add).then_inc(gate_read, 1)
                dve.wait_ge(gate_read, p + 1)
                dve.sem_inc(dve_waited, 1)
                for t in range(TPC):
                    step = V.max(m8[:, t], lg[:, t])
                own.then(step)
                V.tensor_tensor(gd[:], m8[:, :, 1], m8[:, :, 0], ALU.subtract).then_inc(gd_ready, 1)
                for t in range(TPC):
                    step = V.max_index(i8[:, t], m8[:, t], lg[:, t])
                own.then(step)
                own.then(V.tensor_copy(if2[:], i8[:, :, 0:2]))
                iota = rep(cst[:, C_IOTA:C_IOTA + E], 1, TPC)
                V.tensor_tensor(oh1[:], iota, rep(if2[:, :, 0], 2, E), ALU.is_equal)
                V.tensor_tensor(oh2[:], iota, rep(if2[:, :, 1], 2, E), ALU.is_equal)
                dve.wait_ge(ge_ready, p + 1)
                own.then(V.tensor_scalar(gs[:], ge[:], 1.0, None, ALU.add))
                own.then(V.reciprocal(gw1[:], gs[:]))
                own.then(V.tensor_tensor(gw2[:], gw1[:], ge[:], ALU.mult))
                V.tensor_tensor(oh1[:], oh1[:], rep(gw1[:], 2, E), ALU.mult)
                own.then(V.tensor_tensor(oh2[:], oh2[:], rep(gw2[:], 2, E), ALU.mult))
                own.then(V.tensor_tensor(gate[:], oh1[:], oh2[:], ALU.add))
                own.then(V.tensor_copy(gate_h[:], gate[:]))
                V.tensor_copy(g_st[:, :, 0:E], raw(gate_h[:]))
                V.tensor_tensor(g_st[:, :, E:2 * E], gate[:], raw(gate_h[:]), ALU.subtract)
                V.tensor_copy(g_st[:, :, 2 * E:3 * E], raw(gate_h[:])).then_inc(gst_ready, 1)
                dve.wait_ge(gst_ready, p + 1)

            def combine(p, t):
                if t == 0:
                    dve.wait_ge(res_ready, TPC * (p + 1))
                    dve.wait_ge(x1_ready, TPC * (p + 2))
                for e in range(E):
                    n = 16 * p + 4 * t + e // 2
                    if e % 2 == 0:
                        dve.wait_ge(ffn_done, n + 1)
                    src = bank[2 + (e // 2) % 2][:, 256 * (e % 2):256 * (e % 2) + 256]
                    step = V.scalar_tensor_tensor(acc[:, t], src, gate[:, t, e:e + 1], x1[:, t] if e == 0 else acc[:, t],
                                                  ALU.mult, ALU.add)
                    if e % 2 == 0:
                        own.then(step)
                    else:
                        step.then_inc(comb_done, 1)
                        dve.wait_ge(comb_done, 2 + n + 1)

            def result_stats(p, t):
                if t % 2 == 0:
                    dve.wait_ge(be_done, 2 * p + t // 2 + 1)
                V.tensor_tensor(acc[:, t], bank[t // 2][:, 256 * (t % 2):256 * (t % 2) + 256], acc[:, t],
                                ALU.add).then_inc(acc_done, 1)
                dve.wait_ge(acc_done, TPC * (p + 1) + t + 1)
                own.then(V.bn_stats(st2[:, t], acc[:, t]))
                dve.sem_inc(dve_waited, 1)
                V.bn_aggr(mv2[:, t], st2[:, t]).then_inc(ln2_stats, 1)

            dve.wait_ge(z_done, TPC * (NCH + 1))
            dve.wait_ge(winv_stored, 32)
            own.then(V.memset(y_cur[:], 0.0))
            for i in range(2 * KC):
                dve.wait_ge(w_split_h, i + 2)
                k, half = i // 2, slice(1024 * (i % 2), 1024 * (i % 2 + 1))
                V.tensor_tensor(wel[:, k, half], we_raw[i], raw(weh[:, k, half]), ALU.subtract).then_inc(w_split_l, 1)
            dve.wait_ge(w_split_l, 1 + 2 * KC)
            queries_lo(0)
            query_norms(0)
            q_clamp(0, 0)
            landmark_values(0)
            normalise(0, 0)
            q_clamp(0, 1)
            normalise(0, 1)
            with dve.Fori(0, BATCH) as b:
                own.enter(b, CPB * (1 + 1 + 10 + 2 * KC + TPC * (E // 2 + 1)))
                for cc in range(CPB):
                    p = b * CPB + cc
                    residual_stats(p, cc % 2)
                    queries_lo(p + 1)
                    query_norms(p + 1)
                    for tp in range(2):
                        dve.wait_ge(x1h_ready, 2 * p + tp + 1)
                        V.tensor_tensor(x1l[:, :, tp * 256:tp * 256 + 256].rearrange("p k (t j) -> p t k j", t=2),
                                        bank[tp][:].rearrange("p (t k j) -> p t k j", t=2, k=KC),
                                        raw(x1h[:, :, tp * 256:tp * 256 + 256]).rearrange("p k (t j) -> p t k j", t=2),
                                        ALU.subtract).then_inc(x1l_ready, 1)
                    q_clamp(p + 1, 0)
                    gates(p)
                    if cc == CPB - 1:
                        landmark_values(b + 1)
                    combine(p, 0)
                    normalise(p + 1, 0)
                    result_stats(p, 0)
                    combine(p, 1)
                    result_stats(p, 1)
                    q_clamp(p + 1, 1)
                    combine(p, 2)
                    result_stats(p, 2)
                    normalise(p + 1, 1)
                    combine(p, 3)
                    result_stats(p, 3)
                own.leave(BATCH)

        @block.tensor
        def _(pe):
            mm = nc.tensor.matmul
            WK, WV, WQ, WO = range(4)

            def project_T(w, at, s, dst):
                cols = slice(s * P, (s + 1) * P)
                for k in range(KC):
                    last = product3(dst, wh[:, w, k, cols], wl[:, w, k, cols], xh[at][:, k], xl[at][:, k],
                                    k == 0, k == KC - 1)
                return last

            def square_norms(dst):
                for s in range(KC):
                    last = mm(dst[0:32, :], neg_block[:, s, :], sq[:, s], start=(s == 0), stop=(s == KC - 1))
                return last

            pe.wait_ge(small_loaded, 16 * 11)
            pe.wait_ge(gathered, 64)
            for k in range(KC):
                for i in range(4):
                    last = nc.tensor.transpose(bank[k][:, i * P:(i + 1) * P], lm_x[:, i, k * P:(k + 1) * P], ident)
                last.then_inc(lmT_done, 1)
            pe.wait_ge(w_split_l, 1)
            pe.wait_ge(xl_ready, 1)
            for s in range(KC):
                project_T(WK, 0, s, bank[2 + s][:]).then_inc(kproj_done, 1)
            pe.wait_ge(s_ready, 2)
            square_norms(bank[4]).then_inc(norm_done, 1)
            for b in range(BATCH):
                for s in range(KC):
                    for u in range(2):
                        at = b * PAIRS + s * 4
                        last = mm(bank[5][64 * u:64 * u + 64, at:at + 4], sq[:, s, b * NL:(b + 1) * NL],
                                  neg_sel[:, u, :], start=True, stop=True)
            last.then_inc(nl_done, 1)
            pe.wait_ge(aug_done, 1)
            pe.wait_ge(setup_done, 1)

            def key_dists(dst, at, tok, bd, s):
                wide = lambda a: a.rearrange("p h k -> p (h k)")
                mm(dst, kh[at][:, s, tok], wide(bdh[bd][:, s]), start=True, stop=False)
                mm(dst, kl[at][:, s, tok], wide(bdh[bd][:, s]), start=False, stop=False)
                mm(dst, kh[at][:, s, tok], wide(bdl[bd][:, s]), start=False, stop=False)
                return mm(dst, augk[at][:, tok], wide(augm[bd][:, s]), start=False, stop=True)

            for b in range(BATCH):
                pe.wait_ge(bd_ready, b + 1)
                pe.wait_ge(bdl_ready, b + 1)
                for s in range(KC):
                    if b:
                        pe.wait_ge(exp_done, 2 * b + s - 1)
                    key_dists(bank[6 + s][0:64, :], 0, slice(b * NL, (b + 1) * NL), b % 2, s).then_inc(dist_done, 1)

            def keys(c, at):
                pe.wait_ge(xh_ready, c + 2)
                pe.wait_ge(xl_ready, c + 2)
                pe.wait_ge(kl_done, 2 * (c + 1))
                for s in range(KC):
                    project_T(WK, at, s, bank[2 + s][:]).then_inc(kproj_done, 1)

            def values(c, tp, at):
                if isinstance(c, int):
                    pe.wait_ge(xl_ready, 1)
                else:
                    pe.wait_ge(v_done, 2 * c + tp - 1)
                for t in (2 * tp, 2 * tp + 1):
                    tok = slice(t * P, (t + 1) * P)
                    dst = bank[tp][:, 256 * (t % 2):256 * (t % 2) + 256]
                    for k in range(KC):
                        last = product3(dst, xh[at][:, k, tok], xl[at][:, k, tok], wh[:, WV, k], wl[:, WV, k],
                                        k == 0, k == KC - 1)
                last.then_inc(vproj_done, 1)

            def key_norms(c):
                pe.wait_ge(s_ready, 2 * (c + 2))
                pe.wait_ge(aug_done, c + 1)
                square_norms(bank[4]).then_inc(norm_done, 1)

            def dists(c, t, at):
                if t == 0:
                    pe.wait_ge(kl_done, 2 * (c + 2))
                    pe.wait_ge(aug_done, c + 2)
                for s in range(KC):
                    pe.wait_ge(exp_done, W_EXPS + 8 * c + 2 * t + s - 1)
                    key_dists(bank[6 + s][:], at, slice(t * P, (t + 1) * P), 0, s).then_inc(dist_done, 1)

            def sums(c, t, at, first, last_tile):
                pe.wait_ge(phi_ready, 8 * c + 2 * t + 2)
                for g in range(4):
                    for j in range(4):
                        head = 4 * g + j
                        s, hs = head // HPS, head % HPS
                        last = mm(bank[5][32 * j:32 * j + 32, g * NL:(g + 1) * NL], v_aug[at][:, t, head, :],
                                  phi[:, 2 * t + s, hs * NL:(hs + 1) * NL], start=(first and g == 0), stop=last_tile,
                                  skip_group_check=True)
                last.then_inc(z_done, 1)

            keys(0, 1)
            for tp in range(2):
                values(0, tp, 1)
            key_norms(0)
            pe.wait_ge(nl_ready, 1)
            with pe.Fori(0, BATCH) as b:
                for cc in range(CPB):
                    c = b * CPB + cc
                    me, nxt = (cc + 1) % 2, cc % 2
                    if cc == 0:
                        pe.wait_ge(bd_ready, BATCH + 1 + b)
                    dists(c, 0, me)
                    keys(c + 1, nxt)
                    dists(c, 1, me)
                    if cc == 0:
                        pe.wait_ge(zt_saved, b + 1)
                    pe.wait_ge(v_done, 2 * (c + 1))
                    sums(c, 0, cc % 2, cc == 0, False)
                    values(c + 1, 0, nxt)
                    dists(c, 2, me)
                    sums(c, 1, cc % 2, False, False)
                    values(c + 1, 1, nxt)
                    dists(c, 3, me)
                    sums(c, 2, cc % 2, False, False)
                    key_norms(c + 1)
                    sums(c, 3, cc % 2, False, cc == CPB - 1)

            def queries(c, at):
                pe.wait_ge(xqh_ready, c + 1)
                pe.wait_ge(xql_ready, c + 1)
                for s in range(KC):
                    pe.wait_ge(qexp_done, PAIRS * c + s + 7)
                    project_T(WQ, at, s, bank[6 + s][:]).then_inc(qproj_done, 1)

            def query_norms(c):
                pe.wait_ge(qs_ready, 2 * (c + 1))
                pe.wait_ge(attn_ready, 2 * c)
                square_norms(bank[4]).then_inc(qnorm_done, 1)

            def query_dists(c, half):
                if half == 0:
                    pe.wait_ge(qaug_done, c + 1)
                for i in range(4 * half, 4 * half + 4):
                    s, h0 = i // 4, 2 * (i % 4)
                    dst = bank[6 + i % 2][:]
                    if i < 2:
                        pe.wait_ge(ql_done, 2 * (c + 1))
                    else:
                        pe.wait_ge(qexp_done, PAIRS * c + i + 7)
                    pair = lambda a: a[:, s, h0:h0 + 2].rearrange("p u k -> p (u k)")
                    product3(dst, pair(bdh[0]), pair(bdl[0]), kh[0][:, s], kl[0][:, s], True, False)
                    mm(dst, sel_q[:, i], augk[0][0:32, :], start=False, stop=True).then_inc(qdist_done, 1)

            def z_transposes(b):
                pe.wait_ge(zt_cur_ready, b + 1)
                pe.sem_inc(pe_waited, 1)
                for g in range(4):
                    last = nc.tensor.transpose(bank[5][0:64, g * P:(g + 1) * P], zt_cur[:, g * NL:(g + 1) * NL], ident)
                last.then_inc(ztr_done, 1)

            def landmark_solve(b):
                pe.wait_ge(zk_ready, b + 1)
                pe.wait_ge(winv_loaded, 16 * (b + 1))
                pe.sem_inc(pe_waited, 1)
                for head in range(H):
                    u, i = head % 2, head // 2
                    last = mm(bank[4][64 * u:64 * u + 64, 32 * i:32 * i + 32], winv_sb[:, head, :],
                              zk[:, 32 * head:32 * head + 32], start=True, stop=True)
                last.then_inc(y_done, 1)

            def attention(c, half):
                pe.wait_ge(qphi_ready, PAIRS * c + 4 * half + 4)
                pe.wait_ge(attn_ready, 2 * c + half)
                for n, dst in ((0, bank[4]), (32, bank[5])):
                    for j in range(4):
                        last = mm(dst[32 * j:32 * j + 32, :], y_cur[:, 4 * half + j, n:n + 32], phi[:, 4 * half + j],
                                  start=True, stop=True)
                last.then_inc(out_done, 1)

            def output_projection(p):
                pe.wait_ge(attnl_ready, 2 * (p + 1))
                for tp in range(2):
                    pe.wait_ge(acc_done, TPC * p + 2 * tp + 2)
                    for t in (2 * tp, 2 * tp + 1):
                        tok = slice(t * P, (t + 1) * P)
                        dst = bank[tp][:, 256 * (t % 2):256 * (t % 2) + 256]
                        for k in range(KC):
                            last = product3(dst, attn_h[:, k, tok], attn_l[:, k, tok], wh[:, WO, k], wl[:, WO, k],
                                            k == 0, k == KC - 1)
                    last.then_inc(wo_done, 1)

            def x1_transposes(p):
                for tp in range(2):
                    pe.wait_ge(x1_ready, TPC * (p + 1) + 2 * tp + 2)
                    for t in (2 * tp, 2 * tp + 1):
                        for k in range(KC):
                            at = 256 * (t % 2) + 128 * k
                            last = nc.tensor.transpose(bank[tp][:, at:at + P], x1[:, t, k * P:(k + 1) * P], ident)
                    last.then_inc(x1t_done, 1)

            def gate_logits(p):
                pe.wait_ge(x1l_ready, 2 * (p + 1))
                for t in range(TPC):
                    tok = slice(t * P, (t + 1) * P)
                    for k in range(KC):
                        for a in (x1h, x1l):
                            last = mm(bank[0][:, 16 * t:16 * t + 16], a[:, k, tok], wg_s[:, k],
                                      start=(k == 0 and a is x1h), stop=(k == KC - 1 and a is x1l))
                last.then_inc(gate_done, 1)

            def gate_transposes(p):
                pe.wait_ge(gst_ready, p + 1)
                for t in range(TPC):
                    last = nc.tensor.transpose(bank[1][0:24, t * P:(t + 1) * P], g_st[:, t], ident)
                last.then_inc(gtr_done, 1)

            def bias_term(p):
                pe.wait_ge(gt_ready, p + 1)
                pe.wait_ge(gate_read, p + 1)
                for tp in range(2):
                    for t in (2 * tp, 2 * tp + 1):
                        last = mm(bank[tp][:, 256 * (t % 2):256 * (t % 2) + 256], g_t[:, t * P:(t + 1) * P], be_s[:],
                                  start=True, stop=True)
                    last.then_inc(be_done, 1)

            def experts(p, t):
                tok = slice(t * P, (t + 1) * P)
                for q in range(E // 2):
                    pe.wait_ge(comb_done, 16 * p + 4 * t + q + 1)
                    cols = slice(512 * q, 512 * (q + 1))
                    for k in range(KC):
                        last = product3(bank[2 + q % 2][:], x1h[:, k, tok], x1l[:, k, tok], weh[:, k, cols],
                                        wel[:, k, cols], k == 0, k == KC - 1)
                    last.then_inc(ffn_done, 1)

            pe.wait_ge(exp_done, W_EXPS + 8 * NCH)
            pe.wait_ge(kl_done, 2 * (NCH + 2))
            pe.wait_ge(v_done, 2 * (NCH + 1))
            pe.wait_ge(aug_done, NCH + 2)
            pe.wait_ge(zt_saved, BATCH + 1)
            pe.wait_ge(w_split_l, 1 + 2 * KC)
            z_transposes(0)
            queries(0, 0)
            query_norms(0)
            pe.wait_ge(qbd_ready, 1)
            query_dists(0, 0)
            pe.wait_ge(qaug_done, 1)
            landmark_solve(0)
            pe.wait_ge(y_ready, 1)
            attention(0, 0)
            query_dists(0, 1)
            attention(0, 1)
            with pe.Fori(0, BATCH) as b:
                for cc in range(CPB):
                    p = b * CPB + cc
                    c = p + 1
                    output_projection(p)
                    queries(c, (cc + 1) % 2)
                    if cc == CPB - 1:
                        pe.wait_ge(attn_ready, 2 * c)
                        z_transposes(b + 1)
                    query_norms(c)
                    x1_transposes(p)
                    if cc == CPB - 1:
                        pe.wait_ge(qbd_ready, b + 2)
                    query_dists(c, 0)
                    gate_logits(p)
                    if cc == CPB - 1:
                        landmark_solve(b + 1)
                    experts(p, 0)
                    gate_transposes(p)
                    if cc == CPB - 1:
                        pe.wait_ge(y_ready, b + 2)
                    attention(c, 0)
                    bias_term(p)
                    experts(p, 1)
                    query_dists(c, 1)
                    experts(p, 2)
                    attention(c, 1)
                    experts(p, 3)


def shape_constants():
    import numpy as np
    c = np.zeros((P, C_END), np.float32)
    part = np.arange(P)
    c[:, C_ID:C_ID + P] = np.eye(P)
    c[:, C_HEAD:C_HEAD + HPS] = part[:, None] // HD == np.arange(HPS)
    for s in range(KC):
        c[:, C_NEG + 32 * s:C_NEG + 32 * (s + 1)] = -(np.arange(32) % H == (HPS * s + part // HD)[:, None]).astype(np.float32)
    c[:, C_LO] = -(part % 32 >= 16).astype(np.float32)
    c[:, C_M16:C_M16 + H] = part[:, None] % 16 == np.arange(H)
    for u in range(2):
        c[:, C_NSEL + 4 * u:C_NSEL + 4 * (u + 1)] = -(part[:, None] // HD == 2 * np.arange(4) + u).astype(np.float32)
    c[:, C_IOTA:C_IOTA + E] = np.arange(E)
    c[0:NL, C_REG:C_REG + NL] = REG * np.eye(NL)
    c[:, C_EXP:C_EXP + TPC] = -0.5
    c[16:24, C_BES] = -1.0
    c[:, C_EPS:C_EPS + TPC] = EPS
    c[:, C_MINUS:C_MINUS + TPC] = -1.0
    return c


def kernel(**inputs):
    import numpy as np
    import concourse.bacc as bacc
    from concourse.bass_utils import run_bass_kernel_spmd

    a = {k: np.asarray(v) for k, v in inputs.items()}
    rows = a["L0_attn_query"].reshape(T, D)
    x = np.concatenate([rows, rows[:CH]])
    x_t = np.ascontiguousarray(np.concatenate([rows, rows[:AHEAD * CH]]).T)

    def columns(v):
        return np.ascontiguousarray(v.reshape(KC, P).T)

    def every_partition(v):
        return np.ascontiguousarray(np.broadcast_to(v.reshape(1, -1), (P, v.size)))

    first_row = (2 * np.arange(4)[None, :] + np.arange(P)[:, None] // NL) * SEQ
    arrays = {
        "xT": x_t, "x": x,
        "wq": a["L0_attn_Wq"].T, "wk": a["L0_attn_Wk"].T, "wv": a["L0_attn_Wv"].T, "wo": a["L0_attn_Wo"].T,
        "we": a["L0_ffn_We"].transpose(2, 0, 1).reshape(D, E * D), "wg": a["L0_ffn_Wg"].T,
        "bq": columns(a["L0_attn_bq"]), "bk": columns(a["L0_attn_bk"]),
        "bv": every_partition(a["L0_attn_bv"]), "bo": every_partition(a["L0_attn_bo"]),
        "be3": np.tile(a["L0_ffn_be"], (3, 1)), "bg": every_partition(a["L0_ffn_bg"]),
        "temp": every_partition(a["L0_attn_temperature"]),
        "idx": np.tile(a["L0_attn_landmark_idx"], 2).reshape(P, 1),
        "gbase": first_row.astype(np.int32), "consts": shape_constants(),
    }
    nc = bacc.Bacc("TRN2", target_bir_lowering=False, num_devices=1)
    arrays = {f"in_{k}": np.ascontiguousarray(v) for k, v in arrays.items()}
    args = [nc.dram_tensor(k, v.shape, mybir.dt.from_np(v.dtype), kind="ExternalInput").ap() for k, v in arrays.items()]
    out = nc.dram_tensor("out", (T, D), mybir.dt.float32, kind="ExternalOutput").ap()
    program(nc, *args, out)
    r = run_bass_kernel_spmd(nc, [arrays], core_ids=[0])
    return r.results[0]["out"].reshape(BATCH, SEQ, D)
```

```python
import concourse.bass as bass
from concourse import mybir
from contextlib import ExitStack

BATCH, SEQ, D, H, HD, NL, E = 8, 2048, 256, 16, 16, 64, 8
P = 128
T = BATCH * SEQ
CH = 512
CPB = SEQ // CH
NCH = T // CH
KC = D // P
HPS = H // KC
PAIRS = H // 2
TPC = CH // P
AHEAD = 3
REG = 1e-6
EPS = 1e-5
NORM_MIN = 1e-10
BIG = 3.0e38
BANK_ORDER = (*range(14), 15, 14)
SW = 16
SWB = NL // SW

C_ID, C_HEAD, C_NEG, C_LO, C_M16, C_NSEL, C_IOTA, C_EXP, C_BES, C_EPS, C_MINUS, C_END = (
    0, 128, 136, 200, 201, 217, 225, 233, 237, 238, 242, 246)


def program(nc, xT, x, wq, wk, wv, wo, we, wg, bq, bk, bv, bo, be3, bg, temp, idx, gbase, consts, out):
    f32, f32r = mybir.dt.float32, mybir.dt.float32r
    i32, u32 = mybir.dt.int32, mybir.dt.uint32
    ALU, ACT = mybir.AluOpType, mybir.ActivationFunctionType

    w_dram = nc.dram_tensor("w_dram", [BATCH * H, NL, NL], f32).ap()
    winv_dram = nc.dram_tensor("winv_dram", [(BATCH + 1) * H, NL, NL], f32).ap()
    xT_v = xT.rearrange("(k p) t -> p k t", p=P)
    x_v = x.rearrange("(c t p) d -> c p t d", t=TPC, p=P)
    out_v = out.rearrange("(c t p) d -> c p t d", t=TPC, p=P)

    ctx = ExitStack()
    with ctx:
        def sb(name, shape, dt=f32):
            return ctx.enter_context(nc.sbuf_tensor(name, shape, dt))

        def sem(name):
            return ctx.enter_context(nc.semaphore(name))

        bank = [ctx.enter_context(nc.psum_tensor(f"bank{i}", [P, 512], f32)) for i in range(8)]

        cst = sb("cst", [P, C_END])
        ident = cst[:, C_ID:C_ID + P]
        neg_block = cst[:, C_NEG:C_NEG + 64].rearrange("p (s r) -> p s r", s=KC)
        lo_sign = cst[:, C_LO:C_LO + 1]
        neg_sel = cst[:, C_NSEL:C_NSEL + 8].rearrange("p (u i) -> p u i", u=2)
        bq_sb, bk_sb = sb("bq_sb", [P, KC]), sb("bk_sb", [P, KC])
        bv_sb, bo_sb = sb("bv_sb", [P, D]), sb("bo_sb", [P, D])
        bg_sb, temp_sb, invt = sb("bg_sb", [P, E]), sb("temp_sb", [P, 1]), sb("invt", [P, 1])
        phi_max, phi_min, tpos = sb("phi_max", [P, 1]), sb("phi_min", [P, 1]), sb("tpos", [P, 1])
        idx_sb, gbase_sb, rows_sb = sb("idx_sb", [P, 1], i32), sb("gbase_sb", [P, 4], i32), sb("rows_sb", [P, 4], i32)
        wh, wl = sb("wh", [P, 4, KC, D], f32r), sb("wl", [P, 4, KC, D], f32r)
        with nc.sbuf_tensor("inversion", [P, 2, NL * NL], f32) as inversion:
            g_all, t_all = inversion[:, 0], inversion[:, 1]
        g3 = g_all.rearrange("p (r c) -> p r c", r=NL)
        t3 = t_all.rearrange("p (r c) -> p r c", r=NL)
        w_raw = t_all[:, 0:2048].rearrange("p (w k n) -> p w k n", w=4, k=KC)
        wk_sb = [t_all[0:64, 2048 + 1024 * i:3072 + 1024 * i].rearrange("p (s h k) -> p s h k", s=KC, h=HPS)
                 for i in range(2)]
        weh, wel = sb("weh", [P, KC, E * D], f32r), sb("wel", [P, KC, E * D], f32r)
        wg_raw, wg_s = sb("wg_raw", [P, KC, E]), sb("wg_s", [P, KC, 2 * E], f32r)
        be_s = sb("be_s", [24, D], f32r)
        sel_q = sb("sel_q", [32, PAIRS, P], f32r)

        NB1 = BATCH + 1
        l2h, l2l = sb("l2h", [P, KC, NB1 * NL]), sb("l2l", [P, KC, NB1 * NL])
        nlt, nlt_cur = sb("nlt", [P, NB1, PAIRS]), sb("nlt_cur", [P, PAIRS])
        bdh, bdl = [sb("bdh0", [P, KC, HPS, NL], f32r)], [sb("bdl0", [P, KC, HPS, NL], f32r)]

        x_raw = [sb(f"x_raw{i}", [P, KC, CH]) for i in range(2)]
        xh = [sb(f"xh{i}", [P, KC, CH], f32r) for i in range(2)]
        xl = [sb(f"xl{i}", [P, KC, CH], f32r) for i in range(2)]
        kh, kl = [sb("kh0", [P, KC, CH], f32r)], [sb("kl0", [P, KC, CH], f32r)]
        sq = sb("sq", [P, KC, CH])
        augk = [sb("augk0", [64, CH], f32r)]
        aug_hi = sb("aug_hi", [32, CH], f32r)
        phi = sb("phi", [P, 8, CH])
        zt = sb("zt", [P, NB1, 4 * NL])
        attn_h, attn_l = sb("attn_h", [P, KC, CH], f32r), sb("attn_l", [P, KC, CH], f32r)
        lm_x = phi[:, 0:2, :].rearrange("p a (b d) -> p (a b) d", b=2)
        sw_v, sw_r, sw_p = sb("sw_v", [P, NL]), sb("sw_r", [P, NL]), sb("sw_p", [P, 1])
        zero_c, minus1 = sb("zero_c", [P, NL]), sb("minus1", [P, 1])
        st1, mv1, ve1, rs1, nm1 = (sb("st1", [P, TPC, 6]), sb("mv1", [P, TPC, 2]), sb("ve1", [P, TPC]),
                                   sb("rs1", [P, TPC]), sb("nm1", [P, TPC]))
        st2, mv2, ve2, rs2, nm2 = (sb("st2", [P, TPC, 6]), sb("mv2", [P, TPC, 2]), sb("ve2", [P, TPC]),
                                   sb("rs2", [P, TPC]), sb("nm2", [P, TPC]))
        nt1, nt2 = sb("nt1", [P, TPC]), sb("nt2", [P, TPC])
        lg0, lg, m8, i8 = (sb("lg0", [P, TPC, E]), sb("lg", [P, TPC, E]), sb("m8", [P, TPC, 8]),
                           sb("i8", [P, TPC, 8], u32))
        if2, gd, ge, gs, gw1, gw2 = (sb("if2", [P, TPC, 2]), sb("gd", [P, TPC]), sb("ge", [P, TPC]),
                                     sb("gs", [P, TPC]), sb("gw1", [P, TPC]), sb("gw2", [P, TPC]))
        oh1, oh2, gate, gate_h = (sb("oh1", [P, TPC, E]), sb("oh2", [P, TPC, E]),
                                  [sb(f"gate{i}", [P, TPC, E]) for i in range(2)],
                                  sb("gate_h", [P, TPC, E], f32r))
        g_st, g_t = sb("g_st", [P, TPC, 24]), sb("g_t", [24, CH], f32r)

        with ExitStack() as stage1:
            def sb1(name, shape, dt=f32):
                return stage1.enter_context(nc.sbuf_tensor(name, shape, dt))

            v_aug = [sb1(f"v_aug{i}", [P, TPC, H, 32]) for i in range(2)]
            be_raw, be_tmp = sb1("be_raw", [24, D]), sb1("be_tmp", [24, D], f32r)
            bdh.append(sb1("bdh1", [P, KC, HPS, NL], f32r))
            bdl.append(sb1("bdl1", [P, KC, HPS, NL], f32r))
            augm = [sb1(f"augm{i}", [64, KC, HPS, NL], f32r) for i in range(2)]
            ln_rows = sb1("ln_rows", [64, NB1 * NL])
            kh.append(sb1("kh1", [P, KC, CH], f32r))
            kl.append(sb1("kl1", [P, KC, CH], f32r))
            augk.append(sb1("augk1", [64, CH], f32r))
        x_tok, y_out = sb("x_tok", [P, TPC, D]), sb("y_out", [P, TPC, D])
        x1 = [sb(f"x1_{i}", [P, TPC, D]) for i in range(2)]
        x1h, x1l = [sb("x1h0", [P, KC, CH], f32r)], [sb("x1l0", [P, KC, CH], f32r)]
        x1h.append(sb("x1h1", [P, KC, CH], f32r))
        x1l.append(sb("x1l1", [P, KC, CH], f32r))
        acc, part = sb("acc", [P, 2, D]), sb("part", [P, 2, 2 * D])
        nrm = sb("nrm", [P, CH])
        attn = sb("attn", [P, KC, CH])
        zt_cur, zk = sb("zt_cur", [P, 4 * NL]), sb("zk", [64, H * 32])
        winv_sb, y_cur = sb("winv_sb", [64, H, NL]), sb("y_cur", [P, PAIRS, 64])
        we_raw = [a[:].rearrange("p t d -> p (t d)") for a in (*x1, y_out, part)]

        idx_loaded, small_loaded, w_loaded, we_loaded = (sem("idx_loaded"), sem("small_loaded"), sem("w_loaded"),
                                                         sem("we_loaded"))
        rows_ready, gathered, const_set, setup_done = sem("rows_ready"), sem("gathered"), sem("const_set"), sem("setup_done")
        w_split_h, w_split_l = sem("w_split_h"), sem("w_split_l")
        lmT_done, l2_ready, nl_done, nl_ready = sem("lmT_done"), sem("l2_ready"), sem("nl_done"), sem("nl_ready")
        bd_ready, bdl_ready, w_stored, g_loaded = (
            sem("bd_ready"), sem("bdl_ready"), [sem(f"w_stored{i}") for i in range(2)], sem("g_loaded"))
        dve_step, pool_step = sem("dve_step"), sem("pool_step")
        dve_waited, pe_waited = sem("dve_waited"), sem("pe_waited")
        x_loaded, xh_ready, xl_ready = [sem(f"x_loaded{i}") for i in range(2)], sem("xh_ready"), sem("xl_ready")
        kproj_done, s_ready, kl_done, norm_done, aug_done = (
            sem("kproj_done"), sem("s_ready"), sem("kl_done"), sem("norm_done"), sem("aug_done"))
        vproj_done, v_done = sem("vproj_done"), sem("v_done")
        dist_done, exp_done, phi_ready, z_done, zt_saved = (
            sem("dist_done"), sem("exp_done"), sem("phi_ready"), sem("z_done"), sem("zt_saved"))
        sw_ready, sw_prod, sw_pool_done, inv_done = (
            sem("sw_ready"), sem("sw_prod"), sem("sw_pool_done"), sem("inv_done"))
        winv_stored, winv_loaded, zt_cur_ready, ztr_done, zk_ready, y_done, y_ready = (
            sem("winv_stored"), sem("winv_loaded"), sem("zt_cur_ready"), sem("ztr_done"), sem("zk_ready"),
            sem("y_done"), sem("y_ready"))
        xq_loaded, xqh_ready, xql_ready, xt_loaded, xb_ready = (
            [sem(f"xq_loaded{i}") for i in range(2)], sem("xqh_ready"), sem("xql_ready"),
            sem("xt_loaded"), sem("xb_ready"))
        qproj_done, qs_ready, ql_done, qnorm_done, qaug_done = (
            sem("qproj_done"), sem("qs_ready"), sem("ql_done"), sem("qnorm_done"), sem("qaug_done"))
        nlt_ready, qbdh_ready, qbdl_ready, qdist_done, qexp_done, qphi_ready = (
            sem("nlt_ready"), sem("qbdh_ready"), sem("qbdl_ready"), sem("qdist_done"), sem("qexp_done"), sem("qphi_ready"))
        out_done, attn_ready, attnh_ready, attnl_ready = (
            sem("out_done"), sem("attn_ready"), sem("attnh_ready"), sem("attnl_ready"))
        wo_done, h_done, ln1_stats, ln1_coef, x1_ready, x1t_done, x1h_ready, x1l_ready = (
            sem("wo_done"), sem("h_done"), sem("ln1_stats"), sem("ln1_coef"), sem("x1_ready"),
            sem("x1t_done"), sem("x1h_ready"), sem("x1l_ready"))
        gate_done, gate_read, gd_ready, ge_ready, gst_ready, gtr_done, gt_ready, be_done, be_added = (
            sem("gate_done"), sem("gate_read"), sem("gd_ready"), sem("ge_ready"), sem("gst_ready"),
            sem("gtr_done"), sem("gt_ready"), sem("be_done"), sem("be_added"))
        ffn_done, comb_done, part_ready, part_sum, acc_done, ln2_stats, ln2_coef, res_ready, res_stored = (
            sem("ffn_done"), sem("comb_done"), sem("part_ready"), sem("part_sum"), sem("acc_done"), sem("ln2_stats"), sem("ln2_coef"),
            sem("res_ready"), sem("res_stored"))

        block = ctx.enter_context(nc.Block())

        W_ORDER = range(BATCH - 1, -1, -1)
        W_EXPS = 2 * BATCH

        def raw(ap):
            return ap.bitcast(f32)

        def rep(ap, axis, n):
            a = ap.unsqueeze(axis)
            shape = list(a.shape)
            shape[axis] = n
            return a.broadcast_to(shape)

        def in_batch(b, n=NL):
            return bass.ds(b * n, n)

        class Steps:

            def __init__(self, eng, semaphore):
                self.eng, self.sem, self.base, self.n = eng, semaphore, 0, 0

            def did(self, instruction):
                self.n += 1
                instruction.then_inc(self.sem, 1)

            def wait(self):
                self.eng.wait_ge(self.sem, self.base + self.n)

            def then(self, instruction):
                self.did(instruction)
                self.wait()

            def enter(self, i, per_turn):
                self.start = self.base + self.n
                self.per_turn, self.n = per_turn, 0
                self.base = self.start + i * per_turn

            def leave(self, turns):
                assert self.n == self.per_turn, (self.n, self.per_turn)
                self.base, self.n = self.start + turns * self.per_turn, 0

        def q_starts_batch(cc):
            return cc == CPB - 2

        def q_ends_batch(cc):
            return cc == CPB - 3

        def block_row(m, n):
            return m[:, n * SW:(n + 1) * SW, 0:(n + 1) * SW]

        def outer(n):
            return rep(sw_v[:, n * SW:(n + 1) * SW], 2, (n + 1) * SW), rep(sw_r[:, 0:(n + 1) * SW], 1, SW)

        def product3(outp, ah, al, bh, bl, first, last):
            nc.tensor.matmul(outp, ah, bh, start=first, stop=False)
            nc.tensor.matmul(outp, al, bh, start=False, stop=False)
            return nc.tensor.matmul(outp, ah, bl, start=False, stop=last)

        @block.sync
        def _(sp):
            sp.sem_inc(z_done, TPC)
            sp.sem_inc(qexp_done, PAIRS)
            sp.sem_inc(acc_done, 1)
            sp.sem_inc(sw_pool_done, 1)
            sp.sem_inc(comb_done, 1)
            sp.sem_inc(part_ready, 1)
            sp.sem_inc(h_done, TPC)
            sp.sem_inc(x1_ready, TPC)
            sp.sem_inc(res_ready, TPC)
            sp.sem_inc(zt_saved, 1)
            sp.sem_inc(res_stored, 16)
            sp.sem_inc(xqh_ready, 2)
            sp.sem_inc(xql_ready, 2)
            for dst, src in ((idx_sb, idx), (gbase_sb, gbase)):
                sp.dma_start(dst[:], src).then_inc(idx_loaded, 16)
            for dst, src in ((cst, consts), (bq_sb, bq), (bk_sb, bk), (bv_sb, bv), (bo_sb, bo), (bg_sb, bg),
                             (temp_sb, temp), (be_raw, be3)):
                sp.dma_start(dst[:], src).then_inc(small_loaded, 16)
            sp.dma_start(wg_raw[:], wg.rearrange("(k p) e -> p k e", p=P)).then_inc(small_loaded, 16)
            for i, w in enumerate((wk, wv, wq, wo)):
                sp.dma_start(w_raw[:, i], w.rearrange("(k p) n -> p k n", p=P)).then_inc(w_loaded, 16)
            for c in range(2):
                sp.dma_start(x_raw[(c + 1) % 2][:], xT_v[:, :, c * CH:(c + 1) * CH]).then_inc(x_loaded[c], 16)
            for i, b in enumerate(W_ORDER):
                sp.wait_ge(exp_done, 2 * i + 2)
                sp.dma_start(w_dram[b * H:(b + 1) * H].rearrange("s k j -> k s j"),
                             wk_sb[i % 2].rearrange("p s h k -> p (s h) k")).then_inc(w_stored[i % 2], 16)
            for i in range(2):
                sp.wait_ge(w_stored[i], 16 * BATCH // 2)
            sp.dma_start(g_all, w_dram.rearrange("s k j -> s (k j)")).then_inc(g_loaded, 16)
            with sp.Fori(0, BATCH) as b:
                for cc in range(CPB):
                    c = b * CPB + cc
                    sp.wait_ge(xl_ready, c + 2)
                    sp.dma_start(x_raw[(cc + 1) % 2][:],
                                 xT_v[:, :, bass.ds((c + 2) * CH, CH)]).then_inc(x_loaded[cc % 2], 16)
            sp.wait_ge(xl_ready, NCH + 3)
            sp.dma_start(x_raw[1][:], xT_v[:, :, 2 * CH:3 * CH]).then_inc(xq_loaded[1], 16)
            sp.wait_ge(inv_done, 1)
            flat = winv_dram.rearrange("s k j -> s (k j)")
            sp.dma_start(flat[0:P], g_all).then_inc(winv_stored, 16)
            sp.dma_start(flat[P:P + H], g_all[0:H]).then_inc(winv_stored, 16)
            for sem_done, count in ((z_done, TPC * (NCH + 1)), (v_done, 2 * (NCH + 1)), (kl_done, 2 * (NCH + 2)),
                                    (aug_done, NCH + 2)):
                sp.wait_ge(sem_done, count)
            sp.dma_start(x_tok[:], x_v[0]).then_inc(xt_loaded, 16)
            sp.wait_ge(winv_stored, 32)
            winv_b = winv_dram.rearrange("s k j -> k s j")
            sp.dma_start(winv_sb[:], winv_b[:, 0:H, :]).then_inc(winv_loaded, 16)
            for i in range(2 * KC):
                k, half = i // 2, i % 2
                sp.dma_start(we_raw[i], we[k * P:(k + 1) * P, 1024 * half:1024 * (half + 1)]).then_inc(we_loaded, 16)
            sp.wait_ge(h_done, 2 * TPC)
            sp.dma_start(x_tok[:], x_v[1]).then_inc(xt_loaded, 16)
            with sp.Fori(0, BATCH) as b:
                for cc in range(CPB):
                    p = b * CPB + cc
                    sp.wait_ge(xql_ready, p + 2)
                    sp.dma_start(x_raw[cc % 2][:],
                                 xT_v[:, :, bass.ds((p + 3) * CH, CH)]).then_inc(xq_loaded[cc % 2], 16)
                    if cc == 0:
                        sp.wait_ge(y_done, b + 1)
                        sp.dma_start(winv_sb[:], winv_b[:, in_batch(b + 1, H), :]).then_inc(winv_loaded, 16)
                    sp.wait_ge(h_done, TPC * (p + 3))
                    sp.dma_start(x_tok[:], x_v[bass.ds(p + 2, 1)].rearrange("a p t d -> (a p) t d")).then_inc(xt_loaded, 16)
                    sp.wait_ge(res_ready, TPC * (p + 2))
                    sp.dma_start(out_v[bass.ds(p, 1)].rearrange("a p t d -> (a p) t d"), y_out[:]).then_inc(res_stored, 16)
            sp.wait_ge(res_stored, 16 * (NCH + 1))

        @block.gpsimd
        def _(pool):
            own = Steps(pool, pool_step)
            pool.wait_ge(idx_loaded, 32)
            nc.gpsimd.tensor_tensor(rows_sb[:], gbase_sb[:], idx_sb[:].broadcast_to([P, 4]), ALU.add).then_inc(rows_ready, 1)
            pool.wait_ge(rows_ready, 1)
            for i in range(4):
                nc.gpsimd.indirect_dma_start(
                    out=lm_x[:, i, :], out_offset=None, in_=x,
                    in_offset=bass.IndirectOffsetOnAxis(ap=rows_sb[:, i:i + 1].bitcast(u32), axis=0)).then_inc(gathered, 16)
            nc.gpsimd.memset(v_aug[0][:], 0.0)
            own.then(nc.gpsimd.memset(v_aug[1][:], 0.0))
            for i in range(2):
                last = nc.gpsimd.memset(v_aug[i][:, :, :, HD:HD + 1], 1.0)
            last.then_inc(const_set, 1)

            def block_lo(b, at):
                for s in range(KC):
                    last = nc.gpsimd.tensor_tensor(
                        bdl[at][:, s], rep(l2l[:, s, in_batch(b)], 1, HPS),
                        rep(cst[:, C_HEAD:C_HEAD + HPS], 2, NL), ALU.mult)
                return last

            pool.wait_ge(l2_ready, 1)
            pool.wait_ge(small_loaded, 16 * 9)
            for i, b in enumerate(W_ORDER):
                if i >= 2:
                    pool.wait_ge(dist_done, 2 * (i - 1))
                block_lo(b, b % 2).then_inc(bdl_ready, 1)
            def sweep(s):
                pool.wait_ge(sw_ready, s + 1)
                nc.gpsimd.tensor_tensor(block_row(t3, SWB - 1), *outer(SWB - 1), ALU.mult).then_inc(sw_prod, 1)
                nc.gpsimd.tensor_tensor(block_row(t3, SWB - 2), *outer(SWB - 2), ALU.mult).then_inc(sw_prod, 1)
                pool.wait_ge(sw_prod, 2 * s + 2)
                nc.gpsimd.tensor_tensor(block_row(g3, SWB - 2), block_row(g3, SWB - 2), block_row(t3, SWB - 2),
                                        ALU.subtract).then_inc(sw_pool_done, 1)

            with pool.Fori(0, BATCH) as b:
                for cc in range(CPB):
                    c = b * CPB + cc
                    sweep(2 * c)
                    at = (cc + 1) % 2
                    pool.wait_ge(xh_ready, c + 4)
                    nc.gpsimd.tensor_tensor(xl[at][:], x_raw[at][:], raw(xh[at][:]), ALU.subtract).then_inc(xl_ready, 1)
                    sweep(2 * c + 1)

            def layernorm_coefs(mv, ve, rs, nt, nm, cols):
                own.then(nc.gpsimd.tensor_tensor(ve[:, cols], mv[:, cols, 1], cst[:, C_EPS:C_EPS + TPC][:, cols], ALU.add))
                own.then(nc.gpsimd.tensor_tensor(rs[:, cols], ve[:, cols], cst[:, C_EXP:C_EXP + TPC][:, cols], ALU.pow))
                own.then(nc.gpsimd.tensor_tensor(nt[:, cols], mv[:, cols, 0], rs[:, cols], ALU.mult))
                return nc.gpsimd.tensor_tensor(nm[:, cols], nt[:, cols], cst[:, C_MINUS:C_MINUS + TPC][:, cols], ALU.mult)

            def block_lo_q(b):
                for s in range(KC):
                    nc.gpsimd.tensor_tensor(bdl[0][:, s], rep(l2l[:, s, in_batch(b)], 1, HPS),
                                            rep(cst[:, C_HEAD:C_HEAD + HPS], 2, NL), ALU.mult).then_inc(qbdl_ready, 1)

            def split_lo(c, at):
                pool.wait_ge(xqh_ready, c + 1)
                nc.gpsimd.tensor_tensor(xl[at][:], x_raw[at][:], raw(xh[at][:]), ALU.subtract).then_inc(xql_ready, 1)

            def attn_lo(c, s):
                pool.wait_ge(attnh_ready, 2 * c + s + 1)
                nc.gpsimd.tensor_tensor(attn_l[:, s], attn[:, s], raw(attn_h[:, s]), ALU.subtract).then_inc(attnl_ready, 1)

            def residual(c):
                pool.wait_ge(xt_loaded, 16 * (c + 1))
                nc.gpsimd.tensor_tensor(x_tok[:], x_tok[:], rep(bo_sb[:], 1, TPC), ALU.add).then_inc(xb_ready, 1)

            def ln1(c):
                pool.wait_ge(ln1_stats, c + 1)
                layernorm_coefs(mv1, ve1, rs1, nt1, nm1, slice(0, TPC)).then_inc(ln1_coef, 1)

            def sum_parts(p, t):
                pool.wait_ge(part_ready, 8 * p + 2 * t + 3)
                own.then(nc.gpsimd.tensor_tensor(part[:, 0], part[:, 0], part[:, 1], ALU.add))
                nc.gpsimd.tensor_tensor(part[:, 0, 0:D], part[:, 0, 0:D], part[:, 0, D:2 * D], ALU.add).then_inc(part_sum, 1)

            def ln2(p, t):
                pool.wait_ge(ln2_stats, TPC * p + t + 1)
                layernorm_coefs(mv2, ve2, rs2, nt2, nm2, slice(t, t + 1)).then_inc(ln2_coef, 1)

            pool.wait_ge(dist_done, W_EXPS + 8 * NCH)
            pool.wait_ge(bd_ready, 2 * BATCH)
            block_lo_q(0)
            residual(0)
            attn_lo(0, 0)
            attn_lo(0, 1)
            ln1(0)
            split_lo(2, 1)
            residual(1)
            attn_lo(1, 0)
            attn_lo(1, 1)
            with pool.Fori(0, BATCH) as b:
                own.enter(b, CPB * (3 + 4 * TPC))
                for cc in range(CPB):
                    p = b * CPB + cc
                    c, q = p + 1, p + 2
                    ln1(c)
                    sum_parts(p, 0)
                    split_lo(q + 1, cc % 2)
                    ln2(p, 0)
                    residual(q)
                    sum_parts(p, 1)
                    attn_lo(q, 0)
                    ln2(p, 1)
                    sum_parts(p, 2)
                    attn_lo(q, 1)
                    if q_ends_batch(cc):
                        pool.wait_ge(qdist_done, PAIRS * (q + 1))
                        block_lo_q(b + 1)
                    ln2(p, 2)
                    sum_parts(p, 3)
                    ln2(p, 3)
                own.leave(BATCH)

        @block.scalar
        def _(act):
            def split_hi(at, ready):
                nc.scalar.activation(xh[at][:], x_raw[at][:], ACT.Copy).then_inc(ready, 1)

            act.wait_ge(small_loaded, 16 * 9)
            act.wait_ge(w_loaded, 64)
            nc.scalar.activation(wh[:], w_raw, ACT.Copy).then_inc(w_split_h, 1)
            for k in range(KC):
                act.wait_ge(lmT_done, k + 1)
                last = nc.scalar.activation(xh[0][:, k], bank[k][:], ACT.Copy)
            last.then_inc(xh_ready, 1)
            for s in range(KC):
                act.wait_ge(kproj_done, s + 1)
                nc.scalar.activation(kh[0][:, s], bank[2 + s][:], ACT.Identity, bias=bk_sb[:, s:s + 1])
                nc.scalar.activation(sq[:, s], bank[2 + s][:], ACT.Square, bias=bk_sb[:, s:s + 1]).then_inc(s_ready, 1)
            act.wait_ge(setup_done, 1)
            act.wait_ge(nl_done, 1)
            nc.scalar.activation(nlt[:, 0:BATCH, :].rearrange("p b i -> p (b i)"), bank[5][:, 0:BATCH * PAIRS], ACT.Copy,
                                 scale=invt[:]).then_inc(nl_ready, 1)
            act.wait_ge(nl_ready, 1)
            nc.scalar.activation(nlt[:, BATCH, :], nlt[:, 0, :], ACT.Copy).then_inc(nl_ready, 1)
            def exps(c, t):
                for s in range(KC):
                    n = 2 * t + s
                    act.wait_ge(dist_done, W_EXPS + 8 * c + n + 1)
                    if s == 0:
                        act.wait_ge(z_done, TPC * c + t + 1)
                    nc.scalar.activation(phi[:, n], bank[6 + s][:], ACT.Exp, scale=invt[:]).then_inc(exp_done, 1)

            def keys(c, at):
                for s in range(KC):
                    act.wait_ge(kproj_done, 2 * (c + 1) + s + 1)
                    if s == 0:
                        act.wait_ge(norm_done, c + 1)
                    nc.scalar.activation(kh[at][:, s], bank[2 + s][:], ACT.Identity, bias=bk_sb[:, s:s + 1])
                    nc.scalar.activation(sq[:, s], bank[2 + s][:], ACT.Square, bias=bk_sb[:, s:s + 1]).then_inc(s_ready, 1)

            act.wait_ge(x_loaded[0], 16)
            split_hi(1, xh_ready)
            act.wait_ge(kproj_done, 2)
            act.wait_ge(x_loaded[1], 16)
            split_hi(0, xh_ready)
            keys(0, 1)
            for i in range(BATCH):
                for s in range(KC):
                    act.wait_ge(dist_done, 2 * i + s + 1)
                    if i >= 2:
                        act.wait_ge(w_stored[i % 2], 16 * (i // 2))
                    nc.scalar.activation(wk_sb[i % 2][:, s].rearrange("p h k -> p (h k)"), bank[6 + s][0:64, :],
                                         ACT.Exp, scale=invt[0:64, :]).then_inc(exp_done, 1)
            act.wait_ge(dist_done, W_EXPS)
            act.wait_ge(l2_ready, 1)
            with act.Fori(0, BATCH) as b:
                for cc in range(CPB):
                    c = b * CPB + cc
                    exps(c, 0)
                    act.wait_ge(dist_done, W_EXPS + 8 * c)
                    keys(c + 1, cc % 2)
                    exps(c, 1)
                    act.wait_ge(x_loaded[cc % 2], 16 * (2 * b + cc // 2 + 2))
                    act.wait_ge(vproj_done, 2 * (c + 1))
                    split_hi((cc + 1) % 2, xh_ready)
                    exps(c, 2)
                    exps(c, 3)
                    if cc == CPB - 1:
                        act.wait_ge(z_done, TPC * (c + 2))
                        nc.scalar.activation(zt[:, bass.ds(b, 1), :].rearrange("p a z -> p (a z)"),
                                             bank[5][:, 0:4 * NL], ACT.Copy).then_inc(zt_saved, 1)
            act.wait_ge(zt_saved, BATCH + 1)
            nc.scalar.activation(zt[:, BATCH, :], zt[:, 0, :], ACT.Copy).then_inc(zt_saved, 1)
            act.wait_ge(zt_saved, BATCH + 2)

            def z_of_batch(b):
                act.wait_ge(ztr_done, b)
                nc.scalar.activation(zt_cur[:], zt[:, bass.ds(b, 1), :].rearrange("p a z -> p (a z)"),
                                     ACT.Copy).then_inc(zt_cur_ready, 1)

            def norms_of_batch(b):
                nc.scalar.activation(nlt_cur[:], nlt[:, bass.ds(b, 1), :].rearrange("p a i -> p (a i)"),
                                     ACT.Copy).then_inc(nlt_ready, 1)
                act.wait_ge(nlt_ready, b + 1)

            def z_landmark_major(b):
                act.wait_ge(ztr_done, b + 1)
                act.wait_ge(y_done, b)
                nc.scalar.activation(zk[:], bank[5][0:64, :], ACT.Copy).then_inc(zk_ready, 1)

            def queries(c, slices=range(KC)):
                for s in slices:
                    act.wait_ge(qproj_done, 2 * c + s + 1)
                    if s == 0:
                        act.wait_ge(qdist_done, PAIRS * c)
                        act.wait_ge(qnorm_done, c)
                    nc.scalar.activation(kh[0][:, s], bank[6 + s][:], ACT.Identity, bias=bq_sb[:, s:s + 1])
                    nc.scalar.activation(sq[:, s], bank[6 + s][:], ACT.Square, bias=bq_sb[:, s:s + 1]).then_inc(qs_ready, 1)

            def q_exps(c, pairs):
                for i in pairs:
                    act.wait_ge(qdist_done, PAIRS * c + i + 1)
                    if i % 4 == 0:
                        act.wait_ge(out_done, 2 * c)
                    nc.scalar.activation(phi[:, i], bank[6 + i % 2][:], ACT.Exp,
                                         bias=nlt_cur[:, i:i + 1], scale=invt[:]).then_inc(qexp_done, 1)

            def attn_hi(c, s):
                act.wait_ge(attn_ready, 2 * c + s + 1)
                act.wait_ge(wo_done, 2 * c)
                nc.scalar.activation(attn_h[:, s], attn[:, s], ACT.Copy).then_inc(attnh_ready, 1)

            def query_hi(c, at, turn):
                act.wait_ge(xq_loaded[at], 16 * turn)
                act.wait_ge(qproj_done, 2 * c - 2)
                split_hi(at, xqh_ready)

            def normalise_rows(c, at):
                act.wait_ge(ln1_coef, c + 1)
                for t in range(TPC):
                    nc.scalar.activation(x1[at][:, t], x1[at][:, t], ACT.Identity, bias=nm1[:, t:t + 1],
                                         scale=rs1[:, t:t + 1]).then_inc(x1_ready, 1)

            def x1_hi(c, at):
                for tp in range(2):
                    act.wait_ge(x1t_done, 2 * c + tp + 1)
                    nc.scalar.activation(x1h[at][:, :, tp * 256:tp * 256 + 256].rearrange("p k (t j) -> p t k j", t=2),
                                         bank[tp][:].rearrange("p (t k j) -> p t k j", t=2, k=KC),
                                         ACT.Copy).then_inc(x1h_ready, 1)

            def gate_exp(c):
                act.wait_ge(gd_ready, c + 1)
                nc.scalar.activation(ge[:], gd[:], ACT.Exp).then_inc(ge_ready, 1)

            def gates_T(c):
                act.wait_ge(gtr_done, c + 1)
                nc.scalar.activation(g_t[:], bank[1][0:24, :], ACT.Copy).then_inc(gt_ready, 1)

            def weigh(p, n, at):
                t, q = n // 4, n % 4
                act.wait_ge(ffn_done, 16 * p + BANK_ORDER.index(n) + 1)
                act.wait_ge(acc_done, TPC * p + t + 1)
                for u in range(2):
                    e = 2 * q + u
                    last = nc.scalar.activation(part[:, q // 2, u * D:(u + 1) * D], bank[3][:, u * D:(u + 1) * D],
                                                ACT.Copy, scale=gate[at][:, t, e:e + 1])
                last.then_inc(part_ready, 1)

            def result(p, t):
                act.wait_ge(ln2_coef, TPC * p + t + 1)
                if t == 0:
                    act.wait_ge(res_stored, 16 * (p + 1))
                nc.scalar.activation(y_out[:, t], acc[:, t % 2], ACT.Identity, bias=nm2[:, t:t + 1],
                                     scale=rs2[:, t:t + 1]).then_inc(res_ready, 1)

            act.wait_ge(vproj_done, 2 * (NCH + 1))
            act.wait_ge(v_done, 2 * (NCH + 1))
            act.wait_ge(norm_done, NCH + 2)
            z_of_batch(0)
            norms_of_batch(0)
            queries(0)
            z_landmark_major(0)
            q_exps(0, range(PAIRS))
            attn_hi(0, 0)
            attn_hi(0, 1)
            queries(1)
            act.wait_ge(winv_stored, 32)
            for i in range(2 * KC):
                act.wait_ge(we_loaded, 32 * KC)
                nc.scalar.activation(weh[:, i // 2, 1024 * (i % 2):1024 * (i % 2 + 1)], we_raw[i],
                                     ACT.Copy).then_inc(w_split_h, 1)
            query_hi(2, 1, 1)
            q_exps(1, range(PAIRS))
            normalise_rows(0, 0)
            x1_hi(0, 0)
            gate_exp(0)
            attn_hi(1, 0)
            attn_hi(1, 1)
            queries(2)
            gates_T(0)
            with act.Fori(0, BATCH) as b:
                for cc in range(CPB):
                    p = b * CPB + cc
                    c, q = p + 1, p + 2
                    me, nxt = cc % 2, (cc + 1) % 2
                    q_exps(q, range(0, 2))
                    weigh(p, 1, me)
                    q_exps(q, range(2, 4))
                    normalise_rows(c, nxt)
                    weigh(p, 3, me)
                    q_exps(q, range(4, 6))
                    x1_hi(c, nxt)
                    query_hi(q + 1, me, 2 * b + (cc + 3) // 2)
                    q_exps(q, range(6, 8))
                    weigh(p, 5, me)
                    result(p, 0)
                    gate_exp(c)
                    weigh(p, 7, me)
                    attn_hi(q, 0)
                    queries(q + 1, (0,))
                    weigh(p, 9, me)
                    queries(q + 1, (1,))
                    result(p, 1)
                    gates_T(c)
                    weigh(p, 11, me)
                    attn_hi(q, 1)
                    if q_ends_batch(cc):
                        z_of_batch(b + 1)
                        act.wait_ge(qexp_done, PAIRS * (q + 2))
                        norms_of_batch(b + 1)
                    weigh(p, 13, me)
                    result(p, 2)
                    if q_ends_batch(cc):
                        z_landmark_major(b + 1)
                    weigh(p, 15, me)
                    result(p, 3)

        @block.vector
        def _(dve):
            own = Steps(dve, dve_step)
            V = nc.vector
            V.memset(zero_c[:], 0.0)
            V.memset(raw(augk[0][:]), 1.0)
            V.memset(raw(augk[1][:]), 1.0)
            own.did(V.memset(minus1[:], -1.0))
            dve.wait_ge(small_loaded, 16 * 9)
            V.reciprocal(invt[:], temp_sb[:])
            own.then(V.tensor_scalar(tpos[:], temp_sb[:], 0.0, None, ALU.is_gt))
            own.then(V.tensor_scalar(phi_min[:], tpos[:], -1.0, 1.0, ALU.mult, ALU.add))
            V.scalar_tensor_tensor(phi_max[:], phi_min[:], BIG, tpos[:], ALU.mult, ALU.add)
            mask = cst[0:32, C_M16:C_M16 + H]
            V.tensor_copy(sel_q[:].rearrange("p i (u k) -> p i u k", u=2),
                          rep(mask.rearrange("p (i u) -> p i u", u=2), 3, NL))
            for i in range(2):
                last = V.tensor_copy(augm[i][0:32], rep(mask.rearrange("p (s h) -> p s h", s=KC), 3, NL))
            V.tensor_copy(be_tmp[:], be_raw[:])
            own.then(V.tensor_copy(wg_s[:, :, 0:E], wg_raw[:]))
            V.tensor_tensor(wg_s[:, :, E:2 * E], wg_raw[:], raw(wg_s[:, :, 0:E]), ALU.subtract)
            V.scalar_tensor_tensor(be_s[:], raw(be_tmp[:]), cst[0:24, C_BES:C_BES + 1], be_raw[:], ALU.mult,
                                   ALU.add).then_inc(setup_done, 1)
            dve.wait_ge(w_split_h, 1)
            V.tensor_tensor(wl[:], w_raw, raw(wh[:]), ALU.subtract).then_inc(w_split_l, 1)
            dve.wait_ge(xh_ready, 1)
            for k in range(KC):
                last = V.tensor_tensor(xl[0][:, k], bank[k][:], raw(xh[0][:, k]), ALU.subtract)
            last.then_inc(xl_ready, 1)

            def project_lo(dst, hi, src, bias, s):
                return V.scalar_tensor_tensor(dst[:, s], src[:], bias[:, s:s + 1], raw(hi[:, s]), ALU.add, ALU.subtract)

            def norm_rows(dst, src):
                own.then(V.tensor_copy(aug_hi[:], src[0:32, :]))
                return V.scalar_tensor_tensor(dst, raw(aug_hi[:]), lo_sign[0:32, :], src[0:32, :], ALU.mult, ALU.add)

            for s in range(KC):
                dve.wait_ge(s_ready, s + 1)
                project_lo(kl[0], kh[0], bank[2 + s], bk_sb, s).then_inc(kl_done, 1)
            dve.wait_ge(kl_done, 2)
            V.tensor_scalar(l2h[:, :, 0:BATCH * NL], raw(kh[0][:]), 2.0, None, ALU.mult)
            V.tensor_scalar(l2l[:, :, 0:BATCH * NL], raw(kl[0][:]), 2.0, None, ALU.mult)
            V.tensor_scalar(l2h[:, :, BATCH * NL:], raw(kh[0][:, :, 0:NL]), 2.0, None, ALU.mult)
            V.tensor_scalar(l2l[:, :, BATCH * NL:], raw(kl[0][:, :, 0:NL]), 2.0, None, ALU.mult).then_inc(l2_ready, 1)
            dve.wait_ge(norm_done, 1)
            norm_rows(augk[0][0:32, :], bank[4]).then_inc(aug_done, 1)
            dve.wait_ge(aug_done, 1)
            V.tensor_copy(ln_rows[32:64, 0:BATCH * NL], raw(augk[0][0:32, :]))
            own.then(V.tensor_copy(ln_rows[32:64, BATCH * NL:], raw(augk[0][0:32, 0:NL])))

            def block_hi(b, at, low):
                for s in range(KC):
                    V.tensor_tensor(bdh[at][:, s], rep(l2h[:, s, in_batch(b)], 1, HPS),
                                    rep(cst[:, C_HEAD:C_HEAD + HPS], 2, NL), ALU.mult)
                    if low:
                        V.tensor_tensor(bdl[at][:, s], rep(l2l[:, s, in_batch(b)], 1, HPS),
                                        rep(cst[:, C_HEAD:C_HEAD + HPS], 2, NL), ALU.mult)
                    last = V.tensor_tensor(augm[at][32:64, s], rep(ln_rows[32:64, in_batch(b)], 1, HPS),
                                           rep(cst[32:64, C_M16 + HPS * s:C_M16 + HPS * (s + 1)], 2, NL), ALU.mult)
                return last

            def clamp(c, t):
                for s in range(KC):
                    n = 2 * t + s
                    dve.wait_ge(exp_done, W_EXPS + 8 * c + n + 1)
                    V.tensor_scalar(phi[:, n], phi[:, n], phi_max[:], phi_min[:], ALU.min, ALU.max).then_inc(phi_ready, 1)

            def keys_lo(c, at):
                for s in range(KC):
                    dve.wait_ge(s_ready, 2 * (c + 1) + s + 1)
                    project_lo(kl[at], kh[at], bank[2 + s], bk_sb, s).then_inc(kl_done, 1)

            def values(c, tp, at):
                dve.wait_ge(vproj_done, 2 * c + tp + 1)
                dve.wait_ge(z_done, TPC * c)
                V.tensor_tensor(v_aug[at][:, 2 * tp:2 * tp + 2, :, 0:HD],
                                bank[tp][:].rearrange("p (t h d) -> p t h d", t=2, h=H),
                                rep(bv_sb[:].rearrange("p (h d) -> p h d", h=H), 1, 2), ALU.add).then_inc(v_done, 1)

            def key_norms(c, at):
                dve.wait_ge(norm_done, c + 2)
                norm_rows(augk[at][0:32, :], bank[4]).then_inc(aug_done, 1)

            def split_lo(c, at):
                dve.wait_ge(xh_ready, c + 2)
                V.tensor_tensor(xl[at][:], x_raw[at][:], raw(xh[at][:]), ALU.subtract).then_inc(xl_ready, 1)

            def sweep_begin(s, blk):
                dve.wait_ge(sw_pool_done, s + 1)
                own.wait()
                at, kept = bass.ds(s, 1), (blk + 1) * SW
                row = g3[:, at, 0:kept].rearrange("p a c -> p (a c)")
                V.tensor_scalar(sw_v[:, 0:kept], row, 1.0, None, ALU.mult)
                if kept < NL:
                    V.tensor_scalar(sw_v[:, kept:], g3[:, kept:, at].rearrange("p r a -> p (r a)"), 1.0, None, ALU.mult)
                own.then(V.reciprocal(sw_p[:], g3[:, at, at].rearrange("p a c -> p (a c)")))
                own.then(V.tensor_scalar(sw_r[:], sw_v[:], sw_p[:], None, ALU.mult))
                V.tensor_scalar(sw_r[:, at], sw_p[:], -1.0, None, ALU.mult)
                V.tensor_copy(sw_v[:, at], minus1[:])
                own.then(V.tensor_scalar(g3[:, blk * SW:, at].rearrange("p r a -> p (r a)"), zero_c[:, blk * SW:], 1.0, None,
                                         ALU.mult))
                V.tensor_scalar(row, zero_c[:, 0:kept], 1.0, None, ALU.mult).then_inc(sw_ready, 1)

            def sweep_first_rows(s):
                dve.wait_ge(sw_ready, s + 1)
                for n in range(SWB - 2):
                    step = V.tensor_tensor(block_row(t3, n), *outer(n), ALU.mult)
                own.then(step)
                for n in range(SWB - 2):
                    step = V.tensor_tensor(block_row(g3, n), block_row(g3, n), block_row(t3, n), ALU.subtract)
                own.did(step)

            def sweep_last_row(s):
                dve.wait_ge(sw_prod, 2 * s + 1)
                own.did(V.tensor_tensor(block_row(g3, SWB - 1), block_row(g3, SWB - 1), block_row(t3, SWB - 1), ALU.subtract))

            dve.wait_ge(l2_ready, 1)
            for i, b in enumerate(W_ORDER):
                if i == 1:
                    dve.wait_ge(x_loaded[0], 16)
                    split_lo(0, 1)
                if i == 2:
                    keys_lo(0, 1)
                    dve.wait_ge(const_set, 1)
                    for tp in range(2):
                        values(0, tp, 0)
                    key_norms(0, 1)
                    dve.wait_ge(x_loaded[1], 16)
                    split_lo(1, 0)
                if i >= 2:
                    dve.wait_ge(dist_done, 2 * (i - 1))
                block_hi(b, b % 2, False).then_inc(bd_ready, 1)
            dve.wait_ge(g_loaded, 16)
            own.then(V.tensor_scalar(g_all, g_all, phi_max[:], phi_min[:], ALU.min, ALU.max))
            own.did(V.tensor_scalar(g_all[:, 0:NL * NL:NL + 1], g_all[:, 0:NL * NL:NL + 1], REG, None, ALU.add))
            for blk in range(SWB):
                with dve.Fori(0, BATCH // SWB) as turn:
                    own.enter(turn, CPB * (2 * (3 + 3) + 1))
                    b = turn + blk * (BATCH // SWB)
                    for cc in range(CPB):
                        c = b * CPB + cc
                        clamp(c, 0)
                        sweep_begin(2 * c, blk)
                        sweep_first_rows(2 * c)
                        keys_lo(c + 1, cc % 2)
                        clamp(c, 1)
                        values(c + 1, 0, (cc + 1) % 2)
                        dve.wait_ge(dist_done, W_EXPS + 8 * c)
                        key_norms(c + 1, cc % 2)
                        sweep_last_row(2 * c)
                        clamp(c, 2)
                        sweep_begin(2 * c + 1, blk)
                        values(c + 1, 1, (cc + 1) % 2)
                        clamp(c, 3)
                        sweep_first_rows(2 * c + 1)
                        if cc == CPB - 1:
                            dve.wait_ge(dist_done, W_EXPS + 8 * (c + 1))
                            block_hi(b + 1, 0, True).then_inc(bd_ready, 1)
                        sweep_last_row(2 * c + 1)
                    own.leave(BATCH // SWB)
            own.wait()
            dve.wait_ge(sw_pool_done, NL + 1)
            for n in range(1, SWB):
                for m in range(n):
                    step = V.tensor_copy(g3[:, m * SW:(m + 1) * SW, n * SW:(n + 1) * SW],
                                         g3[:, n * SW:(n + 1) * SW, m * SW:(m + 1) * SW].rearrange("p r c -> p c r"))
            step.then_inc(inv_done, 1)

            def queries_lo(c):
                for s in range(KC):
                    dve.wait_ge(qs_ready, 2 * c + s + 1)
                    project_lo(kl[0], kh[0], bank[6 + s], bq_sb, s).then_inc(ql_done, 1)

            def query_norms(c):
                dve.wait_ge(qnorm_done, c + 1)
                norm_rows(augk[0][0:32, :], bank[4]).then_inc(qaug_done, 1)

            def block_hi_q(b):
                for s in range(KC):
                    V.tensor_tensor(bdh[0][:, s], rep(l2h[:, s, in_batch(b)], 1, HPS),
                                    rep(cst[:, C_HEAD:C_HEAD + HPS], 2, NL), ALU.mult).then_inc(qbdh_ready, 1)

            def q_clamp(c, pairs):
                for i in pairs:
                    dve.wait_ge(qexp_done, PAIRS * (c + 1) + i + 1)
                    V.tensor_scalar(phi[:, i], phi[:, i], phi_max[:], phi_min[:], ALU.min, ALU.max).then_inc(qphi_ready, 1)

            def landmark_values(b):
                dve.wait_ge(y_done, b + 1)
                y = bank[4][:, 0:PAIRS * 32].rearrange("p (i c) -> p i c", i=PAIRS)
                for u in range(2):
                    half = slice(64 * u, 64 * u + 64)
                    V.tensor_scalar(y_cur[half, :, 16 * u:16 * u + 16], y[half, :, 0:HD], -1.0, None, ALU.mult)
                    last = V.tensor_scalar(y_cur[half, :, 32 + 16 * u:48 + 16 * u],
                                           y[half, :, HD:HD + 1].broadcast_to([64, PAIRS, HD]), -1.0, None, ALU.mult)
                last.then_inc(y_ready, 1)

            def norm_begin(c, s):
                dve.wait_ge(out_done, 2 * c + s + 1)
                dve.wait_ge(attn_ready, 2 * c + s)
                own.then(V.tensor_scalar(nrm[:], bank[5][:], NORM_MIN, None, ALU.max))
                own.did(V.reciprocal(nrm[:, 0:CH // 2], nrm[:, 0:CH // 2]))

            def norm_end(c, s):
                own.then(V.reciprocal(nrm[:, CH // 2:], nrm[:, CH // 2:]))
                if not isinstance(c, int):
                    dve.wait_ge(attnl_ready, 2 * c + s - 1)
                V.tensor_tensor(attn[:, s], bank[4][:], nrm[:], ALU.mult).then_inc(attn_ready, 1)

            def residual_stats(c, at):
                dve.wait_ge(xb_ready, c + 1)
                for t in range(TPC):
                    if t % 2 == 0:
                        dve.wait_ge(wo_done, 2 * c + t // 2 + 1)
                    V.tensor_tensor(x1[at][:, t], bank[t // 2][:, 256 * (t % 2):256 * (t % 2) + 256], x_tok[:, t],
                                    ALU.add).then_inc(h_done, 1)
                dve.wait_ge(h_done, TPC * (c + 2))
                for t in range(TPC):
                    step = V.bn_stats(st1[:, t], x1[at][:, t])
                own.then(step)
                dve.sem_inc(dve_waited, 1)
                for t in range(TPC):
                    step = V.bn_aggr(mv1[:, t], st1[:, t])
                step.then_inc(ln1_stats, 1)

            def x1_lo(c, at):
                for tp in range(2):
                    dve.wait_ge(x1h_ready, 2 * c + tp + 1)
                    V.tensor_tensor(x1l[at][:, :, tp * 256:tp * 256 + 256].rearrange("p k (t j) -> p t k j", t=2),
                                    bank[tp][:].rearrange("p (t k j) -> p t k j", t=2, k=KC),
                                    raw(x1h[at][:, :, tp * 256:tp * 256 + 256]).rearrange("p k (t j) -> p t k j", t=2),
                                    ALU.subtract).then_inc(x1l_ready, 1)

            def gates(p, at):
                dve.wait_ge(gate_done, p + 1)
                logit = bank[0][:, 0:TPC * 2 * E].rearrange("p (t e) -> p t e", t=TPC)
                own.then(V.tensor_tensor(lg0[:], logit[:, :, 0:E], rep(bg_sb[:], 1, TPC), ALU.add))
                V.tensor_tensor(lg[:], logit[:, :, E:2 * E], lg0[:], ALU.add).then_inc(gate_read, 1)
                dve.wait_ge(gate_read, p + 1)
                dve.sem_inc(dve_waited, 1)
                for t in range(TPC):
                    step = V.max(m8[:, t], lg[:, t])
                own.then(step)
                V.tensor_tensor(gd[:], m8[:, :, 1], m8[:, :, 0], ALU.subtract).then_inc(gd_ready, 1)
                for t in range(TPC):
                    step = V.max_index(i8[:, t], m8[:, t], lg[:, t])
                own.then(step)
                own.then(V.tensor_copy(if2[:], i8[:, :, 0:2]))
                iota = rep(cst[:, C_IOTA:C_IOTA + E], 1, TPC)
                V.tensor_tensor(oh1[:], iota, rep(if2[:, :, 0], 2, E), ALU.is_equal)
                V.tensor_tensor(oh2[:], iota, rep(if2[:, :, 1], 2, E), ALU.is_equal)
                dve.wait_ge(ge_ready, p + 1)
                own.then(V.tensor_scalar(gs[:], ge[:], 1.0, None, ALU.add))
                own.then(V.reciprocal(gw1[:], gs[:]))
                own.then(V.tensor_tensor(gw2[:], gw1[:], ge[:], ALU.mult))
                V.tensor_tensor(oh1[:], oh1[:], rep(gw1[:], 2, E), ALU.mult)
                own.then(V.tensor_tensor(oh2[:], oh2[:], rep(gw2[:], 2, E), ALU.mult))
                own.then(V.tensor_tensor(gate[at][:], oh1[:], oh2[:], ALU.add))
                own.then(V.tensor_copy(gate_h[:], gate[at][:]))
                V.tensor_copy(g_st[:, :, 0:E], raw(gate_h[:]))
                V.tensor_tensor(g_st[:, :, E:2 * E], gate[at][:], raw(gate_h[:]), ALU.subtract)
                V.tensor_copy(g_st[:, :, 2 * E:3 * E], raw(gate_h[:])).then_inc(gst_ready, 1)
                dve.wait_ge(gst_ready, p + 1)

            def add_bias(p, at):
                for t in range(TPC):
                    if t % 2 == 0:
                        dve.wait_ge(be_done, 2 * p + t // 2 + 1)
                    step = V.tensor_tensor(x1[at][:, t], bank[t // 2][:, 256 * (t % 2):256 * (t % 2) + 256],
                                           x1[at][:, t], ALU.add)
                step.then_inc(be_added, 1)

            def combine(p, n, at):
                t, q = n // 4, n % 4
                k = 8 * p + n // 2
                dve.wait_ge(ffn_done, 16 * p + BANK_ORDER.index(n) + 1)
                if q == 0:
                    dve.wait_ge(be_added, p + 1)
                    dve.wait_ge(res_ready, TPC * p + t + 3)
                else:
                    dve.wait_ge(comb_done, k + 1)
                a = acc[:, t % 2]
                own.then(V.scalar_tensor_tensor(a, bank[2][:, 0:D], gate[at][:, t, 2 * q:2 * q + 1],
                                                x1[at][:, t] if q == 0 else a, ALU.mult, ALU.add))
                V.scalar_tensor_tensor(a, bank[2][:, D:2 * D], gate[at][:, t, 2 * q + 1:2 * q + 2], a,
                                       ALU.mult, ALU.add).then_inc(comb_done, 1)

            def finish(p, t):
                dve.wait_ge(part_sum, TPC * p + t + 1)
                dve.wait_ge(comb_done, 8 * p + 2 * t + 3)
                V.tensor_tensor(acc[:, t % 2], acc[:, t % 2], part[:, 0, 0:D], ALU.add).then_inc(acc_done, 1)
                dve.wait_ge(acc_done, TPC * p + t + 2)
                own.then(V.bn_stats(st2[:, t], acc[:, t % 2]))
                dve.sem_inc(dve_waited, 1)
                V.bn_aggr(mv2[:, t], st2[:, t]).then_inc(ln2_stats, 1)

            dve.wait_ge(z_done, TPC * (NCH + 1))
            dve.wait_ge(winv_stored, 32)
            own.then(V.memset(y_cur[:], 0.0))
            block_hi_q(0)
            queries_lo(0)
            query_norms(0)
            q_clamp(0, range(PAIRS))
            landmark_values(0)
            norm_begin(0, 0)
            norm_end(0, 0)
            norm_begin(0, 1)
            norm_end(0, 1)
            queries_lo(1)
            query_norms(1)
            for i in range(2 * KC):
                dve.wait_ge(w_split_h, i + 2)
                k, half = i // 2, slice(1024 * (i % 2), 1024 * (i % 2 + 1))
                V.tensor_tensor(wel[:, k, half], we_raw[i], raw(weh[:, k, half]), ALU.subtract).then_inc(w_split_l, 1)
            dve.wait_ge(w_split_l, 1 + 2 * KC)
            residual_stats(0, 0)
            q_clamp(1, range(PAIRS))
            x1_lo(0, 0)
            gates(0, 0)
            norm_begin(1, 0)
            norm_end(1, 0)
            norm_begin(1, 1)
            norm_end(1, 1)
            queries_lo(2)
            query_norms(2)
            with dve.Fori(0, BATCH) as b:
                own.enter(b, CPB * (2 * 3 + 1 + 11 + 2 * TPC + TPC))
                for cc in range(CPB):
                    p = b * CPB + cc
                    c, q = p + 1, p + 2
                    me, nxt = cc % 2, (cc + 1) % 2
                    add_bias(p, me)
                    combine(p, 0, me)
                    residual_stats(c, nxt)
                    q_clamp(q, range(0, 2))
                    combine(p, 2, me)
                    if q_starts_batch(cc):
                        landmark_values(b + 1)
                    q_clamp(q, range(2, 4))
                    q_clamp(q, range(4, 6))
                    x1_lo(c, nxt)
                    finish(p, 0)
                    combine(p, 4, me)
                    norm_begin(q, 0)
                    q_clamp(q, range(6, 8))
                    norm_end(q, 0)
                    combine(p, 6, me)
                    gates(c, nxt)
                    combine(p, 8, me)
                    finish(p, 1)
                    norm_begin(q, 1)
                    combine(p, 10, me)
                    norm_end(q, 1)
                    queries_lo(q + 1)
                    finish(p, 2)
                    combine(p, 12, me)
                    query_norms(q + 1)
                    if q_ends_batch(cc):
                        dve.wait_ge(qdist_done, PAIRS * (q + 1))
                        block_hi_q(b + 1)
                    combine(p, 14, me)
                    finish(p, 3)
                own.leave(BATCH)

        @block.tensor
        def _(pe):
            mm = nc.tensor.matmul
            WK, WV, WQ, WO = range(4)

            def project_T(w, at, s, dst):
                cols = slice(s * P, (s + 1) * P)
                for k in range(KC):
                    last = product3(dst, wh[:, w, k, cols], wl[:, w, k, cols], xh[at][:, k], xl[at][:, k],
                                    k == 0, k == KC - 1)
                return last

            def square_norms(dst):
                for s in range(KC):
                    last = mm(dst[0:32, :], neg_block[:, s, :], sq[:, s], start=(s == 0), stop=(s == KC - 1))
                return last

            pe.wait_ge(small_loaded, 16 * 9)
            pe.wait_ge(gathered, 64)
            for k in range(KC):
                for i in range(4):
                    last = nc.tensor.transpose(bank[k][:, i * P:(i + 1) * P], lm_x[:, i, k * P:(k + 1) * P], ident)
                last.then_inc(lmT_done, 1)
            pe.wait_ge(w_split_l, 1)
            pe.wait_ge(xl_ready, 1)
            for s in range(KC):
                project_T(WK, 0, s, bank[2 + s][:]).then_inc(kproj_done, 1)
            pe.wait_ge(s_ready, 2)
            square_norms(bank[4]).then_inc(norm_done, 1)
            for b in range(BATCH):
                for s in range(KC):
                    for u in range(2):
                        at = b * PAIRS + s * 4
                        last = mm(bank[5][64 * u:64 * u + 64, at:at + 4], sq[:, s, b * NL:(b + 1) * NL],
                                  neg_sel[:, u, :], start=True, stop=True)
            last.then_inc(nl_done, 1)
            pe.wait_ge(aug_done, 1)
            pe.wait_ge(setup_done, 1)

            def key_dists(dst, at, tok, bd, s):
                wide = lambda a: a.rearrange("p h k -> p (h k)")
                mm(dst, kh[at][:, s, tok], wide(bdh[bd][:, s]), start=True, stop=False)
                mm(dst, kl[at][:, s, tok], wide(bdh[bd][:, s]), start=False, stop=False)
                mm(dst, kh[at][:, s, tok], wide(bdl[bd][:, s]), start=False, stop=False)
                return mm(dst, augk[at][:, tok], wide(augm[bd][:, s]), start=False, stop=True)

            def keys(c, at):
                pe.wait_ge(xh_ready, c + 2)
                pe.wait_ge(xl_ready, c + 2)
                pe.wait_ge(kl_done, 2 * (c + 1))
                for s in range(KC):
                    project_T(WK, at, s, bank[2 + s][:]).then_inc(kproj_done, 1)

            def values(c, tp, at):
                if isinstance(c, int):
                    pe.wait_ge(xl_ready, 1)
                else:
                    pe.wait_ge(v_done, 2 * c + tp - 1)
                for t in (2 * tp, 2 * tp + 1):
                    tok = slice(t * P, (t + 1) * P)
                    dst = bank[tp][:, 256 * (t % 2):256 * (t % 2) + 256]
                    for k in range(KC):
                        last = product3(dst, xh[at][:, k, tok], xl[at][:, k, tok], wh[:, WV, k], wl[:, WV, k],
                                        k == 0, k == KC - 1)
                last.then_inc(vproj_done, 1)

            def key_norms(c):
                pe.wait_ge(s_ready, 2 * (c + 2))
                pe.wait_ge(aug_done, c + 1)
                square_norms(bank[4]).then_inc(norm_done, 1)

            def dists(c, t, at):
                if t == 0:
                    pe.wait_ge(kl_done, 2 * (c + 2))
                    pe.wait_ge(aug_done, c + 2)
                for s in range(KC):
                    pe.wait_ge(exp_done, W_EXPS + 8 * c + 2 * t + s - 1)
                    key_dists(bank[6 + s][:], at, slice(t * P, (t + 1) * P), 0, s).then_inc(dist_done, 1)

            def sums(c, t, at, first, last_tile):
                pe.wait_ge(phi_ready, 8 * c + 2 * t + 2)
                for g in range(4):
                    for j in range(4):
                        head = 4 * g + j
                        s, hs = head // HPS, head % HPS
                        last = mm(bank[5][32 * j:32 * j + 32, g * NL:(g + 1) * NL], v_aug[at][:, t, head, :],
                                  phi[:, 2 * t + s, hs * NL:(hs + 1) * NL], start=(first and g == 0), stop=last_tile,
                                  skip_group_check=True)
                last.then_inc(z_done, 1)

            keys(0, 1)
            for tp in range(2):
                values(0, tp, 1)
            key_norms(0)
            for i, b in enumerate(W_ORDER):
                pe.wait_ge(bd_ready, i + 1)
                pe.wait_ge(bdl_ready, i + 1)
                for s in range(KC):
                    if i:
                        pe.wait_ge(exp_done, 2 * i + s - 1)
                    key_dists(bank[6 + s][0:64, :], 0, slice(b * NL, (b + 1) * NL), b % 2, s).then_inc(dist_done, 1)
            pe.wait_ge(nl_ready, 1)
            with pe.Fori(0, BATCH) as b:
                for cc in range(CPB):
                    c = b * CPB + cc
                    me, nxt = (cc + 1) % 2, cc % 2
                    if cc == 0:
                        pe.wait_ge(bd_ready, BATCH + b)
                    dists(c, 0, me)
                    keys(c + 1, nxt)
                    dists(c, 1, me)
                    if cc == 0:
                        pe.wait_ge(zt_saved, b + 1)
                    pe.wait_ge(v_done, 2 * (c + 1))
                    sums(c, 0, cc % 2, cc == 0, False)
                    values(c + 1, 0, nxt)
                    key_norms(c + 1)
                    dists(c, 2, me)
                    sums(c, 1, cc % 2, False, False)
                    values(c + 1, 1, nxt)
                    dists(c, 3, me)
                    sums(c, 2, cc % 2, False, False)
                    sums(c, 3, cc % 2, False, cc == CPB - 1)

            def queries(c, at):
                pe.wait_ge(xqh_ready, c + 1)
                pe.wait_ge(xql_ready, c + 1)
                for s in range(KC):
                    pe.wait_ge(qexp_done, PAIRS * c + s + 7)
                    project_T(WQ, at, s, bank[6 + s][:]).then_inc(qproj_done, 1)

            def query_norms(c):
                pe.wait_ge(qs_ready, 2 * (c + 1))
                pe.wait_ge(attn_ready, 2 * c)
                square_norms(bank[4]).then_inc(qnorm_done, 1)

            def query_dists(c, pairs):
                for i in pairs:
                    s, h0 = i // 4, 2 * (i % 4)
                    dst = bank[6 + i % 2][:]
                    if i == 0:
                        pe.wait_ge(qaug_done, c + 1)
                    if i < 2:
                        pe.wait_ge(ql_done, 2 * (c + 1))
                    else:
                        pe.wait_ge(qexp_done, PAIRS * c + i + 7)
                    pair = lambda a: a[:, s, h0:h0 + 2].rearrange("p u k -> p (u k)")
                    product3(dst, pair(bdh[0]), pair(bdl[0]), kh[0][:, s], kl[0][:, s], True, False)
                    mm(dst, sel_q[:, i], augk[0][0:32, :], start=False, stop=True).then_inc(qdist_done, 1)

            def z_transposes(b):
                pe.wait_ge(zt_cur_ready, b + 1)
                pe.sem_inc(pe_waited, 1)
                for g in range(4):
                    last = nc.tensor.transpose(bank[5][0:64, g * P:(g + 1) * P], zt_cur[:, g * NL:(g + 1) * NL], ident)
                last.then_inc(ztr_done, 1)

            def landmark_solve(b):
                pe.wait_ge(zk_ready, b + 1)
                pe.wait_ge(winv_loaded, 16 * (b + 1))
                pe.sem_inc(pe_waited, 1)
                for head in range(H):
                    u, i = head % 2, head // 2
                    last = mm(bank[4][64 * u:64 * u + 64, 32 * i:32 * i + 32], winv_sb[:, head, :],
                              zk[:, 32 * head:32 * head + 32], start=True, stop=True)
                last.then_inc(y_done, 1)

            def attention(c, half):
                pe.wait_ge(qphi_ready, PAIRS * c + 4 * half + 4)
                pe.wait_ge(attn_ready, 2 * c + half)
                for n, dst in ((0, bank[4]), (32, bank[5])):
                    for j in range(4):
                        last = mm(dst[32 * j:32 * j + 32, :], y_cur[:, 4 * half + j, n:n + 32], phi[:, 4 * half + j],
                                  start=True, stop=True)
                last.then_inc(out_done, 1)

            def output_projection(p):
                pe.wait_ge(attnl_ready, 2 * (p + 1))
                pe.wait_ge(be_added, p)
                for tp in range(2):
                    for t in (2 * tp, 2 * tp + 1):
                        tok = slice(t * P, (t + 1) * P)
                        dst = bank[tp][:, 256 * (t % 2):256 * (t % 2) + 256]
                        for k in range(KC):
                            last = product3(dst, attn_h[:, k, tok], attn_l[:, k, tok], wh[:, WO, k], wl[:, WO, k],
                                            k == 0, k == KC - 1)
                    last.then_inc(wo_done, 1)

            def x1_transposes(p, at_x):
                for tp in range(2):
                    pe.wait_ge(x1_ready, TPC * (p + 1) + 2 * tp + 2)
                    for t in (2 * tp, 2 * tp + 1):
                        for k in range(KC):
                            at = 256 * (t % 2) + 128 * k
                            last = nc.tensor.transpose(bank[tp][:, at:at + P], x1[at_x][:, t, k * P:(k + 1) * P], ident)
                    last.then_inc(x1t_done, 1)

            def gate_logits(p, at):
                pe.wait_ge(x1l_ready, 2 * (p + 1))
                for t in range(TPC):
                    tok = slice(t * P, (t + 1) * P)
                    for k in range(KC):
                        for u, a in enumerate((x1h[at], x1l[at])):
                            last = mm(bank[0][:, 16 * t:16 * t + 16], a[:, k, tok], wg_s[:, k],
                                      start=(k == 0 and u == 0), stop=(k == KC - 1 and u == 1))
                last.then_inc(gate_done, 1)

            def gate_transposes(p):
                pe.wait_ge(gst_ready, p + 1)
                for t in range(TPC):
                    last = nc.tensor.transpose(bank[1][0:24, t * P:(t + 1) * P], g_st[:, t], ident)
                last.then_inc(gtr_done, 1)

            def bias_term(p):
                pe.wait_ge(gt_ready, p + 1)
                pe.wait_ge(gate_read, p + 1)
                for tp in range(2):
                    for t in (2 * tp, 2 * tp + 1):
                        last = mm(bank[tp][:, 256 * (t % 2):256 * (t % 2) + 256], g_t[:, t * P:(t + 1) * P], be_s[:],
                                  start=True, stop=True)
                    last.then_inc(be_done, 1)

            def experts(p, n, at):
                t, q = n // 4, n % 4
                tok = slice(t * P, (t + 1) * P)
                pe.wait_ge((comb_done, part_ready)[n % 2], 8 * p + n // 2 + 1)
                cols = slice(512 * q, 512 * (q + 1))
                for k in range(KC):
                    last = product3(bank[2 + n % 2][:], x1h[at][:, k, tok], x1l[at][:, k, tok], weh[:, k, cols],
                                    wel[:, k, cols], k == 0, k == KC - 1)
                last.then_inc(ffn_done, 1)

            pe.wait_ge(exp_done, W_EXPS + 8 * NCH)
            pe.wait_ge(kl_done, 2 * (NCH + 2))
            pe.wait_ge(v_done, 2 * (NCH + 1))
            pe.wait_ge(aug_done, NCH + 2)
            pe.wait_ge(zt_saved, BATCH + 1)
            pe.wait_ge(xl_ready, NCH + 3)
            queries(0, 1)
            z_transposes(0)
            query_norms(0)
            pe.wait_ge(qbdh_ready, KC)
            pe.wait_ge(qbdl_ready, KC)
            query_dists(0, range(PAIRS))
            landmark_solve(0)
            pe.wait_ge(y_ready, 1)
            attention(0, 0)
            attention(0, 1)
            queries(1, 0)
            query_norms(1)
            output_projection(0)
            query_dists(1, range(PAIRS))
            x1_transposes(0, 0)
            gate_logits(0, 0)
            attention(1, 0)
            attention(1, 1)
            queries(2, 1)
            query_norms(2)
            gate_transposes(0)
            pe.wait_ge(w_split_l, 1 + 2 * KC)
            with pe.Fori(0, BATCH) as b:
                for cc in range(CPB):
                    p = b * CPB + cc
                    c, q = p + 1, p + 2
                    me, nxt = cc % 2, (cc + 1) % 2
                    bias_term(p)
                    if q_starts_batch(cc):
                        pe.wait_ge(qbdh_ready, KC * (b + 2))
                        pe.wait_ge(qbdl_ready, KC * (b + 2))
                    query_dists(q, range(0, 2))
                    experts(p, 0, me)
                    experts(p, 1, me)
                    output_projection(c)
                    experts(p, 2, me)
                    if q_starts_batch(cc):
                        landmark_solve(b + 1)
                    query_dists(q, range(2, 4))
                    experts(p, 3, me)
                    query_dists(q, range(4, 6))
                    x1_transposes(c, nxt)
                    experts(p, 4, me)
                    if q_starts_batch(cc):
                        pe.wait_ge(y_ready, b + 2)
                    attention(q, 0)
                    query_dists(q, range(6, 8))
                    experts(p, 5, me)
                    gate_logits(c, nxt)
                    experts(p, 6, me)
                    experts(p, 7, me)
                    attention(q, 1)
                    experts(p, 8, me)
                    queries(q + 1, me)
                    experts(p, 9, me)
                    experts(p, 10, me)
                    gate_transposes(c)
                    experts(p, 11, me)
                    experts(p, 12, me)
                    experts(p, 13, me)
                    query_norms(q + 1)
                    if q_ends_batch(cc):
                        pe.wait_ge(attn_ready, 2 * (q + 1))
                        z_transposes(b + 1)
                    experts(p, 15, me)
                    experts(p, 14, me)


def shape_constants():
    import numpy as np
    c = np.zeros((P, C_END), np.float32)
    part = np.arange(P)
    c[:, C_ID:C_ID + P] = np.eye(P)
    c[:, C_HEAD:C_HEAD + HPS] = part[:, None] // HD == np.arange(HPS)
    for s in range(KC):
        c[:, C_NEG + 32 * s:C_NEG + 32 * (s + 1)] = -(np.arange(32) % H == (HPS * s + part // HD)[:, None]).astype(np.float32)
    c[:, C_LO] = -(part % 32 >= 16).astype(np.float32)
    c[:, C_M16:C_M16 + H] = part[:, None] % 16 == np.arange(H)
    for u in range(2):
        c[:, C_NSEL + 4 * u:C_NSEL + 4 * (u + 1)] = -(part[:, None] // HD == 2 * np.arange(4) + u).astype(np.float32)
    c[:, C_IOTA:C_IOTA + E] = np.arange(E)
    c[:, C_EXP:C_EXP + TPC] = -0.5
    c[16:24, C_BES] = -1.0
    c[:, C_EPS:C_EPS + TPC] = EPS
    c[:, C_MINUS:C_MINUS + TPC] = -1.0
    return c


def kernel(**inputs):
    import numpy as np
    import concourse.bacc as bacc
    from concourse.bass_utils import run_bass_kernel_spmd

    a = {k: np.asarray(v) for k, v in inputs.items()}
    rows = a["L0_attn_query"].reshape(T, D)
    x = np.concatenate([rows, rows[:2 * CH]])
    x_t = np.ascontiguousarray(np.concatenate([rows, rows[:AHEAD * CH]]).T)

    def columns(v):
        return np.ascontiguousarray(v.reshape(KC, P).T)

    def every_partition(v):
        return np.ascontiguousarray(np.broadcast_to(v.reshape(1, -1), (P, v.size)))

    first_row = (2 * np.arange(4)[None, :] + np.arange(P)[:, None] // NL) * SEQ
    arrays = {
        "xT": x_t, "x": x,
        "wq": a["L0_attn_Wq"].T, "wk": a["L0_attn_Wk"].T, "wv": a["L0_attn_Wv"].T, "wo": a["L0_attn_Wo"].T,
        "we": a["L0_ffn_We"].transpose(2, 0, 1).reshape(D, E * D), "wg": a["L0_ffn_Wg"].T,
        "bq": columns(a["L0_attn_bq"]), "bk": columns(a["L0_attn_bk"]),
        "bv": every_partition(a["L0_attn_bv"]), "bo": every_partition(a["L0_attn_bo"]),
        "be3": np.tile(a["L0_ffn_be"], (3, 1)), "bg": every_partition(a["L0_ffn_bg"]),
        "temp": every_partition(a["L0_attn_temperature"]),
        "idx": np.tile(a["L0_attn_landmark_idx"], 2).reshape(P, 1),
        "gbase": first_row.astype(np.int32), "consts": shape_constants(),
    }
    nc = bacc.Bacc("TRN2", target_bir_lowering=False, num_devices=1)
    arrays = {f"in_{k}": np.ascontiguousarray(v) for k, v in arrays.items()}
    args = [nc.dram_tensor(k, v.shape, mybir.dt.from_np(v.dtype), kind="ExternalInput").ap() for k, v in arrays.items()]
    out = nc.dram_tensor("out", (T, D), mybir.dt.float32, kind="ExternalOutput").ap()
    program(nc, *args, out)
    r = run_bass_kernel_spmd(nc, [arrays], core_ids=[0])
    return r.results[0]["out"].reshape(BATCH, SEQ, D)
```

```python
import concourse.bass as bass
from concourse import mybir
from contextlib import ExitStack

BATCH, SEQ, D, H, HD, NL, E = 8, 2048, 256, 16, 16, 64, 8
P = 128
T = BATCH * SEQ
CH = 512
CPB = SEQ // CH
NCH = T // CH
KC = D // P
HPS = H // KC
PAIRS = H // 2
GROUPS = H // 4
TPC = CH // P
AHEAD = 4
REG = 1e-6
EPS = 1e-5
NORM_MIN = 1e-10
BIG = 3.0e38
SW = 16
SWB = NL // SW

C_ID, C_HEAD, C_NEG, C_LO, C_M16, C_NSEL, C_IOTA, C_EXP, C_BES, C_EPS, C_MINUS, C_END = (
    0, 128, 136, 200, 201, 217, 225, 233, 237, 238, 242, 246)


def program(nc, xT, x, wq, wk, wv, wo, we, wg, bq, bk, bv, bo, be3, bg, temp, idx, gbase, consts, out):
    f32, f32r = mybir.dt.float32, mybir.dt.float32r
    i32, u32 = mybir.dt.int32, mybir.dt.uint32
    ALU, ACT = mybir.AluOpType, mybir.ActivationFunctionType

    w_dram = nc.dram_tensor("w_dram", [BATCH * H, NL, NL], f32).ap()
    winv_dram = nc.dram_tensor("winv_dram", [(BATCH + 1) * H, NL, NL], f32).ap()
    xT_v = xT.rearrange("(k p) t -> p k t", p=P)
    x_v = x.rearrange("(c t p) d -> c p t d", t=TPC, p=P)
    out_v = out.rearrange("(c t p) d -> c p t d", t=TPC, p=P)

    ctx = ExitStack()
    with ctx:
        def sb(name, shape, dt=f32):
            return ctx.enter_context(nc.sbuf_tensor(name, shape, dt))

        def sem(name):
            return ctx.enter_context(nc.semaphore(name))

        bank = [ctx.enter_context(nc.psum_tensor(f"bank{i}", [P, 512], f32)) for i in range(8)]

        cst = sb("cst", [P, C_END])
        ident = cst[:, C_ID:C_ID + P]
        neg_block = cst[:, C_NEG:C_NEG + 64].rearrange("p (s r) -> p s r", s=KC)
        lo_sign = cst[:, C_LO:C_LO + 1]
        neg_sel = cst[:, C_NSEL:C_NSEL + 8].rearrange("p (u i) -> p u i", u=2)
        bq_sb, bk_sb = sb("bq_sb", [P, KC]), sb("bk_sb", [P, KC])
        bo_sb = sb("bo_sb", [P, D])
        bg_sb, temp_sb, invt = sb("bg_sb", [P, E]), sb("temp_sb", [P, 1]), sb("invt", [P, 1])
        phi_max, phi_min, tpos = sb("phi_max", [P, 1]), sb("phi_min", [P, 1]), sb("tpos", [P, 1])
        idx_sb, gbase_sb, rows_sb = sb("idx_sb", [P, 1], i32), sb("gbase_sb", [P, 4], i32), sb("rows_sb", [P, 4], i32)
        wh, wl = sb("wh", [P, 4, KC, D], f32r), sb("wl", [P, 4, KC, D], f32r)
        with nc.sbuf_tensor("inversion", [P, 2, NL * NL], f32) as inversion:
            g_all, t_all = inversion[:, 0], inversion[:, 1]
        g3 = g_all.rearrange("p (r c) -> p r c", r=NL)
        t3 = t_all.rearrange("p (r c) -> p r c", r=NL)
        w_raw = t_all[:, 0:2048].rearrange("p (w k n) -> p w k n", w=4, k=KC)
        wk_sb = [t_all[0:64, 2048 + 1024 * i:3072 + 1024 * i].rearrange("p (s h k) -> p s h k", s=KC, h=HPS)
                 for i in range(2)]
        weh, wel = sb("weh", [P, KC, E * D], f32r), sb("wel", [P, KC, E * D], f32r)
        wg_raw, wg_s = sb("wg_raw", [P, KC, E]), sb("wg_s", [P, KC, 2 * E], f32r)
        be_s = sb("be_s", [24, D], f32r)

        NB1 = BATCH + 1
        l2h, l2l = sb("l2h", [P, KC, NB1 * NL]), sb("l2l", [P, KC, NB1 * NL])
        nlt, nlt_cur = sb("nlt", [P, NB1, PAIRS]), sb("nlt_cur", [P, PAIRS])

        x_raw = [sb("x_raw0", [P, KC, CH])]
        with nc.sbuf_tensor("xh0", [P, KC, CH], f32r) as xh0, nc.sbuf_tensor("xl0", [P, KC, CH], f32r) as xl0:
            xh, xl = [xh0], [xl0]
        part_x = sb("part_x", [P, 2, KC, 2 * D])
        xh.append(sb("xh1", [P, KC, CH], f32r))
        xl.append(sb("xl1", [P, KC, CH], f32r))
        kh, kl = [sb("kh0", [P, KC, CH], f32r)], [sb("kl0", [P, KC, CH], f32r)]
        sq = sb("sq", [P, KC, CH])
        augk = [sb("augk0", [64, CH], f32r)]
        aug_hi = sb("aug_hi", [32, CH], f32r)
        phi = sb("phi", [P, 8, CH])
        zt = sb("zt", [P, NB1, 4 * NL])
        attn_h, attn_l = sb("attn_h", [P, KC, CH], f32r), sb("attn_l", [P, KC, CH], f32r)
        lm_x = phi[:, 0:2, :].rearrange("p a (b d) -> p (a b) d", b=2)
        sw_v, sw_r, sw_p = sb("sw_v", [P, NL]), sb("sw_r", [P, NL]), sb("sw_p", [P, 1])
        zero_c, minus1 = sb("zero_c", [P, NL]), sb("minus1", [P, 1])
        st1, mv1, ve1, rs1, nm1 = (sb("st1", [P, TPC, 6]), sb("mv1", [P, TPC, 2]), sb("ve1", [P, TPC]),
                                   sb("rs1", [P, TPC]), sb("nm1", [P, TPC]))
        st2, mv2, ve2, rs2, nm2 = (sb("st2", [P, TPC, 6]), sb("mv2", [P, TPC, 2]), sb("ve2", [P, TPC]),
                                   sb("rs2", [P, TPC]), sb("nm2", [P, TPC]))
        nt1, nt2 = sb("nt1", [P, TPC]), sb("nt2", [P, TPC])
        lg0, lg, m8, i8 = (sb("lg0", [P, TPC, E]), sb("lg", [P, TPC, E]), sb("m8", [P, TPC, 8]),
                           sb("i8", [P, TPC, 8], u32))
        if2, gd, ge, gs, gw1, gw2 = (sb("if2", [P, TPC, 2]), sb("gd", [P, TPC]), sb("ge", [P, TPC]),
                                     sb("gs", [P, TPC]), sb("gw1", [P, TPC]), sb("gw2", [P, TPC]))
        oh1, oh2, gate, gate_h = (sb("oh1", [P, TPC, E]), sb("oh2", [P, TPC, E]),
                                  [sb(f"gate{i}", [P, TPC, E]) for i in range(2)],
                                  sb("gate_h", [P, TPC, E], f32r))
        g_st, g_t = sb("g_st", [P, TPC, 24]), sb("g_t", [24, CH], f32r)

        with ExitStack() as stage1:
            def sb1(name, shape, dt=f32):
                return stage1.enter_context(nc.sbuf_tensor(name, shape, dt))

            v_aug = [sb1(f"v_aug{i}", [P, TPC, H, 32]) for i in range(2)]
            bv_sb = sb1("bv_sb", [P, D])
            x_raw.append(sb1("x_raw1", [P, KC, CH]))
            ln_rows = sb1("ln_rows", [64, NB1 * NL])
            l_hh, l_lo = [sb1(f"l_{n}", [P, GROUPS, 4, NL], f32r) for n in ("hh", "lo")]
            with ExitStack() as setup:
                def sb0(name, shape, dt=f32):
                    return setup.enter_context(nc.sbuf_tensor(name, shape, dt))

                bdh = [sb0(f"bdh{i}", [P, KC, HPS, NL], f32r) for i in range(2)]
                bdl = [sb0(f"bdl{i}", [P, KC, HPS, NL], f32r) for i in range(2)]
                kh.append(sb0("kh1", [P, KC, CH], f32r))
                kl.append(sb0("kl1", [P, KC, CH], f32r))
                augk.append(sb0("augk1", [64, CH], f32r))
                augm = [sb0(f"augm{i}", [64, KC, HPS, NL], f32r) for i in range(2)]
                be_raw, be_tmp = sb0("be_raw", [24, D]), sb0("be_tmp", [24, D], f32r)
            k_hl, k_ha = zip(*[[sb1(f"{n}{i}", [P, GROUPS, CH], f32r) for n in ("k_hl", "k_ha")] for i in range(2)])
        x_tok, y_out = sb("x_tok", [P, TPC, D]), sb("y_out", [P, TPC, D])
        x1 = [sb(f"x1_{i}", [P, TPC, D]) for i in range(2)]
        x1h, x1l = [sb("x1h0", [P, KC, CH], f32r)], [sb("x1l0", [P, KC, CH], f32r)]
        x1h.append(sb("x1h1", [P, KC, CH], f32r))
        x1l.append(sb("x1l1", [P, KC, CH], f32r))
        part = sb("part", [P, 2, 2 * D])
        parts = [[*(part_x[:, i, k] for k in range(KC)), part[:, i]] for i in range(2)]
        nrm = sb("nrm", [P, CH])
        q_stack, l_stack = sb("q_stack", [P, PAIRS, CH], f32r), sb("l_stack", [P, PAIRS, 2, NL], f32r)
        attn = sb("attn", [P, KC, CH])
        zt_cur, zk = sb("zt_cur", [P, 4 * NL]), sb("zk", [64, H * 32])
        winv_sb, y_cur = sb("winv_sb", [64, H, NL]), sb("y_cur", [P, PAIRS, 64])
        we_raw = [a[:].rearrange("p t d -> p (t d)") for a in (*x1, y_out, part)]

        idx_loaded, small_loaded, w_loaded, we_loaded = (sem("idx_loaded"), sem("small_loaded"), sem("w_loaded"),
                                                         sem("we_loaded"))
        rows_ready, gathered, const_set, setup_done = sem("rows_ready"), sem("gathered"), sem("const_set"), sem("setup_done")
        w_split_h, w_split_l = sem("w_split_h"), sem("w_split_l")
        lmT_done, l2_ready, nl_done, nl_ready = sem("lmT_done"), sem("l2_ready"), sem("nl_done"), sem("nl_ready")
        bd_ready, bdl_ready, w_stored, g_loaded = (
            sem("bd_ready"), sem("bdl_ready"), [sem(f"w_stored{i}") for i in range(2)], sem("g_loaded"))
        dve_step, pool_step = sem("dve_step"), sem("pool_step")
        dve_waited, pe_waited = sem("dve_waited"), sem("pe_waited")
        x_loaded, xh_ready, xl_ready = [sem(f"x_loaded{i}") for i in range(2)], sem("xh_ready"), sem("xl_ready")
        kproj_done, s_ready, kl_done, norm_done, aug_hi_ready, aug_done, k_stacked = (
            sem("kproj_done"), sem("s_ready"), sem("kl_done"), sem("norm_done"), sem("aug_hi_ready"),
            sem("aug_done"), sem("k_stacked"))
        vproj_done, v_done = sem("vproj_done"), sem("v_done")
        dist_done, exp_done, phi_ready, z_done, zt_saved = (
            sem("dist_done"), sem("exp_done"), sem("phi_ready"), sem("z_done"), sem("zt_saved"))
        sw_ready, sw_prod, sw_pool_done, inv_done = (
            sem("sw_ready"), sem("sw_prod"), sem("sw_pool_done"), sem("inv_done"))
        winv_stored, winv_loaded, zt_cur_ready, ztr_done, zk_ready, y_done, y_ready = (
            sem("winv_stored"), sem("winv_loaded"), sem("zt_cur_ready"), sem("ztr_done"), sem("zk_ready"),
            sem("y_done"), sem("y_ready"))
        xq_loaded, xqh_ready, xql_ready, xt_loaded, xb_ready = (
            sem("xq_loaded"), sem("xqh_ready"), sem("xql_ready"),
            sem("xt_loaded"), sem("xb_ready"))
        qproj_done, qs_ready, ql_done, qnorm_done, qaug_done = (
            sem("qproj_done"), sem("qs_ready"), sem("ql_done"), sem("qnorm_done"), sem("qaug_done"))
        nlt_ready, l_stacked, q_stacked, qdist_done, qexp_done, qphi_ready = (
            sem("nlt_ready"), sem("l_stacked"), sem("q_stacked"), sem("qdist_done"), sem("qexp_done"), sem("qphi_ready"))
        out_done, attn_ready, attnh_ready, attnl_ready = (
            sem("out_done"), sem("attn_ready"), sem("attnh_ready"), sem("attnl_ready"))
        wo_done, h_done, ln1_stats, ln1_coef, x1_ready, x1t_done, x1h_ready, x1l_ready = (
            sem("wo_done"), sem("h_done"), sem("ln1_stats"), sem("ln1_coef"), sem("x1_ready"),
            sem("x1t_done"), sem("x1h_ready"), sem("x1l_ready"))
        gate_done, gate_read, gd_ready, ge_ready, gst_ready, gtr_done, gt_ready, be_done, be_added = (
            sem("gate_done"), sem("gate_read"), sem("gd_ready"), sem("ge_ready"), sem("gst_ready"),
            sem("gtr_done"), sem("gt_ready"), sem("be_done"), sem("be_added"))
        ffn_done, comb_done, part_ready, part_sum, acc_done, ln2_stats, ln2_coef, res_ready, res_stored = (
            sem("ffn_done"), sem("comb_done"), sem("part_ready"), sem("part_sum"), sem("acc_done"), sem("ln2_stats"), sem("ln2_coef"),
            sem("res_ready"), sem("res_stored"))

        block = ctx.enter_context(nc.Block())

        W_ORDER = range(BATCH - 1, -1, -1)
        W_EXPS = 2 * BATCH

        def raw(ap):
            return ap.bitcast(f32)

        def rep(ap, axis, n):
            a = ap.unsqueeze(axis)
            shape = list(a.shape)
            shape[axis] = n
            return a.broadcast_to(shape)

        def in_batch(b, n=NL):
            return bass.ds(b * n, n)

        class Steps:

            def __init__(self, eng, semaphore):
                self.eng, self.sem, self.base, self.n = eng, semaphore, 0, 0

            def did(self, instruction):
                self.n += 1
                instruction.then_inc(self.sem, 1)

            def wait(self):
                self.eng.wait_ge(self.sem, self.base + self.n)

            def then(self, instruction):
                self.did(instruction)
                self.wait()

            def enter(self, i, per_turn):
                self.start = self.base + self.n
                self.per_turn, self.n = per_turn, 0
                self.base = self.start + i * per_turn

            def leave(self, turns):
                assert self.n == self.per_turn, (self.n, self.per_turn)
                self.base, self.n = self.start + turns * self.per_turn, 0

        def past_end(c):
            return isinstance(c, int) and c >= NCH

        def q_starts_batch(cc, b):
            return cc == CPB - 2 and not past_end((b + 1) * CPB)

        def q_ends_batch(cc, b):
            return cc == CPB - 3 and not past_end((b + 1) * CPB)

        def block_row(m, n):
            return m[:, n * SW:(n + 1) * SW, 0:(n + 1) * SW]

        def outer(n):
            return rep(sw_v[:, n * SW:(n + 1) * SW], 2, (n + 1) * SW), rep(sw_r[:, 0:(n + 1) * SW], 1, SW)

        def pairs_of(a, j, u=slice(None)):
            if len(a.shape) == 4:
                return a[:].rearrange("p (s j) u n -> p j s u n", s=KC)[:, j, :, u]
            return a[:].rearrange("p (s j) n -> p j s n", s=KC)[:, j]

        def groups_of(a, j):
            if len(a.shape) == 4:
                return a[:].rearrange("p (s j) u n -> p j s u n", s=KC)[:, j]
            return a[:].rearrange("p (s j) n -> p j s n", s=KC)[:, j]

        STACKED = 16 * 13
        K_STACKED = 16 * 7

        def product3(outp, ah, al, bh, bl, first, last):
            nc.tensor.matmul(outp, ah, bh, start=first, stop=False)
            nc.tensor.matmul(outp, al, bh, start=False, stop=False)
            return nc.tensor.matmul(outp, ah, bl, start=False, stop=last)

        @block.sync
        def _(sp):
            sp.sem_inc(z_done, TPC)
            sp.sem_inc(qexp_done, PAIRS)
            sp.sem_inc(acc_done, 2)
            sp.sem_inc(sw_pool_done, 1)
            sp.sem_inc(comb_done, 1)
            sp.sem_inc(part_ready, 2)
            sp.sem_inc(h_done, TPC)
            sp.sem_inc(x1_ready, TPC)
            sp.sem_inc(zt_saved, 1)
            sp.sem_inc(res_stored, 32)
            sp.sem_inc(xqh_ready, 2)
            sp.sem_inc(xql_ready, 2)
            for dst, src in ((idx_sb, idx), (gbase_sb, gbase)):
                sp.dma_start(dst[:], src).then_inc(idx_loaded, 16)
            for dst, src in ((cst, consts), (bq_sb, bq), (bk_sb, bk), (bv_sb, bv), (bo_sb, bo), (bg_sb, bg),
                             (temp_sb, temp), (be_raw, be3)):
                sp.dma_start(dst[:], src).then_inc(small_loaded, 16)
            sp.dma_start(wg_raw[:], wg.rearrange("(k p) e -> p k e", p=P)).then_inc(small_loaded, 16)
            for i, w in enumerate((wk, wv, wq, wo)):
                sp.dma_start(w_raw[:, i], w.rearrange("(k p) n -> p k n", p=P)).then_inc(w_loaded, 16)
            for c in range(2):
                sp.dma_start(x_raw[(c + 1) % 2][:], xT_v[:, :, c * CH:(c + 1) * CH]).then_inc(x_loaded[c], 16)
            for i, b in enumerate(W_ORDER):
                sp.wait_ge(exp_done, 2 * i + 2)
                sp.dma_start(w_dram[b * H:(b + 1) * H].rearrange("s k j -> k s j"),
                             wk_sb[i % 2].rearrange("p s h k -> p (s h) k")).then_inc(w_stored[i % 2], 16)
            for i in range(2):
                sp.wait_ge(w_stored[i], 16 * BATCH // 2)
            sp.dma_start(g_all, w_dram.rearrange("s k j -> s (k j)")).then_inc(g_loaded, 16)
            def stack_keys(c, src, at):
                for j in range(2):
                    half = slice(64 * j, 64 * j + 64)
                    if j == 0:
                        sp.wait_ge(s_ready, 2 * (c + 2))
                    sp.dma_start(raw(groups_of(k_hl[at], j)[0:64]), raw(kh[src][half])).then_inc(k_stacked, 16)
                    sp.dma_start(raw(groups_of(k_ha[at], j)[0:64]), raw(kh[src][half])).then_inc(k_stacked, 16)
                for j in range(2):
                    if j == 0:
                        sp.wait_ge(kl_done, 2 * (c + 2))
                    sp.dma_start(raw(groups_of(k_hl[at], j)[64:P]),
                                 raw(kl[src][64 * j:64 * j + 64])).then_inc(k_stacked, 16)
                sp.wait_ge(aug_done, c + 2)
                sp.dma_start(raw(k_ha[at][64:P]), rep(raw(augk[src][:]), 1, GROUPS)).then_inc(k_stacked, 16)

            sp.wait_ge(dist_done, W_EXPS)
            stack_keys(0, 1, 0)
            with sp.Fori(0, BATCH) as b:
                for cc in range(CPB):
                    c = b * CPB + cc
                    sp.wait_ge(xl_ready, c + 2)
                    sp.dma_start(x_raw[(cc + 1) % 2][:],
                                 xT_v[:, :, bass.ds((c + 2) * CH, CH)]).then_inc(x_loaded[cc % 2], 16)
                    sp.wait_ge(dist_done, W_EXPS + 8 * c)
                    stack_keys(c + 1, 0, (cc + 1) % 2)
            def stack_queries(c):
                if past_end(c):
                    return
                sp.wait_ge(qdist_done, PAIRS * c)
                for g, src, there in ((0, kh[0], qs_ready), (2, kh[0], qs_ready), (1, kl[0], ql_done)):
                    sp.wait_ge(there, 2 * (c + 1))
                    for j in range(4):
                        sp.dma_start(raw(pairs_of(q_stack, j)[32 * g:32 * g + 32]),
                                     raw(src[32 * j:32 * j + 32])).then_inc(q_stacked, 16)
                sp.wait_ge(qaug_done, c + 1)
                sp.dma_start(raw(q_stack[96:128]), rep(raw(augk[0][0:32, :]), 1, PAIRS)).then_inc(q_stacked, 16)

            sp.wait_ge(xl_ready, NCH + 3)
            sp.dma_start(x_raw[0][:], xT_v[:, :, 2 * CH:3 * CH]).then_inc(xq_loaded, 16)
            for sem_done, count in ((z_done, TPC * (NCH + 1)), (v_done, 2 * (NCH + 1)), (kl_done, 2 * (NCH + 2)),
                                    (aug_done, NCH + 2), (dist_done, W_EXPS + 8 * NCH), (k_stacked, K_STACKED * (NCH + 1))):
                sp.wait_ge(sem_done, count)
            sp.dma_start(x_tok[:], x_v[0]).then_inc(xt_loaded, 16)
            for i in range(2 * KC):
                k, half = i // 2, i % 2
                sp.dma_start(we_raw[i], we[k * P:(k + 1) * P, 1024 * half:1024 * (half + 1)]).then_inc(we_loaded, 16)
            stack_queries(0)
            sp.wait_ge(inv_done, 1)
            flat = winv_dram.rearrange("s k j -> s (k j)")
            sp.dma_start(flat[0:P], g_all).then_inc(winv_stored, 16)
            sp.dma_start(flat[P:P + H], g_all[0:H]).then_inc(winv_stored, 16)
            sp.wait_ge(winv_stored, 32)
            winv_b = winv_dram.rearrange("s k j -> k s j")
            sp.dma_start(winv_sb[:], winv_b[:, 0:H, :]).then_inc(winv_loaded, 16)
            stack_queries(1)
            sp.wait_ge(xql_ready, 3)
            sp.dma_start(x_raw[0][:], xT_v[:, :, 3 * CH:4 * CH]).then_inc(xq_loaded, 16)
            sp.wait_ge(h_done, 2 * TPC)
            sp.dma_start(x_tok[:], x_v[1]).then_inc(xt_loaded, 16)
            stack_queries(2)

            def turn(b):
                for cc in range(CPB):
                    p = b * CPB + cc
                    if cc == 0 and not past_end((b + 1) * CPB):
                        sp.wait_ge(y_done, b + 1)
                        sp.dma_start(winv_sb[:], winv_b[:, in_batch(b + 1, H), :]).then_inc(winv_loaded, 16)
                    if not past_end(p + 2):
                        sp.wait_ge(h_done, TPC * (p + 3))
                        sp.dma_start(x_tok[:], x_v[bass.ds(p + 2, 1)].rearrange("a p t d -> (a p) t d")).then_inc(xt_loaded, 16)
                    stack_queries(p + 3)
                    if not past_end(p + 4):
                        sp.wait_ge(xql_ready, p + 4)
                        sp.dma_start(x_raw[0][:], xT_v[:, :, bass.ds((p + 4) * CH, CH)]).then_inc(xq_loaded, 16)
                    for half in range(2):
                        sp.wait_ge(res_ready, TPC * p + 2 * half + 2)
                        sp.dma_start(out_v[bass.ds(p, 1), :, 2 * half:2 * half + 2].rearrange("a p t d -> (a p) t d"),
                                     y_out[:, 2 * half:2 * half + 2]).then_inc(res_stored, 16)

            with sp.Fori(0, BATCH - 1) as b:
                turn(b)
            turn(BATCH - 1)
            sp.wait_ge(res_stored, 32 * (NCH + 1))

        @block.gpsimd
        def _(pool):
            own = Steps(pool, pool_step)
            pool.wait_ge(idx_loaded, 32)
            nc.gpsimd.tensor_tensor(rows_sb[:], gbase_sb[:], idx_sb[:].broadcast_to([P, 4]), ALU.add).then_inc(rows_ready, 1)
            pool.wait_ge(rows_ready, 1)
            for i in range(4):
                nc.gpsimd.indirect_dma_start(
                    out=lm_x[:, i, :], out_offset=None, in_=x,
                    in_offset=bass.IndirectOffsetOnAxis(ap=rows_sb[:, i:i + 1].bitcast(u32), axis=0)).then_inc(gathered, 16)
            nc.gpsimd.memset(v_aug[0][:], 0.0)
            own.then(nc.gpsimd.memset(v_aug[1][:], 0.0))
            for i in range(2):
                last = nc.gpsimd.memset(v_aug[i][:, :, :, HD:HD + 1], 1.0)
            last.then_inc(const_set, 1)

            def block_lo(b, at):
                for s in range(KC):
                    last = nc.gpsimd.tensor_tensor(
                        bdl[at][:, s], rep(l2l[:, s, in_batch(b)], 1, HPS),
                        rep(cst[:, C_HEAD:C_HEAD + HPS], 2, NL), ALU.mult)
                return last

            pool.wait_ge(l2_ready, 1)
            pool.wait_ge(small_loaded, 16 * 9)
            for i, b in enumerate(W_ORDER):
                if i >= 2:
                    pool.wait_ge(dist_done, 2 * (i - 1))
                block_lo(b, b % 2).then_inc(bdl_ready, 1)
            def sweep(s):
                pool.wait_ge(sw_ready, s + 1)
                for n in (SWB - 3, SWB - 1, SWB - 2):
                    nc.gpsimd.tensor_tensor(block_row(t3, n), *outer(n), ALU.mult).then_inc(sw_prod, 1)
                pool.wait_ge(sw_prod, 3 * s + 3)
                nc.gpsimd.tensor_tensor(block_row(g3, SWB - 2), block_row(g3, SWB - 2), block_row(t3, SWB - 2),
                                        ALU.subtract).then_inc(sw_pool_done, 1)

            with pool.Fori(0, BATCH) as b:
                for cc in range(CPB):
                    c = b * CPB + cc
                    sweep(2 * c)
                    at = (cc + 1) % 2
                    pool.wait_ge(xh_ready, c + 4)
                    nc.gpsimd.tensor_tensor(xl[at][:], x_raw[at][:], raw(xh[at][:]), ALU.subtract).then_inc(xl_ready, 1)
                    sweep(2 * c + 1)

            def layernorm_coefs(mv, ve, rs, nt, nm, cols):
                own.then(nc.gpsimd.tensor_tensor(ve[:, cols], mv[:, cols, 1], cst[:, C_EPS:C_EPS + TPC][:, cols], ALU.add))
                own.then(nc.gpsimd.tensor_tensor(rs[:, cols], ve[:, cols], cst[:, C_EXP:C_EXP + TPC][:, cols], ALU.pow))
                own.then(nc.gpsimd.tensor_tensor(nt[:, cols], mv[:, cols, 0], rs[:, cols], ALU.mult))
                return nc.gpsimd.tensor_tensor(nm[:, cols], nt[:, cols], cst[:, C_MINUS:C_MINUS + TPC][:, cols], ALU.mult)

            def split_lo(c, at):
                if past_end(c):
                    return
                pool.wait_ge(xqh_ready, c + 1)
                nc.gpsimd.tensor_tensor(xl[at][:], x_raw[0][:], raw(xh[at][:]), ALU.subtract).then_inc(xql_ready, 1)

            def attn_lo(c, s):
                if past_end(c):
                    return
                pool.wait_ge(attnh_ready, 2 * c + s + 1)
                nc.gpsimd.tensor_tensor(attn_l[:, s], attn[:, s], raw(attn_h[:, s]), ALU.subtract).then_inc(attnl_ready, 1)

            def residual(c):
                if past_end(c):
                    return
                pool.wait_ge(xt_loaded, 16 * (c + 1))
                nc.gpsimd.tensor_tensor(x_tok[:], x_tok[:], rep(bo_sb[:], 1, TPC), ALU.add).then_inc(xb_ready, 1)

            def ln1(c):
                if past_end(c):
                    return
                pool.wait_ge(ln1_stats, c + 1)
                layernorm_coefs(mv1, ve1, rs1, nt1, nm1, slice(0, TPC)).then_inc(ln1_coef, 1)

            def sum_parts(p, t):
                pool.wait_ge(part_ready, 3 * (TPC * p + t) + 5)
                a = parts[t % 2]
                own.then(nc.gpsimd.tensor_tensor(a[0], a[0], a[1], ALU.add))
                own.then(nc.gpsimd.tensor_tensor(a[0], a[0], a[2], ALU.add))
                nc.gpsimd.tensor_tensor(a[0][:, 0:D], a[0][:, 0:D], a[0][:, D:2 * D], ALU.add).then_inc(part_sum, 1)

            def ln2(p, t):
                pool.wait_ge(ln2_stats, TPC * p + t + 1)
                layernorm_coefs(mv2, ve2, rs2, nt2, nm2, slice(t, t + 1)).then_inc(ln2_coef, 1)

            residual(0)
            split_lo(2, 1)
            attn_lo(0, 0)
            attn_lo(0, 1)
            ln1(0)
            residual(1)
            attn_lo(1, 0)
            attn_lo(1, 1)
            ln1(1)

            def turn(b):
                for cc in range(CPB):
                    p = b * CPB + cc
                    c, q = p + 1, p + 2
                    sum_parts(p, 0)
                    split_lo(q + 1, 1)
                    ln2(p, 0)
                    residual(q)
                    sum_parts(p, 1)
                    ln2(p, 1)
                    attn_lo(q, 0)
                    sum_parts(p, 2)
                    attn_lo(q, 1)
                    sum_parts(p, 3)
                    ln2(p, 2)
                    ln2(p, 3)
                    ln1(c + 1)

            with pool.Fori(0, BATCH - 1) as b:
                own.enter(b, CPB * (3 + 5 * TPC))
                turn(b)
                own.leave(BATCH - 1)
            turn(BATCH - 1)

        @block.scalar
        def _(act):
            def split_hi(at, ready):
                nc.scalar.activation(xh[at][:], x_raw[at][:], ACT.Copy).then_inc(ready, 1)

            act.wait_ge(small_loaded, 16 * 9)
            act.wait_ge(w_loaded, 64)
            nc.scalar.activation(wh[:], w_raw, ACT.Copy).then_inc(w_split_h, 1)
            for k in range(KC):
                act.wait_ge(lmT_done, k + 1)
                last = nc.scalar.activation(xh[0][:, k], bank[k][:], ACT.Copy)
            last.then_inc(xh_ready, 1)
            for s in range(KC):
                act.wait_ge(kproj_done, s + 1)
                nc.scalar.activation(kh[0][:, s], bank[2 + s][:], ACT.Identity, bias=bk_sb[:, s:s + 1])
                nc.scalar.activation(sq[:, s], bank[2 + s][:], ACT.Square, bias=bk_sb[:, s:s + 1]).then_inc(s_ready, 1)
            act.wait_ge(setup_done, 1)
            act.wait_ge(nl_done, 1)
            nc.scalar.activation(nlt[:, 0:BATCH, :].rearrange("p b i -> p (b i)"), bank[5][:, 0:BATCH * PAIRS], ACT.Copy,
                                 scale=invt[:]).then_inc(nl_ready, 1)
            act.wait_ge(nl_ready, 1)
            nc.scalar.activation(nlt[:, BATCH, :], nlt[:, 0, :], ACT.Copy).then_inc(nl_ready, 1)
            def exps(c, t):
                for s in range(KC):
                    n = 2 * t + s
                    act.wait_ge(dist_done, W_EXPS + 8 * c + n + 1)
                    if s == 0:
                        act.wait_ge(z_done, TPC * c + t + 1)
                    nc.scalar.activation(phi[:, n], bank[6 + s][:], ACT.Exp, scale=invt[:]).then_inc(exp_done, 1)

            def keys(c, at):
                for s in range(KC):
                    act.wait_ge(kproj_done, 2 * (c + 1) + s + 1)
                    if s == 0:
                        act.wait_ge(norm_done, c + 1)
                    nc.scalar.activation(kh[at][:, s], bank[2 + s][:], ACT.Identity, bias=bk_sb[:, s:s + 1])
                    nc.scalar.activation(sq[:, s], bank[2 + s][:], ACT.Square, bias=bk_sb[:, s:s + 1]).then_inc(s_ready, 1)

            act.wait_ge(x_loaded[0], 16)
            split_hi(1, xh_ready)
            act.wait_ge(kproj_done, 2)
            act.wait_ge(x_loaded[1], 16)
            split_hi(0, xh_ready)
            keys(0, 1)
            for i in range(BATCH):
                for s in range(KC):
                    act.wait_ge(dist_done, 2 * i + s + 1)
                    if i >= 2:
                        act.wait_ge(w_stored[i % 2], 16 * (i // 2))
                    nc.scalar.activation(wk_sb[i % 2][:, s].rearrange("p h k -> p (h k)"), bank[6 + s][0:64, :],
                                         ACT.Exp, scale=invt[0:64, :]).then_inc(exp_done, 1)
            act.wait_ge(dist_done, W_EXPS)
            act.wait_ge(l2_ready, 1)
            with act.Fori(0, BATCH) as b:
                for cc in range(CPB):
                    c = b * CPB + cc
                    exps(c, 0)
                    act.wait_ge(k_stacked, K_STACKED * (c + 1))
                    keys(c + 1, 0)
                    exps(c, 1)
                    act.wait_ge(x_loaded[cc % 2], 16 * (2 * b + cc // 2 + 2))
                    act.wait_ge(vproj_done, 2 * (c + 1))
                    split_hi((cc + 1) % 2, xh_ready)
                    act.wait_ge(norm_done, c + 3)
                    act.wait_ge(aug_done, c + 2)
                    nc.scalar.activation(aug_hi[:], bank[4][0:32, :], ACT.Copy).then_inc(aug_hi_ready, 1)
                    exps(c, 2)
                    exps(c, 3)
                    if cc == CPB - 1:
                        act.wait_ge(z_done, TPC * (c + 2))
                        nc.scalar.activation(zt[:, bass.ds(b, 1), :].rearrange("p a z -> p (a z)"),
                                             bank[5][:, 0:4 * NL], ACT.Copy).then_inc(zt_saved, 1)
            act.wait_ge(zt_saved, BATCH + 1)
            nc.scalar.activation(zt[:, BATCH, :], zt[:, 0, :], ACT.Copy).then_inc(zt_saved, 1)
            act.wait_ge(zt_saved, BATCH + 2)

            def z_of_batch(b):
                act.wait_ge(ztr_done, b)
                nc.scalar.activation(zt_cur[:], zt[:, bass.ds(b, 1), :].rearrange("p a z -> p (a z)"),
                                     ACT.Copy).then_inc(zt_cur_ready, 1)

            def norms_of_batch(b):
                nc.scalar.activation(nlt_cur[:], nlt[:, bass.ds(b, 1), :].rearrange("p a i -> p (a i)"),
                                     ACT.Copy).then_inc(nlt_ready, 1)
                act.wait_ge(nlt_ready, b + 1)

            def z_landmark_major(b):
                act.wait_ge(ztr_done, b + 1)
                act.wait_ge(y_done, b)
                nc.scalar.activation(zk[:], bank[5][0:64, :], ACT.Copy).then_inc(zk_ready, 1)

            def queries(c):
                if past_end(c):
                    return
                for s in range(KC):
                    act.wait_ge(qproj_done, 2 * c + s + 1)
                    if s == 0:
                        act.wait_ge(q_stacked, STACKED * c)
                        act.wait_ge(qnorm_done, c)
                    nc.scalar.activation(kh[0][:, s], bank[6 + s][:], ACT.Identity, bias=bq_sb[:, s:s + 1])
                    nc.scalar.activation(sq[:, s], bank[6 + s][:], ACT.Square, bias=bq_sb[:, s:s + 1]).then_inc(qs_ready, 1)

            def landmarks_of_batch(b, g):
                src = (l2h, l2h, l2l)[g]
                for j in range(4):
                    channels = slice(32 * j, 32 * j + 32)
                    for u in range(2):
                        own_head = cst[channels, C_HEAD + 2 * j + u:C_HEAD + 2 * j + u + 1]
                        last = nc.scalar.activation(pairs_of(l_stack, j, u)[32 * g:32 * g + 32], src[channels, :, in_batch(b)],
                                                    ACT.Copy, scale=own_head)
                last.then_inc(l_stacked, 1)

            def q_exps(c, pairs):
                if past_end(c):
                    return
                for i in pairs:
                    act.wait_ge(qdist_done, PAIRS * c + i + 1)
                    if i % 4 == 0:
                        act.wait_ge(out_done, 2 * c)
                    nc.scalar.activation(phi[:, i], bank[6 + i % 2][:], ACT.Exp,
                                         bias=nlt_cur[:, i:i + 1], scale=invt[:]).then_inc(qexp_done, 1)

            def attn_hi(c, s):
                if past_end(c):
                    return
                act.wait_ge(attn_ready, 2 * c + s + 1)
                act.wait_ge(wo_done, 2 * c)
                nc.scalar.activation(attn_h[:, s], attn[:, s], ACT.Copy).then_inc(attnh_ready, 1)

            def query_hi(c, at):
                if past_end(c):
                    return
                act.wait_ge(xq_loaded, 16 * (c - 1))
                act.wait_ge(qproj_done, 2 * c)
                nc.scalar.activation(xh[at][:], x_raw[0][:], ACT.Copy).then_inc(xqh_ready, 1)

            def normalise_rows(c, at):
                if past_end(c):
                    return
                act.wait_ge(ln1_coef, c + 1)
                for t in range(TPC):
                    nc.scalar.activation(x1[at][:, t], x1[at][:, t], ACT.Identity, bias=nm1[:, t:t + 1],
                                         scale=rs1[:, t:t + 1]).then_inc(x1_ready, 1)

            def x1_hi(c, at):
                if past_end(c):
                    return
                for tp in range(2):
                    act.wait_ge(x1t_done, 2 * c + tp + 1)
                    nc.scalar.activation(x1h[at][:, :, tp * 256:tp * 256 + 256].rearrange("p k (t j) -> p t k j", t=2),
                                         bank[tp][:].rearrange("p (t k j) -> p t k j", t=2, k=KC),
                                         ACT.Copy).then_inc(x1h_ready, 1)

            def gate_exp(c):
                if past_end(c):
                    return
                act.wait_ge(gd_ready, c + 1)
                nc.scalar.activation(ge[:], gd[:], ACT.Exp).then_inc(ge_ready, 1)

            def gates_T(c):
                if past_end(c):
                    return
                act.wait_ge(gtr_done, c + 1)
                nc.scalar.activation(g_t[:], bank[1][0:24, :], ACT.Copy).then_inc(gt_ready, 1)

            def weigh(p, n, at):
                if past_end(p):
                    return
                t, q = n // 4, n % 4
                act.wait_ge(ffn_done, 16 * p + n + 1)
                act.wait_ge(acc_done, TPC * p + t + 1)
                for u in range(2):
                    e = 2 * q + u
                    last = nc.scalar.activation(parts[t % 2][q - 1][:, u * D:(u + 1) * D],
                                                bank[2 + q % 2][:, u * D:(u + 1) * D],
                                                ACT.Copy, scale=gate[at][:, t, e:e + 1])
                last.then_inc(part_ready, 1)

            def result(p, t):
                act.wait_ge(ln2_coef, TPC * p + t + 1)
                nc.scalar.activation(y_out[:, t], y_out[:, t], ACT.Identity, bias=nm2[:, t:t + 1],
                                     scale=rs2[:, t:t + 1]).then_inc(res_ready, 1)

            act.wait_ge(vproj_done, 2 * (NCH + 1))
            act.wait_ge(v_done, 2 * (NCH + 1))
            act.wait_ge(norm_done, NCH + 2)
            z_of_batch(0)
            norms_of_batch(0)
            for sem_done, count in ((kl_done, 2 * (NCH + 2)), (aug_done, NCH + 2), (dist_done, W_EXPS + 8 * NCH),
                                    (bdl_ready, BATCH), (k_stacked, K_STACKED * (NCH + 1))):
                act.wait_ge(sem_done, count)
            queries(0)
            for g in range(3):
                landmarks_of_batch(0, g)
            z_landmark_major(0)
            q_exps(0, range(PAIRS))
            queries(1)
            query_hi(2, 1)
            act.wait_ge(winv_stored, 32)
            for i in range(2 * KC):
                act.wait_ge(we_loaded, 32 * KC)
                nc.scalar.activation(weh[:, i // 2, 1024 * (i % 2):1024 * (i % 2 + 1)], we_raw[i],
                                     ACT.Copy).then_inc(w_split_h, 1)
            attn_hi(0, 0)
            q_exps(1, range(0, 4))
            attn_hi(0, 1)
            q_exps(1, range(4, 8))
            normalise_rows(0, 0)
            x1_hi(0, 0)
            queries(2)
            attn_hi(1, 0)
            gate_exp(0)
            gates_T(0)
            attn_hi(1, 1)

            def first_tile(p, at, first=False, new_batch=None):
                q_exps(p + 2, range(0, 2))
                weigh(p, 1, at)
                weigh(p, 2, at)
                if new_batch is not None:
                    z_landmark_major(new_batch)
                if not first:
                    result(p - 1, 2)
                q_exps(p + 2, range(2, 4))
                weigh(p, 3, at)

            first_tile(0, 0, True)

            def turn(b):
                for cc in range(CPB):
                    p = b * CPB + cc
                    c, q = p + 1, p + 2
                    me, nxt = cc % 2, (cc + 1) % 2
                    q_exps(q, range(4, 6))
                    query_hi(q + 1, 1)
                    weigh(p, 5, me)
                    weigh(p, 6, me)
                    q_exps(q, range(6, 8))
                    normalise_rows(c, nxt)
                    weigh(p, 7, me)
                    x1_hi(c, nxt)
                    weigh(p, 9, me)
                    queries(q + 1)
                    weigh(p, 10, me)
                    attn_hi(q, 0)
                    if q_ends_batch(cc, b):
                        landmarks_of_batch(b + 1, 0)
                        landmarks_of_batch(b + 1, 1)
                    weigh(p, 11, me)
                    gate_exp(c)
                    result(p, 0)
                    if q_ends_batch(cc, b):
                        landmarks_of_batch(b + 1, 2)
                    weigh(p, 13, me)
                    gates_T(c)
                    if q_ends_batch(cc, b):
                        z_of_batch(b + 1)
                        norms_of_batch(b + 1)
                    weigh(p, 14, me)
                    result(p, 1)
                    weigh(p, 15, me)
                    attn_hi(q, 1)
                    first_tile(c, nxt, new_batch=b + 1 if q_ends_batch(cc, b) else None)
                    result(p, 3)

            with act.Fori(0, BATCH - 1) as b:
                turn(b)
            turn(BATCH - 1)

        @block.vector
        def _(dve):
            own = Steps(dve, dve_step)
            V = nc.vector
            V.memset(zero_c[:], 0.0)
            V.memset(raw(augk[0][:]), 1.0)
            V.memset(raw(augk[1][:]), 1.0)
            own.did(V.memset(minus1[:], -1.0))
            dve.wait_ge(small_loaded, 16 * 9)
            V.reciprocal(invt[:], temp_sb[:])
            own.then(V.tensor_scalar(tpos[:], temp_sb[:], 0.0, None, ALU.is_gt))
            own.then(V.tensor_scalar(phi_min[:], tpos[:], -1.0, 1.0, ALU.mult, ALU.add))
            V.scalar_tensor_tensor(phi_max[:], phi_min[:], BIG, tpos[:], ALU.mult, ALU.add)
            mask = cst[0:32, C_M16:C_M16 + H]
            for i in range(2):
                last = V.tensor_copy(augm[i][0:32], rep(mask.rearrange("p (s h) -> p s h", s=KC), 3, NL))
            V.tensor_copy(be_tmp[:], be_raw[:])
            own.then(V.tensor_copy(wg_s[:, :, 0:E], wg_raw[:]))
            V.tensor_tensor(wg_s[:, :, E:2 * E], wg_raw[:], raw(wg_s[:, :, 0:E]), ALU.subtract)
            V.scalar_tensor_tensor(be_s[:], raw(be_tmp[:]), cst[0:24, C_BES:C_BES + 1], be_raw[:], ALU.mult,
                                   ALU.add).then_inc(setup_done, 1)
            dve.wait_ge(w_split_h, 1)
            V.tensor_tensor(wl[:], w_raw, raw(wh[:]), ALU.subtract).then_inc(w_split_l, 1)
            dve.wait_ge(xh_ready, 1)
            for k in range(KC):
                last = V.tensor_tensor(xl[0][:, k], bank[k][:], raw(xh[0][:, k]), ALU.subtract)
            last.then_inc(xl_ready, 1)

            def project_lo(dst, hi, src, bias, s):
                return V.scalar_tensor_tensor(dst[:, s], src[:], bias[:, s:s + 1], raw(hi[:, s]), ALU.add, ALU.subtract)

            def norm_rows(dst, src):
                own.then(V.tensor_copy(aug_hi[:], src[0:32, :]))
                return norm_rows_lo(dst, src)

            def norm_rows_lo(dst, src):
                return V.scalar_tensor_tensor(dst, raw(aug_hi[:]), lo_sign[0:32, :], src[0:32, :], ALU.mult, ALU.add)

            for s in range(KC):
                dve.wait_ge(s_ready, s + 1)
                project_lo(kl[0], kh[0], bank[2 + s], bk_sb, s).then_inc(kl_done, 1)
            dve.wait_ge(kl_done, 2)
            V.tensor_scalar(l2h[:, :, 0:BATCH * NL], raw(kh[0][:]), 2.0, None, ALU.mult)
            V.tensor_scalar(l2l[:, :, 0:BATCH * NL], raw(kl[0][:]), 2.0, None, ALU.mult)
            V.tensor_scalar(l2h[:, :, BATCH * NL:], raw(kh[0][:, :, 0:NL]), 2.0, None, ALU.mult)
            V.tensor_scalar(l2l[:, :, BATCH * NL:], raw(kl[0][:, :, 0:NL]), 2.0, None, ALU.mult).then_inc(l2_ready, 1)
            dve.wait_ge(norm_done, 1)
            norm_rows(augk[0][0:32, :], bank[4]).then_inc(aug_done, 1)
            dve.wait_ge(aug_done, 1)
            V.tensor_copy(ln_rows[32:64, 0:BATCH * NL], raw(augk[0][0:32, :]))
            own.then(V.tensor_copy(ln_rows[32:64, BATCH * NL:], raw(augk[0][0:32, 0:NL])))

            def block_hi(b, at):
                for s in range(KC):
                    V.tensor_tensor(bdh[at][:, s], rep(l2h[:, s, in_batch(b)], 1, HPS),
                                    rep(cst[:, C_HEAD:C_HEAD + HPS], 2, NL), ALU.mult)
                    last = V.tensor_tensor(augm[at][32:64, s], rep(ln_rows[32:64, in_batch(b)], 1, HPS),
                                           rep(cst[32:64, C_M16 + HPS * s:C_M16 + HPS * (s + 1)], 2, NL), ALU.mult)
                return last

            def stack_landmarks(b):
                for j in range(2):
                    channels = slice(64 * j, 64 * j + 64)
                    own_head = rep(rep(cst[channels, C_HEAD + 4 * j:C_HEAD + 4 * j + 4], 1, KC), 3, NL)
                    for dst, src in ((l_hh[0:64], l2h), (l_hh[64:P], l2h), (l_lo[0:64], l2l)):
                        V.tensor_tensor(dst.rearrange("p (s j) u k -> p j s u k", s=KC)[:, j],
                                        rep(src[channels, :, in_batch(b)], 2, 4), own_head, ALU.mult)
                return V.tensor_tensor(l_lo[96:P].rearrange("p g u k -> p (g u) k"), rep(ln_rows[32:64, in_batch(b)], 1, H),
                                       rep(cst[32:64, C_M16:C_M16 + H], 2, NL), ALU.mult)

            def clamp(c, t):
                dve.wait_ge(exp_done, W_EXPS + 8 * c + 2 * t + 2)
                tile = phi[:, 2 * t:2 * t + 2].rearrange("p s n -> p (s n)")
                V.tensor_scalar(tile, tile, phi_max[:], phi_min[:], ALU.min, ALU.max).then_inc(phi_ready, 1)

            def keys_lo(c, at):
                for s in range(KC):
                    dve.wait_ge(s_ready, 2 * (c + 1) + s + 1)
                    project_lo(kl[at], kh[at], bank[2 + s], bk_sb, s).then_inc(kl_done, 1)

            def values(c, tp, at):
                dve.wait_ge(vproj_done, 2 * c + tp + 1)
                dve.wait_ge(z_done, TPC * c)
                V.tensor_tensor(v_aug[at][:, 2 * tp:2 * tp + 2, :, 0:HD],
                                bank[tp][:].rearrange("p (t h d) -> p t h d", t=2, h=H),
                                rep(bv_sb[:].rearrange("p (h d) -> p h d", h=H), 1, 2), ALU.add).then_inc(v_done, 1)

            def key_norms(c, at):
                if isinstance(c, int):
                    dve.wait_ge(norm_done, c + 2)
                    last = norm_rows(augk[at][0:32, :], bank[4])
                else:
                    dve.wait_ge(aug_hi_ready, c)
                    last = norm_rows_lo(augk[at][0:32, :], bank[4])
                last.then_inc(aug_done, 1)

            def split_lo(c, at):
                dve.wait_ge(xh_ready, c + 2)
                V.tensor_tensor(xl[at][:], x_raw[at][:], raw(xh[at][:]), ALU.subtract).then_inc(xl_ready, 1)

            def sweep_begin(s, blk):
                dve.wait_ge(sw_pool_done, s + 1)
                own.wait()
                at, kept = bass.ds(s, 1), (blk + 1) * SW
                row = g3[:, at, 0:kept].rearrange("p a c -> p (a c)")
                V.tensor_scalar(sw_v[:, 0:kept], row, 1.0, None, ALU.mult)
                if kept < NL:
                    V.tensor_scalar(sw_v[:, kept:], g3[:, kept:, at].rearrange("p r a -> p (r a)"), 1.0, None, ALU.mult)
                own.then(V.reciprocal(sw_p[:], g3[:, at, at].rearrange("p a c -> p (a c)")))
                own.then(V.tensor_scalar(sw_r[:], sw_v[:], sw_p[:], None, ALU.mult))
                V.tensor_scalar(sw_r[:, at], sw_p[:], -1.0, None, ALU.mult)
                V.tensor_copy(sw_v[:, at], minus1[:])
                own.then(V.tensor_scalar(g3[:, blk * SW:, at].rearrange("p r a -> p (r a)"), zero_c[:, blk * SW:], 1.0, None,
                                         ALU.mult))
                V.tensor_scalar(row, zero_c[:, 0:kept], 1.0, None, ALU.mult).then_inc(sw_ready, 1)

            def sweep_first_rows(s):
                dve.wait_ge(sw_ready, s + 1)
                for n in range(SWB - 3):
                    step = V.tensor_tensor(block_row(t3, n), *outer(n), ALU.mult)
                own.then(step)
                for n in range(SWB - 2):
                    if n == SWB - 3:
                        dve.wait_ge(sw_prod, 3 * s + 1)
                    step = V.tensor_tensor(block_row(g3, n), block_row(g3, n), block_row(t3, n), ALU.subtract)
                own.did(step)

            def sweep_last_row(s):
                dve.wait_ge(sw_prod, 3 * s + 2)
                own.did(V.tensor_tensor(block_row(g3, SWB - 1), block_row(g3, SWB - 1), block_row(t3, SWB - 1), ALU.subtract))

            dve.wait_ge(l2_ready, 1)
            for i, b in enumerate(W_ORDER):
                if i == 1:
                    dve.wait_ge(x_loaded[0], 16)
                    split_lo(0, 1)
                if i == 2:
                    keys_lo(0, 1)
                    dve.wait_ge(const_set, 1)
                    for tp in range(2):
                        values(0, tp, 0)
                    key_norms(0, 1)
                    dve.wait_ge(x_loaded[1], 16)
                    split_lo(1, 0)
                if i >= 2:
                    dve.wait_ge(dist_done, 2 * (i - 1))
                block_hi(b, b % 2).then_inc(bd_ready, 1)
            V.tensor_copy(l_lo[64:96].rearrange("p g u k -> p (g u) k"), rep(cst[64:96, C_M16:C_M16 + H], 2, NL))
            stack_landmarks(0).then_inc(bd_ready, 1)
            dve.wait_ge(g_loaded, 16)
            own.then(V.tensor_scalar(g_all, g_all, phi_max[:], phi_min[:], ALU.min, ALU.max))
            own.did(V.tensor_scalar(g_all[:, 0:NL * NL:NL + 1], g_all[:, 0:NL * NL:NL + 1], REG, None, ALU.add))
            for blk in range(SWB):
                with dve.Fori(0, BATCH // SWB) as turn:
                    own.enter(turn, CPB * 2 * (3 + 3))
                    b = turn + blk * (BATCH // SWB)
                    for cc in range(CPB):
                        c = b * CPB + cc
                        if cc:
                            clamp(c, 0)
                        sweep_begin(2 * c, blk)
                        if cc == 0:
                            clamp(c, 0)
                        sweep_first_rows(2 * c)
                        keys_lo(c + 1, 0)
                        clamp(c, 1)
                        values(c + 1, 0, (cc + 1) % 2)
                        key_norms(c + 1, 0)
                        sweep_last_row(2 * c)
                        clamp(c, 2)
                        sweep_begin(2 * c + 1, blk)
                        values(c + 1, 1, (cc + 1) % 2)
                        clamp(c, 3)
                        sweep_first_rows(2 * c + 1)
                        if cc == CPB - 1:
                            dve.wait_ge(dist_done, W_EXPS + 8 * (c + 1))
                            stack_landmarks(b + 1).then_inc(bd_ready, 1)
                        sweep_last_row(2 * c + 1)
                    own.leave(BATCH // SWB)
            own.wait()
            dve.wait_ge(sw_pool_done, NL + 1)
            for n in range(1, SWB):
                for m in range(n):
                    step = V.tensor_copy(g3[:, m * SW:(m + 1) * SW, n * SW:(n + 1) * SW],
                                         g3[:, n * SW:(n + 1) * SW, m * SW:(m + 1) * SW].rearrange("p r c -> p c r"))
            step.then_inc(inv_done, 1)

            def queries_lo(c):
                if past_end(c):
                    return
                for s in range(KC):
                    dve.wait_ge(qs_ready, 2 * c + s + 1)
                    project_lo(kl[0], kh[0], bank[6 + s], bq_sb, s).then_inc(ql_done, 1)

            def query_norms(c):
                if past_end(c):
                    return
                dve.wait_ge(qnorm_done, c + 1)
                norm_rows(augk[0][0:32, :], bank[6]).then_inc(qaug_done, 1)

            def q_clamp(c, pairs):
                if past_end(c):
                    return
                for i in pairs[::2]:
                    dve.wait_ge(qexp_done, PAIRS * (c + 1) + i + 2)
                    two = phi[:, i:i + 2].rearrange("p i n -> p (i n)")
                    V.tensor_scalar(two, two, phi_max[:], phi_min[:], ALU.min, ALU.max).then_inc(qphi_ready, 2)

            def landmark_values(b):
                dve.wait_ge(y_done, b + 1)
                y = bank[4][:, 0:PAIRS * 32].rearrange("p (i c) -> p i c", i=PAIRS)
                for u in range(2):
                    half = slice(64 * u, 64 * u + 64)
                    V.tensor_scalar(y_cur[half, :, 16 * u:16 * u + 16], y[half, :, 0:HD], -1.0, None, ALU.mult)
                    last = V.tensor_scalar(y_cur[half, :, 32 + 16 * u:48 + 16 * u],
                                           y[half, :, HD:HD + 1].broadcast_to([64, PAIRS, HD]), -1.0, None, ALU.mult)
                last.then_inc(y_ready, 1)

            def norm_begin(c, s, at=4):
                if past_end(c):
                    return
                dve.wait_ge(out_done, 2 * c + s + 1)
                dve.wait_ge(attn_ready, 2 * c + s)
                own.then(V.tensor_scalar(nrm[:], bank[at + 1][:], NORM_MIN, None, ALU.max))
                own.did(V.reciprocal(nrm[:, 0:CH // 2], nrm[:, 0:CH // 2]))

            def norm_end(c, s, at=4):
                if past_end(c):
                    return
                own.then(V.reciprocal(nrm[:, CH // 2:], nrm[:, CH // 2:]))
                if not isinstance(c, int) or c >= 2:
                    dve.wait_ge(attnl_ready, 2 * c + s - 1)
                V.tensor_tensor(attn[:, s], bank[at][:], nrm[:], ALU.mult).then_inc(attn_ready, 1)

            def residual_stats(c, at):
                if past_end(c):
                    return
                dve.wait_ge(xb_ready, c + 1)
                for t in range(TPC):
                    if t % 2 == 0:
                        dve.wait_ge(wo_done, 2 * c + t // 2 + 1)
                    V.tensor_tensor(x1[at][:, t], bank[t // 2][:, 256 * (t % 2):256 * (t % 2) + 256], x_tok[:, t],
                                    ALU.add).then_inc(h_done, 1)
                dve.wait_ge(h_done, TPC * (c + 2))
                for t in range(TPC):
                    step = V.bn_stats(st1[:, t], x1[at][:, t])
                own.then(step)
                dve.sem_inc(dve_waited, 1)
                for t in range(TPC):
                    step = V.bn_aggr(mv1[:, t], st1[:, t])
                step.then_inc(ln1_stats, 1)

            def x1_lo(c, at):
                if past_end(c):
                    return
                for tp in range(2):
                    dve.wait_ge(x1h_ready, 2 * c + tp + 1)
                    V.tensor_tensor(x1l[at][:, :, tp * 256:tp * 256 + 256].rearrange("p k (t j) -> p t k j", t=2),
                                    bank[tp][:].rearrange("p (t k j) -> p t k j", t=2, k=KC),
                                    raw(x1h[at][:, :, tp * 256:tp * 256 + 256]).rearrange("p k (t j) -> p t k j", t=2),
                                    ALU.subtract).then_inc(x1l_ready, 1)

            def gates_begin(p):
                if past_end(p):
                    return
                dve.wait_ge(gate_done, p + 1)
                logit = bank[0][:, 0:TPC * 2 * E].rearrange("p (t e) -> p t e", t=TPC)
                own.then(V.tensor_tensor(lg0[:], logit[:, :, 0:E], rep(bg_sb[:], 1, TPC), ALU.add))
                V.tensor_tensor(lg[:], logit[:, :, E:2 * E], lg0[:], ALU.add).then_inc(gate_read, 1)
                dve.wait_ge(gate_read, p + 1)
                dve.sem_inc(dve_waited, 1)
                for t in range(TPC):
                    step = V.max(m8[:, t], lg[:, t])
                own.then(step)
                V.tensor_tensor(gd[:], m8[:, :, 1], m8[:, :, 0], ALU.subtract).then_inc(gd_ready, 1)
                for t in range(TPC):
                    step = V.max_index(i8[:, t], m8[:, t], lg[:, t])
                own.then(step)
                own.then(V.tensor_copy(if2[:], i8[:, :, 0:2]))
                iota = rep(cst[:, C_IOTA:C_IOTA + E], 1, TPC)
                V.tensor_tensor(oh1[:], iota, rep(if2[:, :, 0], 2, E), ALU.is_equal)
                V.tensor_tensor(oh2[:], iota, rep(if2[:, :, 1], 2, E), ALU.is_equal)

            def gates_end(p, at):
                if past_end(p):
                    return
                dve.wait_ge(ge_ready, p + 1)
                own.then(V.tensor_scalar(gs[:], ge[:], 1.0, None, ALU.add))
                own.then(V.reciprocal(gw1[:], gs[:]))
                own.then(V.tensor_tensor(gw2[:], gw1[:], ge[:], ALU.mult))
                V.tensor_tensor(oh1[:], oh1[:], rep(gw1[:], 2, E), ALU.mult)
                own.then(V.tensor_tensor(oh2[:], oh2[:], rep(gw2[:], 2, E), ALU.mult))
                own.then(V.tensor_tensor(gate[at][:], oh1[:], oh2[:], ALU.add))
                own.then(V.tensor_copy(gate_h[:], gate[at][:]))
                V.tensor_copy(g_st[:, :, 0:E], raw(gate_h[:]))
                V.tensor_tensor(g_st[:, :, E:2 * E], gate[at][:], raw(gate_h[:]), ALU.subtract)
                V.tensor_copy(g_st[:, :, 2 * E:3 * E], raw(gate_h[:])).then_inc(gst_ready, 1)
                dve.wait_ge(gst_ready, p + 1)

            def add_bias(p, at):
                if past_end(p):
                    return
                for t in range(TPC):
                    if t % 2 == 0:
                        dve.wait_ge(be_done, 2 * p + t // 2 + 1)
                    step = V.tensor_tensor(x1[at][:, t], bank[t // 2][:, 256 * (t % 2):256 * (t % 2) + 256],
                                           x1[at][:, t], ALU.add)
                step.then_inc(be_added, 1)

            def combine(p, t, at):
                if past_end(p):
                    return
                dve.wait_ge(ffn_done, 16 * p + 4 * t + 1)
                dve.wait_ge(be_added, p + 1)
                dve.wait_ge(res_stored, 32 * p + 16 * (t // 2) + 16)
                a = y_out[:, t]
                own.then(V.scalar_tensor_tensor(a, bank[2][:, 0:D], gate[at][:, t, 0:1], x1[at][:, t], ALU.mult, ALU.add))
                V.scalar_tensor_tensor(a, bank[2][:, D:2 * D], gate[at][:, t, 1:2], a, ALU.mult, ALU.add).then_inc(comb_done, 1)

            def finish(p, t):
                dve.wait_ge(part_sum, TPC * p + t + 1)
                dve.wait_ge(comb_done, TPC * p + t + 2)
                V.tensor_tensor(y_out[:, t], y_out[:, t], parts[t % 2][0][:, 0:D], ALU.add).then_inc(acc_done, 1)
                dve.wait_ge(acc_done, TPC * p + t + 3)
                own.then(V.bn_stats(st2[:, t], y_out[:, t]))
                dve.sem_inc(dve_waited, 1)
                V.bn_aggr(mv2[:, t], st2[:, t]).then_inc(ln2_stats, 1)

            for sem_done, count in ((v_done, 2 * (NCH + 1)), (kl_done, 2 * (NCH + 2)), (aug_done, NCH + 2),
                                    (dist_done, W_EXPS + 8 * NCH), (k_stacked, K_STACKED * (NCH + 1)),
                                    (bdl_ready, BATCH), (inv_done, 1), (z_done, TPC * (NCH + 1))):
                dve.wait_ge(sem_done, count)
            queries_lo(0)
            V.tensor_copy(l_stack[96:128], rep(cst[96:128, C_M16:C_M16 + H].rearrange("p (i u) -> p i u", u=2), 3, NL)
                          ).then_inc(l_stacked, 1)
            query_norms(0)
            own.then(V.memset(y_cur[:], 0.0))
            q_clamp(0, range(PAIRS))
            queries_lo(1)
            landmark_values(0)
            query_norms(1)
            norm_begin(0, 0)
            norm_end(0, 0)
            norm_begin(0, 1, 2)
            norm_end(0, 1, 2)
            dve.wait_ge(winv_stored, 32)
            for i in range(2 * KC):
                dve.wait_ge(w_split_h, i + 2)
                k, half = i // 2, slice(1024 * (i % 2), 1024 * (i % 2 + 1))
                V.tensor_tensor(wel[:, k, half], we_raw[i], raw(weh[:, k, half]), ALU.subtract).then_inc(w_split_l, 1)
            dve.wait_ge(w_split_l, 1 + 2 * KC)
            q_clamp(1, range(0, 4))
            residual_stats(0, 0)
            q_clamp(1, range(4, 8))
            norm_begin(1, 0)
            x1_lo(0, 0)
            norm_end(1, 0)
            gates_begin(0)
            queries_lo(2)
            gates_end(0, 0)
            query_norms(2)
            norm_begin(1, 1)
            norm_end(1, 1)

            def first_tile(p, at, first=False):
                add_bias(p, at)
                if not first:
                    finish(p - 1, 2)
                combine(p, 0, at)
                if not first:
                    finish(p - 1, 3)
                residual_stats(p + 1, 1 - at)
                combine(p, 1, at)
                q_clamp(p + 2, range(0, 2))

            first_tile(0, 0, True)

            def turn(b):
                for cc in range(CPB):
                    p = b * CPB + cc
                    c, q = p + 1, p + 2
                    me, nxt = cc % 2, (cc + 1) % 2
                    q_clamp(q, range(2, 4))
                    q_clamp(q, range(4, 6))
                    norm_begin(q, 0)
                    finish(p, 0)
                    q_clamp(q, range(6, 8))
                    combine(p, 2, me)
                    norm_end(q, 0)
                    x1_lo(c, nxt)
                    queries_lo(q + 1)
                    norm_begin(q, 1)
                    finish(p, 1)
                    gates_begin(c)
                    combine(p, 3, me)
                    gates_end(c, nxt)
                    query_norms(q + 1)
                    norm_end(q, 1)
                    first_tile(c, nxt)
                    if q_ends_batch(cc, b):
                        landmark_values(b + 1)

            with dve.Fori(0, BATCH - 1) as b:
                own.enter(b, CPB * (2 * 3 + 1 + 11 + TPC + TPC))
                turn(b)
                own.leave(BATCH - 1)
            turn(BATCH - 1)

        @block.tensor
        def _(pe):
            mm = nc.tensor.matmul
            WK, WV, WQ, WO = range(4)

            def project_T(w, at, s, dst):
                cols = slice(s * P, (s + 1) * P)
                for k in range(KC):
                    last = product3(dst, wh[:, w, k, cols], wl[:, w, k, cols], xh[at][:, k], xl[at][:, k],
                                    k == 0, k == KC - 1)
                return last

            def square_norms(dst):
                for s in range(KC):
                    last = mm(dst[0:32, :], neg_block[:, s, :], sq[:, s], start=(s == 0), stop=(s == KC - 1))
                return last

            pe.wait_ge(small_loaded, 16 * 9)
            pe.wait_ge(gathered, 64)
            for k in range(KC):
                for i in range(4):
                    last = nc.tensor.transpose(bank[k][:, i * P:(i + 1) * P], lm_x[:, i, k * P:(k + 1) * P], ident)
                last.then_inc(lmT_done, 1)
            pe.wait_ge(w_split_l, 1)
            pe.wait_ge(xl_ready, 1)
            for s in range(KC):
                project_T(WK, 0, s, bank[2 + s][:]).then_inc(kproj_done, 1)
            pe.wait_ge(s_ready, 2)
            square_norms(bank[4]).then_inc(norm_done, 1)
            for b in range(BATCH):
                for s in range(KC):
                    for u in range(2):
                        at = b * PAIRS + s * 4
                        last = mm(bank[5][64 * u:64 * u + 64, at:at + 4], sq[:, s, b * NL:(b + 1) * NL],
                                  neg_sel[:, u, :], start=True, stop=True)
            last.then_inc(nl_done, 1)
            pe.wait_ge(aug_done, 1)
            pe.wait_ge(setup_done, 1)

            def key_dists(dst, at, tok, bd, s):
                wide = lambda a: a.rearrange("p h k -> p (h k)")
                mm(dst, kh[at][:, s, tok], wide(bdh[bd][:, s]), start=True, stop=False)
                mm(dst, kl[at][:, s, tok], wide(bdh[bd][:, s]), start=False, stop=False)
                mm(dst, kh[at][:, s, tok], wide(bdl[bd][:, s]), start=False, stop=False)
                return mm(dst, augk[at][:, tok], wide(augm[bd][:, s]), start=False, stop=True)

            def keys(c, at):
                pe.wait_ge(xh_ready, c + 2)
                pe.wait_ge(xl_ready, c + 2)
                pe.wait_ge(kl_done, 2 * (c + 1))
                for s in range(KC):
                    project_T(WK, at, s, bank[2 + s][:]).then_inc(kproj_done, 1)

            def values(c, tp, at):
                if isinstance(c, int):
                    pe.wait_ge(xl_ready, 1)
                else:
                    pe.wait_ge(v_done, 2 * c + tp - 1)
                for t in (2 * tp, 2 * tp + 1):
                    tok = slice(t * P, (t + 1) * P)
                    dst = bank[tp][:, 256 * (t % 2):256 * (t % 2) + 256]
                    for k in range(KC):
                        last = product3(dst, xh[at][:, k, tok], xl[at][:, k, tok], wh[:, WV, k], wl[:, WV, k],
                                        k == 0, k == KC - 1)
                last.then_inc(vproj_done, 1)

            def key_norms(c):
                pe.wait_ge(s_ready, 2 * (c + 2))
                pe.wait_ge(aug_done, c + 1)
                square_norms(bank[4]).then_inc(norm_done, 1)

            def dists(c, t, at):
                tok = slice(t * P, (t + 1) * P)
                if t == 0:
                    pe.wait_ge(k_stacked, K_STACKED * (c + 1))
                for s in range(KC):
                    pe.wait_ge(exp_done, W_EXPS + 8 * c + 2 * t + s - 1)
                    for g in (2 * s, 2 * s + 1):
                        dst = bank[6 + s][:, 256 * (g % 2):256 * (g % 2) + 256]
                        wide = lambda a: a[:, g].rearrange("p u k -> p (u k)")
                        mm(dst, k_hl[at][:, g, tok], wide(l_hh), start=True, stop=False)
                        last = mm(dst, k_ha[at][:, g, tok], wide(l_lo), start=False, stop=True)
                    last.then_inc(dist_done, 1)

            def sums(c, t, at, first, last_tile):
                pe.wait_ge(phi_ready, TPC * c + t + 1)
                for g in range(4):
                    for j in range(4):
                        head = 4 * g + j
                        s, hs = head // HPS, head % HPS
                        last = mm(bank[5][32 * j:32 * j + 32, g * NL:(g + 1) * NL], v_aug[at][:, t, head, :],
                                  phi[:, 2 * t + s, hs * NL:(hs + 1) * NL], start=(first and g == 0), stop=last_tile,
                                  skip_group_check=True)
                last.then_inc(z_done, 1)

            keys(0, 1)
            for tp in range(2):
                values(0, tp, 1)
            key_norms(0)
            for i, b in enumerate(W_ORDER):
                pe.wait_ge(bd_ready, i + 1)
                pe.wait_ge(bdl_ready, i + 1)
                for s in range(KC):
                    if i:
                        pe.wait_ge(exp_done, 2 * i + s - 1)
                    key_dists(bank[6 + s][0:64, :], 0, slice(b * NL, (b + 1) * NL), b % 2, s).then_inc(dist_done, 1)
            pe.wait_ge(nl_ready, 1)
            with pe.Fori(0, BATCH) as b:
                for cc in range(CPB):
                    c = b * CPB + cc
                    nxt = cc % 2
                    if cc == 0:
                        keys(c + 1, nxt)
                        pe.wait_ge(bd_ready, BATCH + 1 + b)
                        dists(c, 0, cc % 2)
                    else:
                        keys(c + 1, nxt)
                    dists(c, 1, cc % 2)
                    if cc == 0:
                        pe.wait_ge(zt_saved, b + 1)
                    pe.wait_ge(v_done, 2 * (c + 1))
                    sums(c, 0, cc % 2, cc == 0, False)
                    values(c + 1, 0, nxt)
                    key_norms(c + 1)
                    dists(c, 2, cc % 2)
                    sums(c, 1, cc % 2, False, False)
                    values(c + 1, 1, nxt)
                    dists(c, 3, cc % 2)
                    sums(c, 2, cc % 2, False, False)
                    if cc < CPB - 1:
                        dists(c + 1, 0, (cc + 1) % 2)
                    sums(c, 3, cc % 2, False, cc == CPB - 1)

            def queries(c, at):
                if past_end(c):
                    return
                pe.wait_ge(xqh_ready, c + 1)
                pe.wait_ge(xql_ready, c + 1)
                for s in range(KC):
                    pe.wait_ge(qexp_done, PAIRS * c + s + 7)
                    project_T(WQ, at, s, bank[6 + s][:]).then_inc(qproj_done, 1)

            def query_norms(c):
                if past_end(c):
                    return
                pe.wait_ge(ql_done, 2 * (c + 1))
                square_norms(bank[6]).then_inc(qnorm_done, 1)

            def query_dists(c, pairs):
                if past_end(c):
                    return
                for i in pairs:
                    if i == 0:
                        pe.wait_ge(q_stacked, STACKED * (c + 1))
                    pe.wait_ge(qexp_done, PAIRS * c + i + 7)
                    mm(bank[6 + i % 2][:], l_stack[:, i].rearrange("p u k -> p (u k)"), q_stack[:, i],
                       start=True, stop=True).then_inc(qdist_done, 1)

            def z_transposes(b):
                pe.wait_ge(zt_cur_ready, b + 1)
                pe.sem_inc(pe_waited, 1)
                for g in range(4):
                    last = nc.tensor.transpose(bank[5][0:64, g * P:(g + 1) * P], zt_cur[:, g * NL:(g + 1) * NL], ident)
                last.then_inc(ztr_done, 1)

            def landmark_solve(b):
                pe.wait_ge(zk_ready, b + 1)
                pe.wait_ge(winv_loaded, 16 * (b + 1))
                pe.sem_inc(pe_waited, 1)
                for head in range(H):
                    u, i = head % 2, head // 2
                    last = mm(bank[4][64 * u:64 * u + 64, 32 * i:32 * i + 32], winv_sb[:, head, :],
                              zk[:, 32 * head:32 * head + 32], start=True, stop=True)
                last.then_inc(y_done, 1)

            def attention(c, half, at=4):
                if past_end(c):
                    return
                pe.wait_ge(qphi_ready, PAIRS * c + 4 * half + 4)
                if at == 4:
                    pe.wait_ge(attn_ready, 2 * c + half)
                for n, dst in ((0, bank[at]), (32, bank[at + 1])):
                    for j in range(4):
                        last = mm(dst[32 * j:32 * j + 32, :], y_cur[:, 4 * half + j, n:n + 32], phi[:, 4 * half + j],
                                  start=True, stop=True)
                last.then_inc(out_done, 1)

            def output_projection(p):
                if past_end(p):
                    return
                pe.wait_ge(attnl_ready, 2 * (p + 1))
                pe.wait_ge(be_added, p)
                for tp in range(2):
                    for t in (2 * tp, 2 * tp + 1):
                        tok = slice(t * P, (t + 1) * P)
                        dst = bank[tp][:, 256 * (t % 2):256 * (t % 2) + 256]
                        for k in range(KC):
                            last = product3(dst, attn_h[:, k, tok], attn_l[:, k, tok], wh[:, WO, k], wl[:, WO, k],
                                            k == 0, k == KC - 1)
                    last.then_inc(wo_done, 1)

            def x1_transposes(p, at_x):
                if past_end(p):
                    return
                for tp in range(2):
                    pe.wait_ge(x1_ready, TPC * (p + 1) + 2 * tp + 2)
                    for t in (2 * tp, 2 * tp + 1):
                        for k in range(KC):
                            at = 256 * (t % 2) + 128 * k
                            last = nc.tensor.transpose(bank[tp][:, at:at + P], x1[at_x][:, t, k * P:(k + 1) * P], ident)
                    last.then_inc(x1t_done, 1)

            def gate_logits(p, at):
                if past_end(p):
                    return
                pe.wait_ge(x1l_ready, 2 * (p + 1))
                for t in range(TPC):
                    tok = slice(t * P, (t + 1) * P)
                    for k in range(KC):
                        for u, a in enumerate((x1h[at], x1l[at])):
                            last = mm(bank[0][:, 16 * t:16 * t + 16], a[:, k, tok], wg_s[:, k],
                                      start=(k == 0 and u == 0), stop=(k == KC - 1 and u == 1))
                last.then_inc(gate_done, 1)

            def gate_transposes(p):
                if past_end(p):
                    return
                pe.wait_ge(gst_ready, p + 1)
                for t in range(TPC):
                    last = nc.tensor.transpose(bank[1][0:24, t * P:(t + 1) * P], g_st[:, t], ident)
                last.then_inc(gtr_done, 1)

            def bias_term(p):
                if past_end(p):
                    return
                pe.wait_ge(gt_ready, p + 1)
                pe.wait_ge(gate_read, p + 1)
                for tp in range(2):
                    for t in (2 * tp, 2 * tp + 1):
                        last = mm(bank[tp][:, 256 * (t % 2):256 * (t % 2) + 256], g_t[:, t * P:(t + 1) * P], be_s[:],
                                  start=True, stop=True)
                    last.then_inc(be_done, 1)

            def experts(p, n, at):
                if past_end(p):
                    return
                t, q = n // 4, n % 4
                tok = slice(t * P, (t + 1) * P)
                if q == 2:
                    pe.wait_ge(comb_done, TPC * p + t + 2)
                else:
                    pe.wait_ge(part_ready, 3 * (TPC * p + t) + (1, 2, 0, 3)[q])
                cols = slice(512 * q, 512 * (q + 1))
                for k in range(KC):
                    last = product3(bank[2 + n % 2][:], x1h[at][:, k, tok], x1l[at][:, k, tok], weh[:, k, cols],
                                    wel[:, k, cols], k == 0, k == KC - 1)
                last.then_inc(ffn_done, 1)

            pe.wait_ge(exp_done, W_EXPS + 8 * NCH)
            pe.wait_ge(kl_done, 2 * (NCH + 2))
            pe.wait_ge(v_done, 2 * (NCH + 1))
            pe.wait_ge(aug_done, NCH + 2)
            pe.wait_ge(zt_saved, BATCH + 1)
            pe.wait_ge(xl_ready, NCH + 3)
            queries(0, 1)
            z_transposes(0)
            query_norms(0)
            pe.wait_ge(l_stacked, 4)
            query_dists(0, range(PAIRS))
            queries(1, 0)
            landmark_solve(0)
            query_norms(1)
            pe.wait_ge(y_ready, 1)
            attention(0, 0)
            attention(0, 1, 2)
            query_dists(1, range(PAIRS))
            output_projection(0)
            attention(1, 0)
            queries(2, 1)
            x1_transposes(0, 0)
            gate_logits(0, 0)
            attention(1, 1)
            query_norms(2)
            gate_transposes(0)
            pe.wait_ge(w_split_l, 1 + 2 * KC)

            def first_tile(p, at, new_batch=None):
                experts(p, 0, at)
                if new_batch is not None:
                    pe.wait_ge(l_stacked, 3 * new_batch + 4)
                experts(p, 1, at)
                query_dists(p + 2, range(0, 2))
                if new_batch is not None:
                    pe.wait_ge(attn_ready, 2 * (p + 2))
                    z_transposes(new_batch)
                output_projection(p + 1)
                experts(p, 2, at)
                query_dists(p + 2, range(2, 4))
                experts(p, 3, at)
                if new_batch is not None:
                    landmark_solve(new_batch)
                experts(p, 4, at)

            bias_term(0)
            first_tile(0, 0)

            def turn(b):
                for cc in range(CPB):
                    p = b * CPB + cc
                    c, q = p + 1, p + 2
                    me, nxt = cc % 2, (cc + 1) % 2
                    query_dists(q, range(4, 6))
                    experts(p, 5, me)
                    experts(p, 6, me)
                    query_dists(q, range(6, 8))
                    if q_starts_batch(cc, b):
                        pe.wait_ge(y_ready, b + 2)
                    attention(q, 0)
                    experts(p, 7, me)
                    experts(p, 8, me)
                    x1_transposes(c, nxt)
                    experts(p, 9, me)
                    queries(q + 1, 1)
                    experts(p, 10, me)
                    attention(q, 1)
                    gate_logits(c, nxt)
                    experts(p, 11, me)
                    experts(p, 12, me)
                    query_norms(q + 1)
                    experts(p, 13, me)
                    experts(p, 14, me)
                    gate_transposes(c)
                    experts(p, 15, me)
                    bias_term(c)
                    first_tile(c, nxt, b + 1 if q_ends_batch(cc, b) else None)

            with pe.Fori(0, BATCH - 1) as b:
                turn(b)
            turn(BATCH - 1)


def shape_constants():
    import numpy as np
    c = np.zeros((P, C_END), np.float32)
    part = np.arange(P)
    c[:, C_ID:C_ID + P] = np.eye(P)
    c[:, C_HEAD:C_HEAD + HPS] = part[:, None] // HD == np.arange(HPS)
    for s in range(KC):
        c[:, C_NEG + 32 * s:C_NEG + 32 * (s + 1)] = -(np.arange(32) % H == (HPS * s + part // HD)[:, None]).astype(np.float32)
    c[:, C_LO] = -(part % 32 >= 16).astype(np.float32)
    c[:, C_M16:C_M16 + H] = part[:, None] % 16 == np.arange(H)
    for u in range(2):
        c[:, C_NSEL + 4 * u:C_NSEL + 4 * (u + 1)] = -(part[:, None] // HD == 2 * np.arange(4) + u).astype(np.float32)
    c[:, C_IOTA:C_IOTA + E] = np.arange(E)
    c[:, C_EXP:C_EXP + TPC] = -0.5
    c[16:24, C_BES] = -1.0
    c[:, C_EPS:C_EPS + TPC] = EPS
    c[:, C_MINUS:C_MINUS + TPC] = -1.0
    return c


def kernel(**inputs):
    import numpy as np
    import concourse.bacc as bacc
    from concourse.bass_utils import run_bass_kernel_spmd

    a = {k: np.asarray(v) for k, v in inputs.items()}
    rows = a["L0_attn_query"].reshape(T, D)
    x = np.concatenate([rows, rows[:2 * CH]])
    x_t = np.ascontiguousarray(np.concatenate([rows, rows[:AHEAD * CH]]).T)

    def columns(v):
        return np.ascontiguousarray(v.reshape(KC, P).T)

    def every_partition(v):
        return np.ascontiguousarray(np.broadcast_to(v.reshape(1, -1), (P, v.size)))

    first_row = (2 * np.arange(4)[None, :] + np.arange(P)[:, None] // NL) * SEQ
    arrays = {
        "xT": x_t, "x": x,
        "wq": a["L0_attn_Wq"].T, "wk": a["L0_attn_Wk"].T, "wv": a["L0_attn_Wv"].T, "wo": a["L0_attn_Wo"].T,
        "we": a["L0_ffn_We"].transpose(2, 0, 1).reshape(D, E * D), "wg": a["L0_ffn_Wg"].T,
        "bq": columns(a["L0_attn_bq"]), "bk": columns(a["L0_attn_bk"]),
        "bv": every_partition(a["L0_attn_bv"]), "bo": every_partition(a["L0_attn_bo"]),
        "be3": np.tile(a["L0_ffn_be"], (3, 1)), "bg": every_partition(a["L0_ffn_bg"]),
        "temp": every_partition(a["L0_attn_temperature"]),
        "idx": np.tile(a["L0_attn_landmark_idx"], 2).reshape(P, 1),
        "gbase": first_row.astype(np.int32), "consts": shape_constants(),
    }
    nc = bacc.Bacc("TRN2", target_bir_lowering=False, num_devices=1)
    arrays = {f"in_{k}": np.ascontiguousarray(v) for k, v in arrays.items()}
    args = [nc.dram_tensor(k, v.shape, mybir.dt.from_np(v.dtype), kind="ExternalInput").ap() for k, v in arrays.items()]
    out = nc.dram_tensor("out", (T, D), mybir.dt.float32, kind="ExternalOutput").ap()
    program(nc, *args, out)
    r = run_bass_kernel_spmd(nc, [arrays], core_ids=[0])
    return r.results[0]["out"].reshape(BATCH, SEQ, D)
```
